# Optimizing a Trainium2 kernel written in Bass

```python
import numpy as np
import jax
import jax.numpy as jnp

def _softmax(x, axis=-1):
    return jax.nn.softmax(x, axis=axis)

def _gelu(x):
    return jax.nn.gelu(x, approximate=True)

def _silu(x):
    return jax.nn.silu(x)

def _sigmoid(x):
    return jax.nn.sigmoid(x)

def _layernorm(x, axis=-1, eps=1e-05):
    m = jnp.mean(x, axis=axis, keepdims=True)
    v = jnp.var(x, axis=axis, keepdims=True)
    return (x - m) / jnp.sqrt(v + eps)

def _scatter_add(tgt, idx, src, axis=0):
    return tgt.at[idx].add(src)

def _segment_sum(src, seg, n):
    return jax.ops.segment_sum(src, seg, n)
kernel_name = 'mk_pixart_resid_d4_seqx_r8_9f5b7a'

def setup_inputs(seed: int=0):
    np.random.seed(seed)
    _w = jnp.asarray

    def _rec_inputs():
        import jax
        import jax.numpy as jnp
        _rk = jax.random.key(seed)
        x = -0.003379 + 0.9984 * jax.random.normal(jax.random.fold_in(_rk, 1), (2, 512, 128), jnp.float32)
        _lenS = 512 - jax.random.randint(jax.random.fold_in(_rk, 7), (2,), 0, max(1, 512 // 4) + 1, jnp.int32)
        _lenS2 = 77 - jax.random.randint(jax.random.fold_in(_rk, 8), (2,), 0, max(1, 77 // 4) + 1, jnp.int32)
        cond_1024 = -0.0142567 + 1.00875 * jax.random.normal(jax.random.fold_in(_rk, 11), (2, 128), jnp.float32)
        _ctx_1024P = jax.random.normal(jax.random.fold_in(_rk, 12), (2, 16, 128), jnp.float32)
        _ctx_1024c = jax.random.dirichlet(jax.random.fold_in(_rk, 512), 0.3 * jnp.ones((16,), jnp.float32), (2, 77))
        _ctx_1024t = jnp.einsum('bsk,bkd->bsd', _ctx_1024c, _ctx_1024P)
        _ctx_1024t = _ctx_1024t * jax.lax.rsqrt(jnp.mean(jnp.square(_ctx_1024t)) + 1e-12) * 0.953939
        ctx_1024 = -5.72187e-05 + 0.999849 * (_ctx_1024t + 0.3 * jax.random.normal(jax.random.fold_in(_rk, 612), (2, 77, 128), jnp.float32))
        _validS = jnp.arange(512)[None, :] < _lenS[:, None]
        _validS2 = jnp.arange(77)[None, :] < _lenS2[:, None]
        _causal = jnp.tril(jnp.ones((512, 512), dtype=bool))
        mask_BxS_bf0 = jnp.logical_not(jnp.ones((2, 512), dtype=bool))
        mask_BxS2_bf0 = jnp.logical_not(jnp.ones((2, 77), dtype=bool))
        return (x, cond_1024, ctx_1024, mask_BxS_bf0, mask_BxS2_bf0)
    x, cond_1024, ctx_1024, mask_BxS_bf0, mask_BxS2_bf0 = _rec_inputs()

    def _L0_xcond_setup():
        import jax, jax.numpy as jnp
        import numpy as np
        B, N, K, D, T = (16, 512, 16, 128, 3)
        EPS_ATTN = 1e-08
        LN_EPS = 1e-05

        def _ln(x, g, b):
            mu = jnp.mean(x, axis=-1, keepdims=True)
            var = jnp.mean(jnp.square(x - mu), axis=-1, keepdims=True)
            return (x - mu) * jax.lax.rsqrt(var + LN_EPS) * g + b
        key = jax.random.key(seed)
        ks = jax.random.split(key, 16)
        w = lambda k, i, o: jax.random.normal(k, (i, o), jnp.float32) * 0.02
        inp = {'x_cls': jax.random.normal(ks[0], (B, D), jnp.float32), 'x': jax.random.normal(ks[1], (B, N, D), jnp.float32), 'noise': jax.random.normal(ks[2], (B, K, D), jnp.float32), 'q_mu': jax.random.normal(ks[3], (1, 1, D), jnp.float32), 'q_logsig': jax.random.normal(ks[4], (1, 1, D), jnp.float32) * 0.02, 'lnkv_g': jnp.ones((D,), jnp.float32), 'lnkv_b': jnp.zeros((D,), jnp.float32), 'lnq_g': jnp.ones((D,), jnp.float32), 'lnq_b': jnp.zeros((D,), jnp.float32), 'lnm_g': jnp.ones((D,), jnp.float32), 'lnm_b': jnp.zeros((D,), jnp.float32), 'lnp_g': jnp.ones((D,), jnp.float32), 'lnp_b': jnp.zeros((D,), jnp.float32), 'wk': w(ks[5], D, D), 'bk': jnp.zeros((D,), jnp.float32), 'wv': w(ks[6], D, D), 'bv': jnp.zeros((D,), jnp.float32), 'wq': w(ks[7], D, D), 'bq': jnp.zeros((D,), jnp.float32), 'wu': w(ks[8], D, D), 'bu': jnp.zeros((D,), jnp.float32), 'w1': w(ks[9], D, D), 'b1': jnp.zeros((D,), jnp.float32), 'w2': w(ks[10], D, D), 'b2': jnp.zeros((D,), jnp.float32)}
        return inp
    _L0_xcond_all = _L0_xcond_setup()
    _L0_xcond_in = {k: v for k, v in _L0_xcond_all.items() if k in ('q_mu', 'q_logsig', 'lnkv_g', 'lnkv_b', 'lnq_g', 'lnq_b', 'lnm_g', 'lnm_b', 'lnp_g', 'lnp_b', 'wk', 'bk', 'wv', 'bv', 'wq', 'bq', 'wu', 'bu', 'w1', 'b1', 'w2', 'b2')}
    del _L0_xcond_all

    def _L0_ffn_setup():
        import jax, jax.numpy as jnp
        import numpy as np
        HIDDEN_SIZE = 128
        NUM_EXPERTS = 8
        MOE_INTERMEDIATE_SIZE = 176
        NUM_EXPERTS_PER_TOK = 2
        SHARED_EXPERT_INTERMEDIATE_SIZE = 352
        B, T = (2, 128)
        W_SCALE = 0.02
        key = jax.random.key(seed)
        ks = jax.random.split(key, 8)
        H, E, I, SI = (HIDDEN_SIZE, NUM_EXPERTS, MOE_INTERMEDIATE_SIZE, SHARED_EXPERT_INTERMEDIATE_SIZE)
        return {'x': jax.random.normal(ks[0], (B, T, H), jnp.float32), 'gate_w': jax.random.normal(ks[1], (E, H), jnp.float32) * W_SCALE, 'experts_gate_up': jax.random.normal(ks[2], (E, 2 * I, H), jnp.float32) * W_SCALE, 'experts_down': jax.random.normal(ks[3], (E, H, I), jnp.float32) * W_SCALE, 'shared_gate_w': jax.random.normal(ks[4], (SI, H), jnp.float32) * W_SCALE, 'shared_up_w': jax.random.normal(ks[5], (SI, H), jnp.float32) * W_SCALE, 'shared_down_w': jax.random.normal(ks[6], (H, SI), jnp.float32) * W_SCALE, 'shared_expert_gate_w': jax.random.normal(ks[7], (1, H), jnp.float32) * W_SCALE}
    _L0_ffn_all = _L0_ffn_setup()
    _L0_ffn_in = {k: v for k, v in _L0_ffn_all.items() if k in ('gate_w', 'experts_gate_up', 'experts_down', 'shared_gate_w', 'shared_up_w', 'shared_down_w', 'shared_expert_gate_w')}
    del _L0_ffn_all

    def _L1_xcond_setup():
        import jax, jax.numpy as jnp
        import numpy as np
        B, T, S, H, E = (128, 32, 32, 128, 128)
        key = jax.random.key(seed)
        ks = jax.random.split(key, 8)
        sc = lambda n: 1.0 / np.sqrt(n)
        return dict(dec_seq=jax.random.normal(ks[0], (B, T, E), jnp.float32), enc_hiddens=jax.random.normal(ks[1], (B, S, H), jnp.float32), last_hidden=jax.random.normal(ks[2], (B, H), jnp.float32), W_att=jax.random.normal(ks[3], (2 * H, H), jnp.float32) * sc(2 * H), V_att=jax.random.normal(ks[4], (H, 1), jnp.float32) * sc(H), Wi=jax.random.normal(ks[5], (E + H, 3 * H), jnp.float32) * sc(E + H), Uh=jax.random.normal(ks[6], (H, 3 * H), jnp.float32) * sc(H), b=jnp.zeros((3 * H,), jnp.float32))
    _L1_xcond_all = _L1_xcond_setup()
    _L1_xcond_in = {k: v for k, v in _L1_xcond_all.items() if k in ('W_att', 'V_att', 'Wi', 'Uh', 'b')}
    del _L1_xcond_all

    def _L1_ffn_setup():
        import jax, jax.numpy as jnp
        import numpy as np
        B, S, D = (4, 512, 128)
        H = 512
        RH = 128
        E = 16
        K = 2
        NS = 1

        def _swiglu(x, w1, w2, w3):
            return jax.nn.silu(x @ w1) * (x @ w2) @ w3
        key = jax.random.key(seed)
        ks = jax.random.split(key, 9)
        s = 0.02
        return {'x': jax.random.normal(ks[0], (B, S, D), dtype=jnp.float32), 'router_w': jax.random.normal(ks[1], (D, E), dtype=jnp.float32) * s, 'expert_bias': jnp.zeros((E,), dtype=jnp.float32), 'shared_w1': jax.random.normal(ks[2], (NS, D, H), dtype=jnp.float32) * s, 'shared_w2': jax.random.normal(ks[3], (NS, D, H), dtype=jnp.float32) * s, 'shared_w3': jax.random.normal(ks[4], (NS, H, D), dtype=jnp.float32) * s, 'routed_w1': jax.random.normal(ks[5], (E, D, RH), dtype=jnp.float32) * s, 'routed_w2': jax.random.normal(ks[6], (E, D, RH), dtype=jnp.float32) * s, 'routed_w3': jax.random.normal(ks[7], (E, RH, D), dtype=jnp.float32) * s}
    _L1_ffn_all = _L1_ffn_setup()
    _L1_ffn_in = {k: v for k, v in _L1_ffn_all.items() if k in ('router_w', 'expert_bias', 'shared_w1', 'shared_w2', 'shared_w3', 'routed_w1', 'routed_w2', 'routed_w3')}
    del _L1_ffn_all

    def _L2_xcond_setup():
        import jax, jax.numpy as jnp
        import numpy as np
        import math
        B, S, CTX, D, H, DH = (2, 256, 32, 128, 16, 64)
        INNER = H * DH
        DFF = 4 * D

        def layernorm(x, eps=1e-05):
            m = jnp.mean(x, axis=-1, keepdims=True)
            v = jnp.var(x, axis=-1, keepdims=True)
            return (x - m) * jax.lax.rsqrt(v + eps)

        def adaln(x, t, w, b):
            emb = t @ w + b
            scale, shift = jnp.split(emb, 2, axis=-1)
            return layernorm(x) * (1.0 + scale) + shift

        def mha(xq, ctx, wq, wk, wv, wo, bo):
            b, sq, _ = xq.shape
            sk = ctx.shape[1]
            q = (xq @ wq).reshape(b, sq, H, DH).transpose(0, 2, 1, 3)
            k = (ctx @ wk).reshape(b, sk, H, DH).transpose(0, 2, 1, 3)
            v = (ctx @ wv).reshape(b, sk, H, DH).transpose(0, 2, 1, 3)
            scores = jnp.einsum('bhqd,bhkd->bhqk', q, k) / math.sqrt(DH)
            attn = jax.nn.softmax(scores, axis=-1)
            out = jnp.einsum('bhqk,bhkd->bhqd', attn, v)
            out = out.transpose(0, 2, 1, 3).reshape(b, sq, INNER)
            return out @ wo + bo

        def glu_ff(x, w1, b1, w2, b2):
            u = x @ w1 + b1
            a, gate = jnp.split(u, 2, axis=-1)
            return a * jax.nn.gelu(gate, approximate=False) @ w2 + b2
        key = jax.random.key(seed)
        ks = jax.random.split(key, 24)
        s = 1.0 / math.sqrt(D)

        def n(k, shape, scale=1.0):
            return jax.random.normal(k, shape, dtype=jnp.float32) * scale
        return {'x': n(ks[0], (B, S, D)), 't': n(ks[1], (B, 1, D)), 'context': n(ks[2], (B, CTX, D)), 'attn1_wq': n(ks[3], (D, INNER), s), 'attn1_wk': n(ks[4], (D, INNER), s), 'attn1_wv': n(ks[5], (D, INNER), s), 'attn1_wo': n(ks[6], (INNER, D), s), 'attn1_bo': n(ks[7], (D,), 0.01), 'attn2_wq': n(ks[8], (D, INNER), s), 'attn2_wk': n(ks[9], (D, INNER), s), 'attn2_wv': n(ks[10], (D, INNER), s), 'attn2_wo': n(ks[11], (INNER, D), s), 'attn2_bo': n(ks[12], (D,), 0.01), 'ff_w1': n(ks[13], (D, 2 * DFF), s), 'ff_b1': n(ks[14], (2 * DFF,), 0.01), 'ff_w2': n(ks[15], (DFF, D), 1.0 / math.sqrt(DFF)), 'ff_b2': n(ks[16], (D,), 0.01), 'norm1_w': n(ks[17], (D, 2 * D), s), 'norm1_b': n(ks[18], (2 * D,), 0.01), 'norm2_w': n(ks[19], (D, 2 * D), s), 'norm2_b': n(ks[20], (2 * D,), 0.01), 'norm3_w': n(ks[21], (D, 2 * D), s), 'norm3_b': n(ks[22], (2 * D,), 0.01)}
    _L2_xcond_all = _L2_xcond_setup()
    _L2_xcond_in = {k: v for k, v in _L2_xcond_all.items() if k in ('attn1_wq', 'attn1_wk', 'attn1_wv', 'attn1_wo', 'attn1_bo', 'attn2_wq', 'attn2_wk', 'attn2_wv', 'attn2_wo', 'attn2_bo', 'ff_w1', 'ff_b1', 'ff_w2', 'ff_b2', 'norm1_w', 'norm1_b', 'norm2_w', 'norm2_b', 'norm3_w', 'norm3_b')}
    del _L2_xcond_all

    def _L2_ffn_setup():
        import jax, jax.numpy as jnp
        import numpy as np

        def _bitlinear(x, w_latent):
            scale = jax.lax.stop_gradient(jnp.clip(jnp.mean(jnp.abs(w_latent), axis=1, keepdims=True), 1e-05, None))
            tern = jnp.clip(jnp.round(w_latent / scale), -1.0, 1.0)
            w = w_latent + jax.lax.stop_gradient(tern - w_latent)
            return x @ (w * scale).T
        key = jax.random.key(seed)
        ks = jax.random.split(key, 6)
        dim, hidden, rank = (128, 512, 16)
        B, S = (4, 512)
        x = jax.random.normal(ks[0], (B, S, dim), dtype=jnp.float32)
        w_fc = 0.02 * jax.random.normal(ks[1], (hidden, dim), dtype=jnp.float32)
        w_proj = 0.02 * jax.random.normal(ks[2], (dim, hidden), dtype=jnp.float32)
        u = 0.02 * jax.random.normal(ks[3], (hidden, rank), dtype=jnp.float32)
        v = 0.02 * jax.random.normal(ks[4], (rank, dim), dtype=jnp.float32)
        fast_b = jax.random.normal(ks[5], (rank, rank), dtype=jnp.float32)
        gate = jnp.float32(0.05)
        return {'x': x, 'fast_b': fast_b, 'w_fc': w_fc, 'w_proj': w_proj, 'u': u, 'v': v, 'gate': gate}
    _L2_ffn_all = _L2_ffn_setup()
    _L2_ffn_in = {k: v for k, v in _L2_ffn_all.items() if k in ('fast_b', 'w_fc', 'w_proj', 'u', 'v', 'gate')}
    del _L2_ffn_all

    def _L3_xcond_setup():
        import jax, jax.numpy as jnp
        import numpy as np
        NL, D, H, DFF = (6, 128, 16, 512)
        HD = D // H

        def _rope(x):
            L = x.shape[1]
            half = HD // 2
            inv = 1.0 / 10000.0 ** (jnp.arange(half, dtype=jnp.float32) / half)
            ang = jnp.arange(L, dtype=jnp.float32)[:, None] * inv
            cos = jnp.cos(ang)[None, :, None, :]
            sin = jnp.sin(ang)[None, :, None, :]
            x1, x2 = (x[..., :half], x[..., half:])
            return jnp.concatenate([x1 * cos - x2 * sin, x1 * sin + x2 * cos], axis=-1)

        def _ln(x, eps=1e-05):
            m = jnp.mean(x, axis=-1, keepdims=True)
            v = jnp.var(x, axis=-1, keepdims=True)
            return (x - m) * jax.lax.rsqrt(v + eps)

        def _adaln(x, emb, w, b):
            gb = emb[:, 0, :] @ w.T + b
            g, be = jnp.split(gb, 2, axis=-1)
            return _ln(x) * (1.0 + g[:, None, :]) + be[:, None, :]

        def _attn(q, k, v, mask):
            scores = jnp.einsum('bqhd,bkhd->bhqk', q, k) / np.float32(np.sqrt(HD))
            scores = jnp.where(mask[:, None, None, :], jnp.float32(-jnp.inf), scores)
            w = jax.nn.softmax(scores, axis=-1)
            return jnp.einsum('bhqk,bkhd->bqhd', w, v)
        key = jax.random.key(seed)
        ks = jax.random.split(key, 20)
        B, L, LC = (4, 128, 64)
        s = 0.02
        inp = {'x': jax.random.normal(ks[0], (B, L, D), jnp.float32), 'noise_emb': jax.random.normal(ks[1], (B, 1, D), jnp.float32), 'context': jax.random.normal(ks[2], (B, LC, D), jnp.float32), 'src_mask': jnp.zeros((B, L), bool), 'ctx_mask': jnp.zeros((B, LC), bool), 'n1_w': jax.random.normal(ks[3], (NL, 2 * D, D), jnp.float32) * s, 'n1_b': jnp.zeros((NL, 2 * D), jnp.float32), 'n2_w': jax.random.normal(ks[4], (NL, 2 * D, D), jnp.float32) * s, 'n2_b': jnp.zeros((NL, 2 * D), jnp.float32), 'n3_w': jax.random.normal(ks[5], (NL, 2 * D, D), jnp.float32) * s, 'n3_b': jnp.zeros((NL, 2 * D), jnp.float32), 'qkv_w': jax.random.normal(ks[6], (NL, 3 * D, D), jnp.float32) * s, 'so_w': jax.random.normal(ks[7], (NL, D, D), jnp.float32) * s, 'cq_w': jax.random.normal(ks[8], (NL, D, D), jnp.float32) * s, 'ck_w': jax.random.normal(ks[9], (NL, D, D), jnp.float32) * s, 'cv_w': jax.random.normal(ks[10], (NL, D, D), jnp.float32) * s, 'co_w': jax.random.normal(ks[11], (NL, D, D), jnp.float32) * s, 'f1_w': jax.random.normal(ks[12], (NL, DFF, D), jnp.float32) * s, 'f1_b': jnp.zeros((NL, DFF), jnp.float32), 'f2_w': jax.random.normal(ks[13], (NL, D, DFF), jnp.float32) * s, 'f2_b': jnp.zeros((NL, D), jnp.float32)}
        return inp
    _L3_xcond_all = _L3_xcond_setup()
    _L3_xcond_in = {k: v for k, v in _L3_xcond_all.items() if k in ('n1_w', 'n1_b', 'n2_w', 'n2_b', 'n3_w', 'n3_b', 'qkv_w', 'so_w', 'cq_w', 'ck_w', 'cv_w', 'co_w', 'f1_w', 'f1_b', 'f2_w', 'f2_b')}
    del _L3_xcond_all

    def _L3_ffn_setup():
        import jax, jax.numpy as jnp
        import numpy as np
        D_MODEL = 128
        NUM_HEADS = 4
        NUM_EXPERTS = 8
        TOP_K = 2
        D_FF = 128
        EPS = 1e-06

        def _rmsnorm(x, g):
            return x * jax.lax.rsqrt(jnp.mean(x * x, axis=-1, keepdims=True) + EPS) * g

        def _swiglu(x, w1, w2, w3):
            return jax.nn.silu(x @ w1.T) * (x @ w3.T) @ w2.T
        key = jax.random.key(seed)
        ks = jax.random.split(key, 16)
        d, e, f = (D_MODEL, NUM_EXPERTS, D_FF)
        dc = d // 4
        s = 0.02
        return {'X': jax.random.normal(ks[0], (2, 128, d), dtype=jnp.float32), 'g1': jnp.ones((d,), jnp.float32), 'g2': jnp.ones((d,), jnp.float32), 'Wq': jax.random.normal(ks[1], (d, d), jnp.float32) * s, 'Wkc': jax.random.normal(ks[2], (dc, d), jnp.float32) * s, 'Wvc': jax.random.normal(ks[3], (dc, d), jnp.float32) * s, 'Wo': jax.random.normal(ks[4], (d, d), jnp.float32) * s, 'Wr': jax.random.normal(ks[5], (e, d), jnp.float32) * s, 'expert_bias': jnp.zeros((e,), jnp.float32), 'sW1': jax.random.normal(ks[6], (f, d), jnp.float32) * s, 'sW2': jax.random.normal(ks[7], (d, f), jnp.float32) * s, 'sW3': jax.random.normal(ks[8], (f, d), jnp.float32) * s, 'eW1': jax.random.normal(ks[9], (e, f, d), jnp.float32) * s, 'eW2': jax.random.normal(ks[10], (e, d, f), jnp.float32) * s, 'eW3': jax.random.normal(ks[11], (e, f, d), jnp.float32) * s}
    _L3_ffn_all = _L3_ffn_setup()
    _L3_ffn_in = {k: v for k, v in _L3_ffn_all.items() if k in ('g1', 'g2', 'Wq', 'Wkc', 'Wvc', 'Wo', 'Wr', 'expert_bias', 'sW1', 'sW2', 'sW3', 'eW1', 'eW2', 'eW3')}
    del _L3_ffn_all
    return {'x': x, 'cond_1024': cond_1024, 'ctx_1024': ctx_1024, 'mask_BxS_bf0': mask_BxS_bf0, 'mask_BxS2_bf0': mask_BxS2_bf0, 'L0_xcond_q_mu': _L0_xcond_in['q_mu'], 'L0_xcond_q_logsig': _L0_xcond_in['q_logsig'], 'L0_xcond_lnkv_g': _L0_xcond_in['lnkv_g'], 'L0_xcond_lnkv_b': _L0_xcond_in['lnkv_b'], 'L0_xcond_lnq_g': _L0_xcond_in['lnq_g'], 'L0_xcond_lnq_b': _L0_xcond_in['lnq_b'], 'L0_xcond_lnm_g': _L0_xcond_in['lnm_g'], 'L0_xcond_lnm_b': _L0_xcond_in['lnm_b'], 'L0_xcond_lnp_g': _L0_xcond_in['lnp_g'], 'L0_xcond_lnp_b': _L0_xcond_in['lnp_b'], 'L0_xcond_wk': _L0_xcond_in['wk'], 'L0_xcond_bk': _L0_xcond_in['bk'], 'L0_xcond_wv': _L0_xcond_in['wv'], 'L0_xcond_bv': _L0_xcond_in['bv'], 'L0_xcond_wq': _L0_xcond_in['wq'], 'L0_xcond_bq': _L0_xcond_in['bq'], 'L0_xcond_wu': _L0_xcond_in['wu'], 'L0_xcond_bu': _L0_xcond_in['bu'], 'L0_xcond_w1': _L0_xcond_in['w1'], 'L0_xcond_b1': _L0_xcond_in['b1'], 'L0_xcond_w2': _L0_xcond_in['w2'], 'L0_xcond_b2': _L0_xcond_in['b2'], 'L0_ffn_gate_w': _L0_ffn_in['gate_w'], 'L0_ffn_experts_gate_up': _L0_ffn_in['experts_gate_up'], 'L0_ffn_experts_down': _L0_ffn_in['experts_down'], 'L0_ffn_shared_gate_w': _L0_ffn_in['shared_gate_w'], 'L0_ffn_shared_up_w': _L0_ffn_in['shared_up_w'], 'L0_ffn_shared_down_w': _L0_ffn_in['shared_down_w'], 'L0_ffn_shared_expert_gate_w': _L0_ffn_in['shared_expert_gate_w'], 'L1_xcond_W_att': _L1_xcond_in['W_att'], 'L1_xcond_V_att': _L1_xcond_in['V_att'], 'L1_xcond_Wi': _L1_xcond_in['Wi'], 'L1_xcond_Uh': _L1_xcond_in['Uh'], 'L1_xcond_b': _L1_xcond_in['b'], 'L1_ffn_router_w': _L1_ffn_in['router_w'], 'L1_ffn_expert_bias': _L1_ffn_in['expert_bias'], 'L1_ffn_shared_w1': _L1_ffn_in['shared_w1'], 'L1_ffn_shared_w2': _L1_ffn_in['shared_w2'], 'L1_ffn_shared_w3': _L1_ffn_in['shared_w3'], 'L1_ffn_routed_w1': _L1_ffn_in['routed_w1'], 'L1_ffn_routed_w2': _L1_ffn_in['routed_w2'], 'L1_ffn_routed_w3': _L1_ffn_in['routed_w3'], 'L2_xcond_attn1_wq': _L2_xcond_in['attn1_wq'], 'L2_xcond_attn1_wk': _L2_xcond_in['attn1_wk'], 'L2_xcond_attn1_wv': _L2_xcond_in['attn1_wv'], 'L2_xcond_attn1_wo': _L2_xcond_in['attn1_wo'], 'L2_xcond_attn1_bo': _L2_xcond_in['attn1_bo'], 'L2_xcond_attn2_wq': _L2_xcond_in['attn2_wq'], 'L2_xcond_attn2_wk': _L2_xcond_in['attn2_wk'], 'L2_xcond_attn2_wv': _L2_xcond_in['attn2_wv'], 'L2_xcond_attn2_wo': _L2_xcond_in['attn2_wo'], 'L2_xcond_attn2_bo': _L2_xcond_in['attn2_bo'], 'L2_xcond_ff_w1': _L2_xcond_in['ff_w1'], 'L2_xcond_ff_b1': _L2_xcond_in['ff_b1'], 'L2_xcond_ff_w2': _L2_xcond_in['ff_w2'], 'L2_xcond_ff_b2': _L2_xcond_in['ff_b2'], 'L2_xcond_norm1_w': _L2_xcond_in['norm1_w'], 'L2_xcond_norm1_b': _L2_xcond_in['norm1_b'], 'L2_xcond_norm2_w': _L2_xcond_in['norm2_w'], 'L2_xcond_norm2_b': _L2_xcond_in['norm2_b'], 'L2_xcond_norm3_w': _L2_xcond_in['norm3_w'], 'L2_xcond_norm3_b': _L2_xcond_in['norm3_b'], 'L2_ffn_fast_b': _L2_ffn_in['fast_b'], 'L2_ffn_w_fc': _L2_ffn_in['w_fc'], 'L2_ffn_w_proj': _L2_ffn_in['w_proj'], 'L2_ffn_u': _L2_ffn_in['u'], 'L2_ffn_v': _L2_ffn_in['v'], 'L2_ffn_gate': _L2_ffn_in['gate'], 'L3_xcond_n1_w': _L3_xcond_in['n1_w'], 'L3_xcond_n1_b': _L3_xcond_in['n1_b'], 'L3_xcond_n2_w': _L3_xcond_in['n2_w'], 'L3_xcond_n2_b': _L3_xcond_in['n2_b'], 'L3_xcond_n3_w': _L3_xcond_in['n3_w'], 'L3_xcond_n3_b': _L3_xcond_in['n3_b'], 'L3_xcond_qkv_w': _L3_xcond_in['qkv_w'], 'L3_xcond_so_w': _L3_xcond_in['so_w'], 'L3_xcond_cq_w': _L3_xcond_in['cq_w'], 'L3_xcond_ck_w': _L3_xcond_in['ck_w'], 'L3_xcond_cv_w': _L3_xcond_in['cv_w'], 'L3_xcond_co_w': _L3_xcond_in['co_w'], 'L3_xcond_f1_w': _L3_xcond_in['f1_w'], 'L3_xcond_f1_b': _L3_xcond_in['f1_b'], 'L3_xcond_f2_w': _L3_xcond_in['f2_w'], 'L3_xcond_f2_b': _L3_xcond_in['f2_b'], 'L3_ffn_g1': _L3_ffn_in['g1'], 'L3_ffn_g2': _L3_ffn_in['g2'], 'L3_ffn_Wq': _L3_ffn_in['Wq'], 'L3_ffn_Wkc': _L3_ffn_in['Wkc'], 'L3_ffn_Wvc': _L3_ffn_in['Wvc'], 'L3_ffn_Wo': _L3_ffn_in['Wo'], 'L3_ffn_Wr': _L3_ffn_in['Wr'], 'L3_ffn_expert_bias': _L3_ffn_in['expert_bias'], 'L3_ffn_sW1': _L3_ffn_in['sW1'], 'L3_ffn_sW2': _L3_ffn_in['sW2'], 'L3_ffn_sW3': _L3_ffn_in['sW3'], 'L3_ffn_eW1': _L3_ffn_in['eW1'], 'L3_ffn_eW2': _L3_ffn_in['eW2'], 'L3_ffn_eW3': _L3_ffn_in['eW3']}

def reference(x, cond_1024, ctx_1024, mask_BxS_bf0, mask_BxS2_bf0, L0_xcond_q_mu, L0_xcond_q_logsig, L0_xcond_lnkv_g, L0_xcond_lnkv_b, L0_xcond_lnq_g, L0_xcond_lnq_b, L0_xcond_lnm_g, L0_xcond_lnm_b, L0_xcond_lnp_g, L0_xcond_lnp_b, L0_xcond_wk, L0_xcond_bk, L0_xcond_wv, L0_xcond_bv, L0_xcond_wq, L0_xcond_bq, L0_xcond_wu, L0_xcond_bu, L0_xcond_w1, L0_xcond_b1, L0_xcond_w2, L0_xcond_b2, L0_ffn_gate_w, L0_ffn_experts_gate_up, L0_ffn_experts_down, L0_ffn_shared_gate_w, L0_ffn_shared_up_w, L0_ffn_shared_down_w, L0_ffn_shared_expert_gate_w, L1_xcond_W_att, L1_xcond_V_att, L1_xcond_Wi, L1_xcond_Uh, L1_xcond_b, L1_ffn_router_w, L1_ffn_expert_bias, L1_ffn_shared_w1, L1_ffn_shared_w2, L1_ffn_shared_w3, L1_ffn_routed_w1, L1_ffn_routed_w2, L1_ffn_routed_w3, L2_xcond_attn1_wq, L2_xcond_attn1_wk, L2_xcond_attn1_wv, L2_xcond_attn1_wo, L2_xcond_attn1_bo, L2_xcond_attn2_wq, L2_xcond_attn2_wk, L2_xcond_attn2_wv, L2_xcond_attn2_wo, L2_xcond_attn2_bo, L2_xcond_ff_w1, L2_xcond_ff_b1, L2_xcond_ff_w2, L2_xcond_ff_b2, L2_xcond_norm1_w, L2_xcond_norm1_b, L2_xcond_norm2_w, L2_xcond_norm2_b, L2_xcond_norm3_w, L2_xcond_norm3_b, L2_ffn_fast_b, L2_ffn_w_fc, L2_ffn_w_proj, L2_ffn_u, L2_ffn_v, L2_ffn_gate, L3_xcond_n1_w, L3_xcond_n1_b, L3_xcond_n2_w, L3_xcond_n2_b, L3_xcond_n3_w, L3_xcond_n3_b, L3_xcond_qkv_w, L3_xcond_so_w, L3_xcond_cq_w, L3_xcond_ck_w, L3_xcond_cv_w, L3_xcond_co_w, L3_xcond_f1_w, L3_xcond_f1_b, L3_xcond_f2_w, L3_xcond_f2_b, L3_ffn_g1, L3_ffn_g2, L3_ffn_Wq, L3_ffn_Wkc, L3_ffn_Wvc, L3_ffn_Wo, L3_ffn_Wr, L3_ffn_expert_bias, L3_ffn_sW1, L3_ffn_sW2, L3_ffn_sW3, L3_ffn_eW1, L3_ffn_eW2, L3_ffn_eW3):
    import jax
    import jax.numpy as jnp

    def _L0_xcond_ref(x_cls, x, noise, q_mu, q_logsig, lnkv_g, lnkv_b, lnq_g, lnq_b, lnm_g, lnm_b, lnp_g, lnp_b, wk, bk, wv, bv, wq, bq, wu, bu, w1, b1, w2, b2):
        import jax, jax.numpy as jnp
        import numpy as np
        B, N, K, D, T = (16, 512, 16, 128, 3)
        EPS_ATTN = 1e-08
        LN_EPS = 1e-05

        def _ln(x, g, b):
            mu = jnp.mean(x, axis=-1, keepdims=True)
            var = jnp.mean(jnp.square(x - mu), axis=-1, keepdims=True)
            return (x - mu) * jax.lax.rsqrt(var + LN_EPS) * g + b
        scale = D ** (-0.5)
        x_in = _ln(x, lnkv_g, lnkv_b)
        k = x_in @ wk + bk
        v = x_in @ wv + bv
        slots = q_mu + jnp.exp(q_logsig) * noise
        for _ in range(T):
            prev = slots
            q = _ln(slots, lnq_g, lnq_b) @ wq + bq
            logits = jnp.einsum('bnd,bkd->bnk', k, q) / scale
            attn = jax.nn.softmax(logits, axis=-1) + EPS_ATTN
            attn = attn / jnp.sum(attn, axis=1, keepdims=True)
            upd = jnp.einsum('bnk,bnd->bkd', attn, v)
            slots = upd @ wu + bu + prev
            h = _ln(slots, lnm_g, lnm_b) @ w1 + b1
            slots = jax.nn.gelu(h, approximate=False) @ w2 + b2 + slots
            slots = _ln(slots + x_cls[:, None, :], lnp_g, lnp_b)
        return slots

    def _L0_ffn_ref(x, gate_w, experts_gate_up, experts_down, shared_gate_w, shared_up_w, shared_down_w, shared_expert_gate_w):
        import jax, jax.numpy as jnp
        import numpy as np
        HIDDEN_SIZE = 128
        NUM_EXPERTS = 8
        MOE_INTERMEDIATE_SIZE = 176
        NUM_EXPERTS_PER_TOK = 2
        SHARED_EXPERT_INTERMEDIATE_SIZE = 352
        B, T = (2, 128)
        W_SCALE = 0.02
        Bx, Tx, H = x.shape
        E = gate_w.shape[0]
        I = experts_down.shape[2]
        x_flat = x.reshape(Bx * Tx, H)
        logits = x_flat @ gate_w.T
        scores = jax.nn.softmax(logits, axis=-1)
        _, topk_ids = jax.lax.top_k(scores, NUM_EXPERTS_PER_TOK)
        in_topk = jax.nn.one_hot(topk_ids, E, dtype=x.dtype).sum(axis=1)
        w = scores * in_topk
        gu = jnp.einsum('nh,eih->nei', x_flat, experts_gate_up)
        g, u = (gu[..., :I], gu[..., I:])
        h = jax.nn.silu(g) * u
        expert_out = jnp.einsum('nei,ehi->neh', h, experts_down)
        out = jnp.einsum('neh,ne->nh', expert_out, w)
        shared = jax.nn.silu(x_flat @ shared_gate_w.T) * (x_flat @ shared_up_w.T) @ shared_down_w.T
        shared_weight = jax.nn.sigmoid(x_flat @ shared_expert_gate_w.T)
        out = out + shared_weight * shared
        return out.reshape(Bx, Tx, H)

    def _L1_xcond_ref(dec_seq, enc_hiddens, last_hidden, W_att, V_att, Wi, Uh, b):
        import jax, jax.numpy as jnp
        import numpy as np
        B, T, S, H, E = (128, 32, 32, 128, 128)
        Bn, Sn, Hn = enc_hiddens.shape

        def step(h, x_t):
            hid = jnp.broadcast_to(h[:, None, :], (Bn, Sn, Hn))
            combined = jnp.concatenate([hid, enc_hiddens], axis=2)
            score = jnp.tanh(jnp.einsum('bsk,kh->bsh', combined, W_att))
            score = jnp.einsum('bsh,h->bs', score, V_att[:, 0])
            attn = jax.nn.softmax(score, axis=-1)
            context = jnp.einsum('bs,bsh->bh', attn, enc_hiddens)
            inp = jnp.concatenate([x_t, context], axis=1)
            gz, gr, gh = jnp.split(inp @ Wi + b, 3, axis=1)
            rz, rr, rh = jnp.split(h @ Uh, 3, axis=1)
            z = jax.nn.sigmoid(gz + rz)
            r = jax.nn.sigmoid(gr + rr)
            hh = jnp.tanh(gh + r * rh)
            h_new = z * h + (1.0 - z) * hh
            return (h_new, h_new)
        _, outs = jax.lax.scan(step, last_hidden, jnp.swapaxes(dec_seq, 0, 1))
        return jnp.swapaxes(outs, 0, 1)

    def _L1_ffn_ref(x, router_w, expert_bias, shared_w1, shared_w2, shared_w3, routed_w1, routed_w2, routed_w3):
        import jax, jax.numpy as jnp
        import numpy as np
        B, S, D = (4, 512, 128)
        H = 512
        RH = 128
        E = 16
        K = 2
        NS = 1

        def _swiglu(x, w1, w2, w3):
            return jax.nn.silu(x @ w1) * (x @ w2) @ w3
        shared_out = jnp.sum(jax.vmap(lambda w1, w2, w3: _swiglu(x, w1, w2, w3))(shared_w1, shared_w2, shared_w3), axis=0)
        scores = jax.nn.sigmoid(x @ router_w)
        sel_scores = scores + expert_bias
        _, top_idx = jax.lax.top_k(sel_scores, K)
        top_scores = jnp.take_along_axis(scores, top_idx, axis=-1)
        gates = jnp.sum(jax.nn.one_hot(top_idx, E, dtype=scores.dtype) * top_scores[..., None], axis=-2)
        xf = x.reshape(-1, D)
        gf = gates.reshape(-1, E).T

        def body(acc, ws):
            w1, w2, w3, g = ws
            return (acc + _swiglu(xf, w1, w2, w3) * g[:, None], None)
        routed_out, _ = jax.lax.scan(body, jnp.zeros_like(xf), (routed_w1, routed_w2, routed_w3, gf))
        return shared_out + routed_out.reshape(x.shape)

    def _L2_xcond_ref(x, t, context, attn1_wq, attn1_wk, attn1_wv, attn1_wo, attn1_bo, attn2_wq, attn2_wk, attn2_wv, attn2_wo, attn2_bo, ff_w1, ff_b1, ff_w2, ff_b2, norm1_w, norm1_b, norm2_w, norm2_b, norm3_w, norm3_b):
        import jax, jax.numpy as jnp
        import numpy as np
        import math
        B, S, CTX, D, H, DH = (2, 256, 32, 128, 16, 64)
        INNER = H * DH
        DFF = 4 * D

        def layernorm(x, eps=1e-05):
            m = jnp.mean(x, axis=-1, keepdims=True)
            v = jnp.var(x, axis=-1, keepdims=True)
            return (x - m) * jax.lax.rsqrt(v + eps)

        def adaln(x, t, w, b):
            emb = t @ w + b
            scale, shift = jnp.split(emb, 2, axis=-1)
            return layernorm(x) * (1.0 + scale) + shift

        def mha(xq, ctx, wq, wk, wv, wo, bo):
            b, sq, _ = xq.shape
            sk = ctx.shape[1]
            q = (xq @ wq).reshape(b, sq, H, DH).transpose(0, 2, 1, 3)
            k = (ctx @ wk).reshape(b, sk, H, DH).transpose(0, 2, 1, 3)
            v = (ctx @ wv).reshape(b, sk, H, DH).transpose(0, 2, 1, 3)
            scores = jnp.einsum('bhqd,bhkd->bhqk', q, k) / math.sqrt(DH)
            attn = jax.nn.softmax(scores, axis=-1)
            out = jnp.einsum('bhqk,bhkd->bhqd', attn, v)
            out = out.transpose(0, 2, 1, 3).reshape(b, sq, INNER)
            return out @ wo + bo

        def glu_ff(x, w1, b1, w2, b2):
            u = x @ w1 + b1
            a, gate = jnp.split(u, 2, axis=-1)
            return a * jax.nn.gelu(gate, approximate=False) @ w2 + b2
        h1 = adaln(x, t, norm1_w, norm1_b)
        x = mha(h1, h1, attn1_wq, attn1_wk, attn1_wv, attn1_wo, attn1_bo) + x
        h2 = adaln(x, t, norm2_w, norm2_b)
        x = mha(h2, context, attn2_wq, attn2_wk, attn2_wv, attn2_wo, attn2_bo) + x
        h3 = adaln(x, t, norm3_w, norm3_b)
        x = glu_ff(h3, ff_w1, ff_b1, ff_w2, ff_b2) + x
        return x

    def _L2_ffn_ref(x, fast_b, w_fc, w_proj, u, v, gate):
        import jax, jax.numpy as jnp
        import numpy as np

        def _bitlinear(x, w_latent):
            scale = jax.lax.stop_gradient(jnp.clip(jnp.mean(jnp.abs(w_latent), axis=1, keepdims=True), 1e-05, None))
            tern = jnp.clip(jnp.round(w_latent / scale), -1.0, 1.0)
            w = w_latent + jax.lax.stop_gradient(tern - w_latent)
            return x @ (w * scale).T
        h = _bitlinear(x, w_fc) + gate * (x @ v.T @ fast_b.T @ u.T)
        r = jnp.maximum(h, 0.0)
        return _bitlinear(r * r, w_proj)

    def _L3_xcond_ref(x, noise_emb, context, src_mask, ctx_mask, n1_w, n1_b, n2_w, n2_b, n3_w, n3_b, qkv_w, so_w, cq_w, ck_w, cv_w, co_w, f1_w, f1_b, f2_w, f2_b):
        import jax, jax.numpy as jnp
        import numpy as np
        NL, D, H, DFF = (6, 128, 16, 512)
        HD = D // H

        def _rope(x):
            L = x.shape[1]
            half = HD // 2
            inv = 1.0 / 10000.0 ** (jnp.arange(half, dtype=jnp.float32) / half)
            ang = jnp.arange(L, dtype=jnp.float32)[:, None] * inv
            cos = jnp.cos(ang)[None, :, None, :]
            sin = jnp.sin(ang)[None, :, None, :]
            x1, x2 = (x[..., :half], x[..., half:])
            return jnp.concatenate([x1 * cos - x2 * sin, x1 * sin + x2 * cos], axis=-1)

        def _ln(x, eps=1e-05):
            m = jnp.mean(x, axis=-1, keepdims=True)
            v = jnp.var(x, axis=-1, keepdims=True)
            return (x - m) * jax.lax.rsqrt(v + eps)

        def _adaln(x, emb, w, b):
            gb = emb[:, 0, :] @ w.T + b
            g, be = jnp.split(gb, 2, axis=-1)
            return _ln(x) * (1.0 + g[:, None, :]) + be[:, None, :]

        def _attn(q, k, v, mask):
            scores = jnp.einsum('bqhd,bkhd->bhqk', q, k) / np.float32(np.sqrt(HD))
            scores = jnp.where(mask[:, None, None, :], jnp.float32(-jnp.inf), scores)
            w = jax.nn.softmax(scores, axis=-1)
            return jnp.einsum('bhqk,bkhd->bqhd', w, v)
        B, L, _ = x.shape
        LC = context.shape[1]
        for i in range(NL):
            xn = _adaln(x, noise_emb, n1_w[i], n1_b[i])
            qkv = xn @ qkv_w[i].T
            q, k, v = jnp.split(qkv, 3, axis=-1)
            q = _rope(q.reshape(B, L, H, HD))
            k = _rope(k.reshape(B, L, H, HD))
            v = v.reshape(B, L, H, HD)
            a = _attn(q, k, v, src_mask).reshape(B, L, D) @ so_w[i].T
            x = x + a
            xn = _adaln(x, noise_emb, n2_w[i], n2_b[i])
            q = _rope((xn @ cq_w[i].T).reshape(B, L, H, HD))
            k = _rope((context @ ck_w[i].T).reshape(B, LC, H, HD))
            v = (context @ cv_w[i].T).reshape(B, LC, H, HD)
            a = _attn(q, k, v, ctx_mask).reshape(B, L, D) @ co_w[i].T
            x = x + a
            xn = _adaln(x, noise_emb, n3_w[i], n3_b[i])
            h = jax.nn.gelu(xn @ f1_w[i].T + f1_b[i], approximate=False)
            x = x + (h @ f2_w[i].T + f2_b[i])
        return x

    def _L3_ffn_ref(X, g1, g2, Wq, Wkc, Wvc, Wo, Wr, expert_bias, sW1, sW2, sW3, eW1, eW2, eW3):
        import jax, jax.numpy as jnp
        import numpy as np
        D_MODEL = 128
        NUM_HEADS = 4
        NUM_EXPERTS = 8
        TOP_K = 2
        D_FF = 128
        EPS = 1e-06

        def _rmsnorm(x, g):
            return x * jax.lax.rsqrt(jnp.mean(x * x, axis=-1, keepdims=True) + EPS) * g

        def _swiglu(x, w1, w2, w3):
            return jax.nn.silu(x @ w1.T) * (x @ w3.T) @ w2.T
        B, S, d = X.shape
        H = NUM_HEADS
        dk = d // H
        scale = 1.0 / jnp.sqrt(jnp.float32(dk))
        nx = _rmsnorm(X, g1)
        Q = (nx @ Wq.T).reshape(B, S, H, dk).transpose(0, 2, 1, 3)
        Kc = nx @ Wkc.T
        Vc = nx @ Wvc.T
        scores = jnp.einsum('bhsd,btd->bhst', Q, Kc) * scale
        attn = jax.nn.softmax(scores, axis=-1)
        out = jnp.einsum('bhst,btd->bhsd', attn, Vc)
        out = out.transpose(0, 2, 1, 3).reshape(B, S, d) @ Wo.T
        X = X + out
        nx = _rmsnorm(X, g2)
        xf = nx.reshape(-1, d)
        logits = xf @ Wr.T + expert_bias
        rw = jax.nn.softmax(logits, axis=-1)
        topw, topi = jax.lax.top_k(rw, TOP_K)
        topw = jax.nn.softmax(topw, axis=-1)
        combine = jnp.sum(jax.nn.one_hot(topi, NUM_EXPERTS, dtype=xf.dtype) * topw[..., None], axis=1)
        shared = _swiglu(xf, sW1, sW2, sW3)
        h = jax.nn.silu(jnp.einsum('td,efd->etf', xf, eW1)) * jnp.einsum('td,efd->etf', xf, eW3)
        eo = jnp.einsum('etf,edf->etd', h, eW2)
        specialist = jnp.einsum('te,etd->td', combine, eo)
        moe_out = (shared + specialist).reshape(B, S, d)
        return X + moe_out
    x = x + _L0_xcond_ref(cond_1024, ctx_1024, _layernorm(x, axis=-1), L0_xcond_q_mu, L0_xcond_q_logsig, L0_xcond_lnkv_g, L0_xcond_lnkv_b, L0_xcond_lnq_g, L0_xcond_lnq_b, L0_xcond_lnm_g, L0_xcond_lnm_b, L0_xcond_lnp_g, L0_xcond_lnp_b, L0_xcond_wk, L0_xcond_bk, L0_xcond_wv, L0_xcond_bv, L0_xcond_wq, L0_xcond_bq, L0_xcond_wu, L0_xcond_bu, L0_xcond_w1, L0_xcond_b1, L0_xcond_w2, L0_xcond_b2)
    x = x + _L0_ffn_ref(_layernorm(x, axis=-1), L0_ffn_gate_w, L0_ffn_experts_gate_up, L0_ffn_experts_down, L0_ffn_shared_gate_w, L0_ffn_shared_up_w, L0_ffn_shared_down_w, L0_ffn_shared_expert_gate_w)
    x = x + _L1_xcond_ref(_layernorm(x, axis=-1), ctx_1024, cond_1024, L1_xcond_W_att, L1_xcond_V_att, L1_xcond_Wi, L1_xcond_Uh, L1_xcond_b)
    x = x + _L1_ffn_ref(_layernorm(x, axis=-1), L1_ffn_router_w, L1_ffn_expert_bias, L1_ffn_shared_w1, L1_ffn_shared_w2, L1_ffn_shared_w3, L1_ffn_routed_w1, L1_ffn_routed_w2, L1_ffn_routed_w3)
    x = x + _L2_xcond_ref(_layernorm(x, axis=-1), cond_1024[:, None, :], ctx_1024, L2_xcond_attn1_wq, L2_xcond_attn1_wk, L2_xcond_attn1_wv, L2_xcond_attn1_wo, L2_xcond_attn1_bo, L2_xcond_attn2_wq, L2_xcond_attn2_wk, L2_xcond_attn2_wv, L2_xcond_attn2_wo, L2_xcond_attn2_bo, L2_xcond_ff_w1, L2_xcond_ff_b1, L2_xcond_ff_w2, L2_xcond_ff_b2, L2_xcond_norm1_w, L2_xcond_norm1_b, L2_xcond_norm2_w, L2_xcond_norm2_b, L2_xcond_norm3_w, L2_xcond_norm3_b)
    x = x + _L2_ffn_ref(_layernorm(x, axis=-1), L2_ffn_fast_b, L2_ffn_w_fc, L2_ffn_w_proj, L2_ffn_u, L2_ffn_v, L2_ffn_gate)
    x = x + _L3_xcond_ref(_layernorm(x, axis=-1), cond_1024[:, None, :], ctx_1024, mask_BxS_bf0, mask_BxS2_bf0, L3_xcond_n1_w, L3_xcond_n1_b, L3_xcond_n2_w, L3_xcond_n2_b, L3_xcond_n3_w, L3_xcond_n3_b, L3_xcond_qkv_w, L3_xcond_so_w, L3_xcond_cq_w, L3_xcond_ck_w, L3_xcond_cv_w, L3_xcond_co_w, L3_xcond_f1_w, L3_xcond_f1_b, L3_xcond_f2_w, L3_xcond_f2_b)
    x = x + _L3_ffn_ref(_layernorm(x, axis=-1), L3_ffn_g1, L3_ffn_g2, L3_ffn_Wq, L3_ffn_Wkc, L3_ffn_Wvc, L3_ffn_Wo, L3_ffn_Wr, L3_ffn_expert_bias, L3_ffn_sW1, L3_ffn_sW2, L3_ffn_sW3, L3_ffn_eW1, L3_ffn_eW2, L3_ffn_eW3)
    return x

_drawn_inputs = setup_inputs


def setup_inputs(seed=0):
    import zlib

    import numpy as np

    out = dict(_drawn_inputs(seed))
    spreads = {'L0_xcond_lnkv_g': (1.0, 0.6),
     'L0_xcond_lnkv_b': (0.0, 0.8),
     'L0_xcond_lnq_g': (1.0, 0.6),
     'L0_xcond_lnq_b': (0.0, 0.8),
     'L0_xcond_lnm_g': (1.0, 0.6),
     'L0_xcond_lnm_b': (0.0, 0.8),
     'L0_xcond_lnp_g': (1.0, 0.2),
     'L0_xcond_lnp_b': (0.0, 0.1),
     'L0_xcond_bk': (0.0, 0.8),
     'L0_xcond_bv': (0.0, 0.531),
     'L0_xcond_bq': (0.0, 0.8),
     'L0_xcond_bu': (0.0, 0.1),
     'L0_xcond_b1': (0.0, 0.8),
     'L0_xcond_b2': (0.0, 0.1),
     'L1_xcond_b': (0.0, 0.1),
     'L1_ffn_expert_bias': (0.0, 0.8),
     'L3_xcond_n1_b': (0.0, 0.8),
     'L3_xcond_n2_b': (0.0, 0.8),
     'L3_xcond_n3_b': (0.0, 0.8),
     'L3_xcond_f1_b': (0.0, 0.8),
     'L3_xcond_f2_b': (0.0, 0.1),
     'L3_ffn_g1': (1.0, 0.6),
     'L3_ffn_g2': (1.0, 0.6),
     'L3_ffn_expert_bias': (0.0, 0.8)}
    factors = {'L0_xcond_q_logsig': 8.0,
     'L0_xcond_wk': 5.724,
     'L0_xcond_wv': 2.708,
     'L0_xcond_wq': 5.791,
     'L0_xcond_w1': 4.078,
     'L0_xcond_w2': 3.736,
     'L0_ffn_gate_w': 8.0,
     'L0_ffn_experts_gate_up': 8.0,
     'L0_ffn_experts_down': 8.0,
     'L0_ffn_shared_gate_w': 8.0,
     'L0_ffn_shared_up_w': 8.0,
     'L0_ffn_shared_down_w': 8.0,
     'L0_ffn_shared_expert_gate_w': 8.0,
     'L1_ffn_router_w': 8.0,
     'L1_ffn_shared_w1': 8.0,
     'L1_ffn_shared_w2': 8.0,
     'L1_ffn_shared_w3': 8.0,
     'L1_ffn_routed_w1': 8.0,
     'L1_ffn_routed_w2': 8.0,
     'L1_ffn_routed_w3': 8.0,
     'L2_xcond_attn1_bo': 8.0,
     'L2_xcond_attn2_bo': 8.0,
     'L2_xcond_ff_b1': 8.0,
     'L2_xcond_ff_b2': 8.0,
     'L2_xcond_norm1_b': 7.399,
     'L2_xcond_norm2_b': 8.0,
     'L2_xcond_norm3_b': 8.0,
     'L2_ffn_fast_b': 8.0,
     'L2_ffn_w_fc': 8.0,
     'L2_ffn_w_proj': 8.0,
     'L2_ffn_u': 8.0,
     'L2_ffn_v': 8.0,
     'L3_xcond_n1_w': 8.0,
     'L3_xcond_n2_w': 8.0,
     'L3_xcond_n3_w': 8.0,
     'L3_xcond_qkv_w': 3.055,
     'L3_xcond_so_w': 3.217,
     'L3_xcond_cq_w': 8.0,
     'L3_xcond_ck_w': 8.0,
     'L3_xcond_cv_w': 5.27,
     'L3_xcond_co_w': 5.494,
     'L3_ffn_Wq': 8.0,
     'L3_ffn_Wkc': 8.0,
     'L3_ffn_Wvc': 8.0,
     'L3_ffn_Wo': 8.0,
     'L3_ffn_Wr': 8.0,
     'L3_ffn_sW1': 8.0,
     'L3_ffn_sW2': 8.0,
     'L3_ffn_sW3': 8.0,
     'L3_ffn_eW1': 8.0,
     'L3_ffn_eW2': 8.0,
     'L3_ffn_eW3': 8.0}
    for name, (base, spread) in spreads.items():
        noise = np.random.default_rng([zlib.crc32(name.encode()), seed]).standard_normal(out[name].shape)
        drawn = base * np.exp(spread * noise) if base else spread * noise
        out[name] = jnp.asarray(drawn.astype(out[name].dtype))
    for name, factor in factors.items():
        out[name] = (out[name] * factor).astype(out[name].dtype)
    return out
```

```python
import concourse.bass as bass
from concourse import mybir
from contextlib import ExitStack
import math
import numpy as np

F32 = mybir.dt.float32
BF16 = mybir.dt.bfloat16
U8 = mybir.dt.uint8
ALU = mybir.AluOpType
ACT = mybir.ActivationFunctionType
AX = mybir.AxisListType.X
AXY = mybir.AxisListType.XY

B, T, D, S = 2, 512, 128, 77
NT = B * T
P = 128
TT = T // P
NTT = NT // P
LN_EPS = 1e-5

E0, I0, SI0 = 8, 176, 352
E1, I1, SI1 = 16, 128, 512
H2, DH2 = 16, 64
INNER2, DFF2 = H2 * DH2, 4 * D
NL3, H3, DH3, DFF3 = 6, 16, 8, 512
E4, H4, DK4, F4 = 8, 4, 32, 128
HID5, RANK5 = 512, 16


class Steps:

    def __init__(self, k, stage, lanes, lead=0, **steps):
        self.sems, self.place, self.size, self.lead, self.lanes = {}, {}, {}, lead, lanes
        for engine, names in steps.items():
            names = names.split()
            self.size[engine] = len(names)
            for lane in range(lanes):
                self.sems[engine, lane] = k.semaphore(f"{stage}_{engine}_{lane}")
            for i, name in enumerate(names):
                assert name not in self.place, name
                self.place[name] = (engine, i)

    def sem(self, name, lane=0):
        return self.sems[self.place[name][0], lane], 1

    def at(self, name, lane=0, round=0):
        engine, i = self.place[name]
        return self.sems[engine, lane], round * self.size[engine] + (i + 1 + self.lead * self.size[engine])

    def prime(self, eng, engine):
        for lane in range(self.lanes):
            eng.sem_inc(self.sems[engine, lane], self.lead * self.size[engine])


class Core:

    def __init__(self, nc, ctx, dram, layout):
        def sb(name, shape, dt=F32):
            return ctx.enter_context(nc.sbuf_tensor(name, shape, dt))

        self.nc, self.dram, self.layout = nc, dram, layout
        self.x = sb("x_res", [P, B, T])
        self.xn = sb("x_norm", [P, B, T])
        self.y = sb("y", [P, B, T])
        self.cond = sb("condT", [P, B])
        self.ctxT = sb("ctxT", [P, B, S])
        self.mean_w = sb("mean_w", [P, P])
        self.ones = sb("ones", [P, P])
        self.ident = sb("ident", [P, P])
        self.eps = sb("eps", [P, 1])
        self.cent = sb("cent", [P, B, T])
        self.sq = sb("sq", [P, B, T])
        self.rstd = sb("rstd", [P, B, T])
        self.ps = ctx.enter_context(nc.psum_tensor("ps", [P, 8, 512], F32))
        self.signals = []

    def semaphore(self, name):
        self.signals.append(self.nc.alloc_semaphore(name))
        return self.signals[-1]

    def release(self):
        self.nc.clear_and_free_semaphores(self.signals)
        self.nc.all_engine_barrier()
        self.signals = []

    def weights(self, ctx, pack):
        rows = self.layout[pack]
        whole = ctx.enter_context(self.nc.sbuf_tensor("w_" + pack, [P, sum(n for _, _, n in rows)], F32))
        parts, at = {}, 0
        for name, p, n in rows:
            parts[name] = whole[0:p, at:at + n]
            at += n
        return whole, parts


LN_PE, LN_ACT, LN_DVE = "{0}.mean {0}.var", "{0}.sq {0}.ln {0}.rstd", "{0}.cent {0}.norm"
LNA_DVE = LN_DVE + " {0}.affine"


def ln_pe(k, pe, st, name, src, width, banks, lanes, ready, rnd=0):
    for c in range(lanes):
        ready(c)
        k.nc.tensor.matmul(k.ps[:, banks[c], 0:width], k.mean_w[:], src(c), start=True, stop=True)\
            .then_inc(*st.sem(name + ".mean", c))
    for c in range(lanes):
        pe.wait_ge(*st.at(name + ".sq", c, rnd))
        k.nc.tensor.matmul(k.ps[:, banks[c], 0:width], k.mean_w[:], k.sq[:, c, 0:width], start=True, stop=True)\
            .then_inc(*st.sem(name + ".var", c))


def ln_act(k, act, st, name, width, banks, lanes, rnd=0):
    for c in range(lanes):
        act.wait_ge(*st.at(name + ".cent", c, rnd))
        k.nc.scalar.activation(k.sq[:, c, 0:width], k.cent[:, c, 0:width], ACT.Square)\
            .then_inc(*st.sem(name + ".sq", c))
    k.nc.scalar.preload_act_table_set("natural_log_exp_and_others")
    for c in range(lanes):
        act.wait_ge(*st.at(name + ".var", c, rnd))
        k.nc.scalar.activation(k.rstd[:, c, 0:width], k.ps[:, banks[c], 0:width], ACT.Ln, bias=k.eps[:, 0:1])\
            .then_inc(*st.sem(name + ".ln", c))
        act.wait_ge(*st.at(name + ".ln", c, rnd))
        k.nc.scalar.activation(k.rstd[:, c, 0:width], k.rstd[:, c, 0:width], ACT.Exp, scale=-0.5)\
            .then_inc(*st.sem(name + ".rstd", c))


def ln_dve(k, dve, st, name, src, dst, width, banks, lanes, rnd=0, affine=None):
    for c in range(lanes):
        dve.wait_ge(*st.at(name + ".mean", c, rnd))
        k.nc.vector.tensor_tensor(k.cent[:, c, 0:width], src(c), k.ps[:, banks[c], 0:width], ALU.subtract)\
            .then_inc(*st.sem(name + ".cent", c))
    for c in range(lanes):
        dve.wait_ge(*st.at(name + ".rstd", c, rnd))
        k.nc.vector.tensor_tensor(dst(c), k.cent[:, c, 0:width], k.rstd[:, c, 0:width], ALU.mult)\
            .then_inc(*st.sem(name + ".norm", c))
        if affine is not None:
            gain, shift = affine(c)
            dve.wait_ge(*st.at(name + ".norm", c, rnd))
            k.nc.vector.tensor_scalar(dst(c), dst(c), gain, shift, ALU.mult, ALU.add)\
                .then_inc(*st.sem(name + ".affine", c))


def setup_stage(k):
    nc = k.nc
    with ExitStack() as ctx:
        made = k.semaphore("constants_made")
        landed = k.semaphore("inputs_landed")
        block = ctx.enter_context(nc.Block())

        @block.sync
        def _(sp):
            sp.dma_start(k.x[:], k.dram["x"]).then_inc(landed, 16)
            sp.dma_start(k.ctxT[:], k.dram["ctx"]).then_inc(landed, 16)
            sp.dma_start(k.cond[:], k.dram["cond"]).then_inc(landed, 16)
            sp.wait_ge(landed, 16 * 3)

        @block.gpsimd
        def _(pool):
            nc.gpsimd.memset(k.ident[:], 0.0).then_inc(made, 1)
            nc.gpsimd.memset(k.mean_w[:], 1.0 / D).then_inc(made, 1)
            nc.gpsimd.memset(k.ones[:], 1.0).then_inc(made, 1)
            nc.gpsimd.memset(k.eps[:], LN_EPS).then_inc(made, 1)
            pool.wait_ge(made, 4)
            nc.gpsimd.affine_select(out=k.ident[:], in_=k.ident[:], compare_op=ALU.not_equal, fill=1.0, base=0,
                                    pattern=[[-1, P]], channel_multiplier=1).then_inc(made, 1)
            pool.wait_ge(made, 5)


def load_stage(k, whole, pack):
    with ExitStack() as ctx:
        landed = k.semaphore("landed_" + pack)
        block = ctx.enter_context(k.nc.Block())

        @block.sync
        def _(sp):
            sp.dma_start(whole[:], k.dram[pack]).then_inc(landed, 16)
            sp.wait_ge(landed, 16)


def store_stage(k, out):
    nc = k.nc
    with ExitStack() as ctx:
        stored = k.semaphore("result_stored")
        block = ctx.enter_context(nc.Block())

        @block.sync
        def _(sp):
            sp.dma_start(out, k.x[:]).then_inc(stored, 16)
            sp.wait_ge(stored, 16)


def slots_stage(k, w):
    nc, ps = k.nc, k.ps
    ROUNDS = 3
    SCALE = math.sqrt(D)
    with ExitStack() as ctx:
        def sb(name, shape, dt=F32):
            return ctx.enter_context(nc.sbuf_tensor("s0_" + name, shape, dt))

        slots, mid, y, q, hid = (sb(n, [P, B, T]) for n in ("slots", "mid", "y", "q", "hid"))
        cn, kT = sb("cn", [P, B, S]), sb("kT", [P, B, S])
        v = sb("v", [P, B, D])
        e, rsum = sb("e", [P, B, T]), sb("rsum", [P, B, T])
        top, ssum = sb("top", [P, B]), sb("ssum", [P, B])
        sig, base = sb("sig", [P, 1]), sb("base", [P, B])
        BANK = (0, 4)
        pre = Steps(k, "s0pre", 2,
                    pe="c.mean c.var x.mean x.var key value", act="c.sq c.ln c.rstd x.sq x.ln x.rstd sig",
                    dve="c.cent c.norm c.affine x.cent x.norm kT v base slots")
        st = Steps(k, "s0", 2,
                   pe="q.mean q.var query logit colsum upd wu m.mean m.var w1 w2 p.mean p.var",
                   act="q.sq q.ln q.rstd e m.sq m.ln m.rstd gelu p.sq p.ln p.rstd",
                   dve="q.cent q.norm q.affine qT top tops inv attn rsum updn wuo m.cent m.norm m.affine w2o "
                       "p.cent p.norm p.affine")
        end = k.semaphore("s0_added")
        block = ctx.enter_context(nc.Block())

        @block.tensor
        def _(pe):
            ln_pe(k, pe, pre, "c", lambda c: k.ctxT[:, c], S, (1, 5), 2, lambda c: None)
            ln_pe(k, pe, pre, "x", lambda c: k.x[:, c], T, BANK, 2, lambda c: None if c else pe.wait_ge(*pre.at("c.rstd", 1)))
            for c in range(B):
                pe.wait_ge(*pre.at("c.affine", c))
                nc.tensor.matmul(ps[:, 2 + 4 * c, 0:S], w["wk"], cn[:, c], start=True, stop=True).then_inc(*pre.sem("key", c))
                nc.tensor.matmul(ps[0:S, 3 + 4 * c, 0:D], cn[:, c], w["wv"], start=True, stop=False)
                nc.tensor.matmul(ps[0:S, 3 + 4 * c, 0:D], k.ones[0:1, 0:S], w["bv"], start=False, stop=True)\
                    .then_inc(*pre.sem("value", c))
            for r in range(ROUNDS):
                ready = (lambda c: pe.wait_ge(*pre.at("slots", c))) if r == 0 else \
                    (lambda c: pe.wait_ge(*st.at("p.affine", c, r - 1)))
                ln_pe(k, pe, st, "q", lambda c: slots[:, c], T, BANK, 2, ready, r)
                for c in range(B):
                    pe.wait_ge(*st.at("q.affine", c, r))
                    nc.tensor.matmul(ps[:, 1 + 4 * c], w["wq"], y[:, c], start=True, stop=True).then_inc(*st.sem("query", c))
                for c in range(B):
                    pe.wait_ge(*st.at("qT", c, r))
                    nc.tensor.matmul(ps[0:S, 2 + 4 * c], kT[:, c], q[:, c], start=True, stop=True).then_inc(*st.sem("logit", c))
                for c in range(B):
                    pe.wait_ge(*st.at("attn", c, r))
                    nc.tensor.matmul(ps[:, 3 + 4 * c], k.ones[0:S, :], e[0:S, c], start=True, stop=True)\
                        .then_inc(*st.sem("colsum", c))
                    nc.tensor.matmul(ps[:, 1 + 4 * c], v[0:S, c], e[0:S, c], start=True, stop=True)\
                        .then_inc(*st.sem("upd", c))
                for c in range(B):
                    pe.wait_ge(*st.at("updn", c, r))
                    nc.tensor.matmul(ps[:, 2 + 4 * c], w["wu"], y[:, c], start=True, stop=True).then_inc(*st.sem("wu", c))
                ln_pe(k, pe, st, "m", lambda c: mid[:, c], T, BANK, 2, lambda c: pe.wait_ge(*st.at("wuo", c, r)), r)
                for c in range(B):
                    pe.wait_ge(*st.at("m.affine", c, r))
                    nc.tensor.matmul(ps[:, 1 + 4 * c], w["w1"], y[:, c], start=True, stop=True).then_inc(*st.sem("w1", c))
                for c in range(B):
                    pe.wait_ge(*st.at("gelu", c, r))
                    nc.tensor.matmul(ps[:, 2 + 4 * c], w["w2"], hid[:, c], start=True, stop=True).then_inc(*st.sem("w2", c))
                ln_pe(k, pe, st, "p", lambda c: mid[:, c], T, BANK, 2, lambda c: pe.wait_ge(*st.at("w2o", c, r)), r)

        @block.scalar
        def _(act):
            ln_act(k, act, pre, "c", S, (1, 5), 2)
            ln_act(k, act, pre, "x", T, BANK, 2)
            nc.scalar.activation(sig[:], w["q_logsig"], ACT.Exp).then_inc(*pre.sem("sig"))
            for r in range(ROUNDS):
                ln_act(k, act, st, "q", T, BANK, 2, r)
                for c in range(B):
                    act.wait_ge(*st.at("tops", c, r))
                    nc.scalar.activation(e[0:S, c], ps[0:S, 2 + 4 * c], ACT.Exp, bias=top[0:S, c:c + 1], scale=SCALE,
                                         accum_out=ssum[0:S, c:c + 1]).then_inc(*st.sem("e", c))
                ln_act(k, act, st, "m", T, BANK, 2, r)
                for c in range(B):
                    act.wait_ge(*st.at("w1", c, r))
                    nc.scalar.activation(hid[:, c], ps[:, 1 + 4 * c], ACT.Gelu, bias=w["b1"]).then_inc(*st.sem("gelu", c))
                ln_act(k, act, st, "p", T, BANK, 2, r)

        @block.vector
        def _(dve):
            ln_dve(k, dve, pre, "c", lambda c: k.ctxT[:, c], lambda c: cn[:, c], S, (1, 5), 2,
                   affine=lambda c: (w["lnkv_g"], w["lnkv_b"]))
            ln_dve(k, dve, pre, "x", lambda c: k.x[:, c], lambda c: k.xn[:, c], T, BANK, 2)
            for c in range(B):
                dve.wait_ge(*pre.at("key", c))
                nc.vector.tensor_scalar(kT[:, c], ps[:, 2 + 4 * c, 0:S], w["bk"], None, ALU.add).then_inc(*pre.sem("kT", c))
                dve.wait_ge(*pre.at("value", c))
                nc.vector.tensor_copy(v[0:S, c], ps[0:S, 3 + 4 * c, 0:D]).then_inc(*pre.sem("v", c))
                nc.vector.tensor_tensor(base[:, c:c + 1], w["b2"], k.cond[:, c:c + 1], ALU.add).then_inc(*pre.sem("base", c))
                if c == 0:
                    dve.wait_ge(*pre.at("sig"))
                dve.wait_ge(*pre.at("x.norm", c))
                nc.vector.tensor_scalar(slots[:, c], k.xn[:, c], sig[:, 0:1], w["q_mu"], ALU.mult, ALU.add)\
                    .then_inc(*pre.sem("slots", c))
            for r in range(ROUNDS):
                ln_dve(k, dve, st, "q", lambda c: slots[:, c], lambda c: y[:, c], T, BANK, 2, r,
                       affine=lambda c: (w["lnq_g"], w["lnq_b"]))
                for c in range(B):
                    dve.wait_ge(*st.at("query", c, r))
                    nc.vector.tensor_scalar(q[:, c], ps[:, 1 + 4 * c], w["bq"], None, ALU.add).then_inc(*st.sem("qT", c))
                for c in range(B):
                    dve.wait_ge(*st.at("logit", c, r))
                    nc.vector.tensor_reduce(top[0:S, c:c + 1], ps[0:S, 2 + 4 * c], AX, ALU.max, negate=True)\
                        .then_inc(*st.sem("top", c))
                    dve.wait_ge(*st.at("top", c, r))
                    nc.vector.tensor_scalar(top[0:S, c:c + 1], top[0:S, c:c + 1], SCALE, None, ALU.mult)\
                        .then_inc(*st.sem("tops", c))
                for c in range(B):
                    dve.wait_ge(*st.at("e", c, r))
                    nc.vector.reciprocal(ssum[0:S, c:c + 1], ssum[0:S, c:c + 1]).then_inc(*st.sem("inv", c))
                    dve.wait_ge(*st.at("inv", c, r))
                    nc.vector.tensor_scalar(e[0:S, c], e[0:S, c], ssum[0:S, c:c + 1], 1e-8, ALU.mult, ALU.add)\
                        .then_inc(*st.sem("attn", c))
                for c in range(B):
                    dve.wait_ge(*st.at("colsum", c, r))
                    nc.vector.reciprocal(rsum[:, c], ps[:, 3 + 4 * c]).then_inc(*st.sem("rsum", c))
                    dve.wait_ge(*st.at("upd", c, r))
                    dve.wait_ge(*st.at("rsum", c, r))
                    nc.vector.tensor_tensor(y[:, c], rsum[:, c], ps[:, 1 + 4 * c], ALU.mult).then_inc(*st.sem("updn", c))
                for c in range(B):
                    dve.wait_ge(*st.at("wu", c, r))
                    nc.vector.scalar_tensor_tensor(out=mid[:, c], in0=ps[:, 2 + 4 * c], scalar=w["bu"], in1=slots[:, c],
                                                   op0=ALU.add, op1=ALU.add).then_inc(*st.sem("wuo", c))
                ln_dve(k, dve, st, "m", lambda c: mid[:, c], lambda c: y[:, c], T, BANK, 2, r,
                       affine=lambda c: (w["lnm_g"], w["lnm_b"]))
                for c in range(B):
                    dve.wait_ge(*st.at("w2", c, r))
                    nc.vector.scalar_tensor_tensor(out=mid[:, c], in0=ps[:, 2 + 4 * c], scalar=base[:, c:c + 1],
                                                   in1=mid[:, c], op0=ALU.add, op1=ALU.add).then_inc(*st.sem("w2o", c))
                ln_dve(k, dve, st, "p", lambda c: mid[:, c], lambda c: slots[:, c], T, BANK, 2, r,
                       affine=lambda c: (w["lnp_g"], w["lnp_b"]))
            for c in range(B):
                dve.wait_ge(*st.at("p.affine", c, ROUNDS - 1))
                nc.vector.tensor_tensor(k.x[:, c], k.x[:, c], slots[:, c], ALU.add).then_inc(end, 1)
            dve.wait_ge(end, 2)


def norm_stage(k, label):
    nc = k.nc
    with ExitStack() as ctx:
        st = Steps(k, label, 2, pe=LN_PE.format("x"), act=LN_ACT.format("x"), dve=LN_DVE.format("x"))
        block = ctx.enter_context(nc.Block())

        @block.tensor
        def _(pe):
            ln_pe(k, pe, st, "x", lambda c: k.x[:, c], T, (0, 4), 2, lambda c: None)

        @block.scalar
        def _(act):
            ln_act(k, act, st, "x", T, (0, 4), 2)

        @block.vector
        def _(dve):
            ln_dve(k, dve, st, "x", lambda c: k.x[:, c], lambda c: k.xn[:, c], T, (0, 4), 2)
            for c in range(B):
                dve.wait_ge(*st.at("x.norm", c))


PICK = "{0}.max {0}.eq {0}.rank {0}.first {0}.pick"


def pick_dve(k, dve, st, name, sel, top, first, eq, rank, pick, E):
    V = k.nc.vector
    V.tensor_reduce(top[:], sel[:], AX, ALU.max).then_inc(*st.sem(name + ".max"))
    dve.wait_ge(*st.at(name + ".max"))
    V.tensor_tensor(eq[:], sel[:], top[:].unsqueeze(2).broadcast_to([P, NTT, E]), ALU.is_equal).then_inc(*st.sem(name + ".eq"))
    dve.wait_ge(*st.at(name + ".eq"))
    V.tensor_tensor(eq[:], eq[:], rank.unsqueeze(1).broadcast_to([P, NTT, E]), ALU.mult).then_inc(*st.sem(name + ".rank"))
    dve.wait_ge(*st.at(name + ".rank"))
    V.tensor_reduce(first[:], eq[:], AX, ALU.max).then_inc(*st.sem(name + ".first"))
    dve.wait_ge(*st.at(name + ".first"))
    V.tensor_tensor(pick[:], eq[:], first[:].unsqueeze(2).broadcast_to([P, NTT, E]), ALU.is_equal).then_inc(*st.sem(name + ".pick"))
    dve.wait_ge(*st.at(name + ".pick"))


def moe_stage(k, label, kind, E, I, n_shared, expert_dram, w):
    nc, ps = k.nc, k.ps
    N = E + n_shared
    cuts = [(i, min(P, I - i)) for i in range(0, I, P)]
    nk = len(cuts)
    WC = 2 * I + nk * D
    with ExitStack() as ctx:
        def sb(name, shape, dt=F32):
            return ctx.enter_context(nc.sbuf_tensor(f"{label}_{name}", shape, dt))

        logit, sel, eq, pick1, pick2 = (sb(n, [P, NTT, E]) for n in ("logit", "sel", "eq", "pick1", "pick2"))
        gate = sb("gate", [P, NTT, N])
        top1, top2, first, tot = (sb(n, [P, NTT]) for n in ("top1", "top2", "first", "tot"))
        sg = sb("sg", [P, NTT])
        wb = [sb(f"wexp{i}", [P, WC]) for i in range(2)]
        th = sb("th", [P, B, nk, T])
        h = sb("h", [P, 2, B, nk, T])
        scaled = sb("scaled", [P, B, TT, D])
        acc = sb("acc", [P, B, TT, D])
        scored = "score sel" if kind == "sigmoid" else "lg max sub sum inv score sel"
        gated = "both gates" if kind != "renorm" else "gap more inv2 w2 g1 g2 gates"
        rt = Steps(k, label + "r", 1, pe="logits",
                   act="prob" + (" gap_exp" if kind == "renorm" else " shared_tanh" if kind == "scores" else ""),
                   dve=" ".join((scored, PICK.format("a"), "drop", PICK.format("b"), gated, "shared")), pool="acc0")
        R = E + (kind == "scores")
        st = Steps(k, label, 2,
                   pe=" ".join(f"gu{i}" for i in range(nk)), act=" ".join(f"t{i}" for i in range(nk)),
                   dve=" ".join(f"s{i} h{i}" for i in range(nk)))
        dn = Steps(k, label + "d", 2, pe="y", dve="scaled", pool="added")
        landed = [k.semaphore(f"{label}_expert_landed{i}") for i in range(2)]
        turned = k.semaphore(f"{label}_turned")
        ended = k.semaphore(f"{label}_ended")
        peel = 2 if N % 2 == 0 else 3
        GB, UB, YB = (0, 3), (1, 4), (2, 5)
        block = ctx.enter_context(nc.Block())

        def rounds(eng, body):
            for e in range(peel):
                body(e, e % 2, e, e // 2)
            with eng.Fori(0, (N - peel) // 2) as j:
                for u in range(2):
                    body(peel + u + 2 * j, (peel + u) % 2, 3, (peel + u) // 2 + j)

        @block.sync
        def _(sp):
            def load(e, b, lead, n):
                if lead >= 2:
                    for c in range(B):
                        sp.wait_ge(*dn.at("y", c, e - 2))
                sp.dma_start(wb[b][:], expert_dram[bass.ds(e, 1)].rearrange("e p n -> (e p) n")
                             if lead == 3 else expert_dram[e]).then_inc(landed[b], 16)
            rounds(sp, load)
            sp.wait_ge(landed[0], 16 * ((N + 1) // 2))
            sp.wait_ge(landed[1], 16 * (N // 2))

        @block.tensor
        def _(pe):
            for t in range(NTT):
                mm = nc.tensor.matmul(ps[:, 6, t * R:(t + 1) * R], k.xn[:, t // TT, (t % TT) * P:(t % TT + 1) * P],
                                      w["router"], start=True, stop=True)
            mm.then_inc(*rt.sem("logits"))

            def up(e, b, lead, n):
                pe.wait_ge(landed[b], 16 * (n + 1))
                for i, (o, m) in enumerate(cuts):
                    for c in range(B):
                        if i > 0:
                            pe.wait_ge(*st.at(f"h{i - 1}", c, e))
                        elif lead:
                            pe.wait_ge(*st.at(f"h{nk - 1}", c, e - 1))
                        nc.tensor.matmul(ps[0:m, GB[c]], wb[b][:, o:o + m], k.xn[:, c], start=True, stop=True)
                        nc.tensor.matmul(ps[0:m, UB[c]], wb[b][:, I + o:I + o + m], k.xn[:, c], start=True, stop=True)\
                            .then_inc(*st.sem(f"gu{i}", c))

            def down(e, b, lead):
                for c in range(B):
                    pe.wait_ge(*st.at(f"h{nk - 1}", c, e))
                    if lead:
                        pe.wait_ge(*dn.at("scaled", c, e - 1))
                    for t in range(TT):
                        for i, (o, m) in enumerate(cuts):
                            mm = nc.tensor.matmul(ps[:, YB[c], t * D:(t + 1) * D], h[0:m, b, c, i, t * P:(t + 1) * P],
                                                  wb[b][0:m, 2 * I + i * D:2 * I + (i + 1) * D],
                                                  start=(i == 0), stop=(i == nk - 1))
                    mm.then_inc(*dn.sem("y", c))

            def body(e, b, lead, n):
                up(e, b, lead, n)
                if lead:
                    down(e - 1, 1 - b, min(lead - 1, 1))
            rounds(pe, body)
            down(N - 1, (N - 1) % 2, 1)
            pe.wait_ge(*dn.at("scaled", 0, N - 1))
            pe.wait_ge(*dn.at("scaled", 1, N - 1))
            for c in range(B):
                pe.wait_ge(*dn.at("added", c, N - 1))
                for t in range(TT):
                    mm = nc.tensor.transpose(ps[:, YB[c], t * P:(t + 1) * P], acc[:, c, t], k.ident[:])
                mm.then_inc(turned, 1)

        @block.scalar
        def _(act):
            lg = ps[:, 6, 0:NTT * R].rearrange("p (t e) -> p t e", e=R)
            if kind == "sigmoid":
                act.wait_ge(*rt.at("logits"))
                nc.scalar.activation(logit[:], lg[:, :, 0:E], ACT.Tanh, scale=0.5).then_inc(*rt.sem("prob"))
            else:
                act.wait_ge(*rt.at("sub"))
                nc.scalar.activation(logit[:], logit[:], ACT.Exp).then_inc(*rt.sem("prob"))
            if kind == "renorm":
                act.wait_ge(*rt.at("gap"))
                nc.scalar.activation(first[:], first[:], ACT.Exp).then_inc(*rt.sem("gap_exp"))
            if kind == "scores":
                nc.scalar.activation(sg[:], lg[:, :, E], ACT.Tanh, scale=0.5).then_inc(*rt.sem("shared_tanh"))

            def body(e, b, lead, n):
                for i, (o, m) in enumerate(cuts):
                    for c in range(B):
                        act.wait_ge(*st.at(f"gu{i}", c, e))
                        nc.scalar.activation(th[0:m, c, i], ps[0:m, GB[c]], ACT.Tanh, scale=0.5).then_inc(*st.sem(f"t{i}", c))
            rounds(act, body)

        @block.gpsimd
        def _(pool):
            nc.gpsimd.memset(acc[:], 0.0).then_inc(*rt.sem("acc0"))
            pool.wait_ge(*rt.at("acc0"))

            def body(e, b, lead, n):
                for c in range(B):
                    pool.wait_ge(*dn.at("scaled", c, e))
                    if lead:
                        pool.wait_ge(*dn.at("added", c, e - 1))
                    nc.gpsimd.tensor_tensor(acc[:, c], acc[:, c], scaled[:, c], ALU.add).then_inc(*dn.sem("added", c))
            rounds(pool, body)

        @block.vector
        def _(dve):
            V = nc.vector
            lg = ps[:, 6, 0:NTT * R].rearrange("p (t e) -> p t e", e=R)

            def wide(a):
                return a[:].unsqueeze(2).broadcast_to([P, NTT, E])

            def over_tokens(a):
                return a.unsqueeze(1).broadcast_to([P, NTT, E])

            def step(name, ins):
                ins.then_inc(*rt.sem(name))
                dve.wait_ge(*rt.at(name))

            if kind == "sigmoid":
                dve.wait_ge(*rt.at("prob"))
                step("score", V.tensor_scalar(logit[:], logit[:], 0.5, 0.5, ALU.mult, ALU.add))
                step("sel", V.tensor_tensor(sel[:], logit[:], over_tokens(w["bias"]), ALU.add))
            else:
                dve.wait_ge(*rt.at("logits"))
                if kind == "renorm":
                    step("lg", V.tensor_tensor(logit[:], lg[:, :, 0:E], over_tokens(w["bias"]), ALU.add))
                else:
                    step("lg", V.tensor_copy(logit[:], lg[:, :, 0:E]))
                step("max", V.tensor_reduce(top1[:], logit[:], AX, ALU.max))
                step("sub", V.tensor_tensor(logit[:], logit[:], wide(top1), ALU.subtract))
                dve.wait_ge(*rt.at("prob"))
                step("sum", V.tensor_reduce(tot[:], logit[:], AX, ALU.add))
                step("inv", V.reciprocal(tot[:], tot[:]))
                step("score", V.tensor_tensor(logit[:], logit[:], wide(tot), ALU.mult))
                step("sel", V.tensor_copy(sel[:], logit[:]))
            pick_dve(k, dve, rt, "a", sel, top1, first, eq, w["rank"], pick1, E)
            step("drop", V.scalar_tensor_tensor(out=sel[:], in0=pick1[:], scalar=-3e38, in1=sel[:],
                                                op0=ALU.mult, op1=ALU.add))
            pick_dve(k, dve, rt, "b", sel, top2, first, eq, w["rank"], pick2, E)
            if kind == "renorm":
                step("gap", V.tensor_tensor(first[:], top2[:], top1[:], ALU.subtract))
                dve.wait_ge(*rt.at("gap_exp"))
                step("more", V.tensor_scalar(tot[:], first[:], 1.0, None, ALU.add))
                step("inv2", V.reciprocal(top1[:], tot[:]))
                step("w2", V.tensor_tensor(top2[:], first[:], top1[:], ALU.mult))
                step("g1", V.tensor_tensor(pick1[:], pick1[:], wide(top1), ALU.mult))
                step("g2", V.tensor_tensor(pick2[:], pick2[:], wide(top2), ALU.mult))
                step("gates", V.tensor_tensor(gate[:, :, 0:E], pick1[:], pick2[:], ALU.add))
            else:
                step("both", V.tensor_tensor(pick1[:], pick1[:], pick2[:], ALU.add))
                step("gates", V.tensor_tensor(gate[:, :, 0:E], pick1[:], logit[:], ALU.mult))
            if kind == "scores":
                dve.wait_ge(*rt.at("shared_tanh"))
                step("shared", V.tensor_scalar(gate[:, :, E:N], sg[:].unsqueeze(2).broadcast_to([P, NTT, n_shared]),
                                               0.5, 0.5, ALU.mult, ALU.add))
            else:
                step("shared", V.memset(gate[:, :, E:N], 1.0))

            def body(e, b, lead, n):
                for i, (o, m) in enumerate(cuts):
                    for c in range(B):
                        dve.wait_ge(*st.at(f"t{i}", c, e))
                        V.scalar_tensor_tensor(out=th[0:m, c, i], in0=th[0:m, c, i], scalar=1.0, in1=ps[0:m, GB[c]],
                                               op0=ALU.add, op1=ALU.mult).then_inc(*st.sem(f"s{i}", c))
                    for c in range(B):
                        dve.wait_ge(*st.at(f"s{i}", c, e))
                        if lead >= 2 and i == 0:
                            dve.wait_ge(*dn.at("y", c, e - 2))
                        V.scalar_tensor_tensor(out=h[0:m, b, c, i], in0=th[0:m, c, i], scalar=0.5, in1=ps[0:m, UB[c]],
                                               op0=ALU.mult, op1=ALU.mult).then_inc(*st.sem(f"h{i}", c))
                if lead:
                    scale(e - 1, min(lead - 1, 1))

            def scale(e, lead):
                for c in range(B):
                    dve.wait_ge(*dn.at("y", c, e))
                    if lead:
                        dve.wait_ge(*dn.at("added", c, e - 1))
                    g = gate[:, c * TT:(c + 1) * TT, bass.ds(e, 1)] if not isinstance(e, int) else gate[:, c * TT:(c + 1) * TT, e:e + 1]
                    V.tensor_tensor(scaled[:, c], ps[:, YB[c]].rearrange("p (t d) -> p t d", d=D),
                                    g.broadcast_to([P, TT, D]), ALU.mult).then_inc(*dn.sem("scaled", c))
            rounds(dve, body)
            scale(N - 1, 1)
            for c in range(B):
                dve.wait_ge(turned, c + 1)
                V.tensor_tensor(k.x[:, c], k.x[:, c], ps[:, YB[c]], ALU.add).then_inc(ended, 1)
            dve.wait_ge(ended, 2)


def gru_stage(k, w):
    nc, ps = k.nc, k.ps
    UNROLL = 16
    with ExitStack() as ctx:
        def sb(name, shape, dt=F32):
            return ctx.enter_context(nc.sbuf_tensor("g_" + name, shape, dt))

        gx = sb("gx", [P, T + 1, 8])
        encp = sb("encp", [P, B, S])
        enc = sb("enc", [P, B, D])
        h = [sb(f"h{i}", [P, B]) for i in range(2)]
        th = sb("th", [P, B, S])
        ntop = sb("ntop", [1, B])
        e, sinv, cv = sb("e", [P, B]), sb("sinv", [P, B]), sb("cv", [P, B])
        tzr, rhh, hin, hh = sb("tzr", [P, 4]), sb("rhh", [P, B]), sb("hin", [P, B]), sb("hh", [P, B])
        omz, zz, zh = sb("omz", [P, B]), sb("zz", [P, B]), sb("zh", [P, B])
        with ExitStack() as pctx:
            pre = Steps(k, "gpre", 2, pe="encp turn g0 g1 g2", dve="encp_s turn_s gx0 gx1 gx2", pool="zero h0")
            block = pctx.enter_context(nc.Block())

            @block.tensor
            def _(pe):
                for c in range(B):
                    nc.tensor.matmul(ps[:, 4 * c, 0:S], w["att_e"], k.ctxT[:, c], start=True, stop=True).then_inc(*pre.sem("encp", c))
                    nc.tensor.transpose(ps[0:S, 4 * c + 1, 0:D], k.ctxT[:, c], k.ident[:]).then_inc(*pre.sem("turn", c))
                for g in range(3):
                    for c in range(B):
                        if g >= 2:
                            pe.wait_ge(*pre.at(f"gx{g - 2}", c))
                        nc.tensor.matmul(ps[:, 4 * c + 2 + g % 2], w["wix"][:, g * D:(g + 1) * D], k.xn[:, c],
                                         start=True, stop=True).then_inc(*pre.sem(f"g{g}", c))

            @block.gpsimd
            def _(pool):
                nc.gpsimd.memset(gx[:, :, 6:8], 0.0).then_inc(*pre.sem("zero", 0))
                nc.gpsimd.memset(gx[:, T:T + 1, 0:6], 0.0).then_inc(*pre.sem("zero", 1))
                nc.gpsimd.tensor_copy(h[0][:], k.cond[:]).then_inc(*pre.sem("h0"))
                pool.wait_ge(*pre.at("h0"))
                pool.wait_ge(*pre.at("zero", 1))

            @block.vector
            def _(dve):
                V = nc.vector
                for c in range(B):
                    dve.wait_ge(*pre.at("encp", c))
                    V.tensor_copy(encp[:, c], ps[:, 4 * c, 0:S]).then_inc(*pre.sem("encp_s", c))
                    dve.wait_ge(*pre.at("turn", c))
                    V.tensor_copy(enc[0:S, c], ps[0:S, 4 * c + 1, 0:D]).then_inc(*pre.sem("turn_s", c))
                for g in range(3):
                    for c in range(B):
                        dve.wait_ge(*pre.at(f"g{g}", c))
                        V.tensor_scalar(gx[:, 0:T, 2 * g + c], ps[:, 4 * c + 2 + g % 2], w["bi"][:, g:g + 1], None, ALU.add)\
                            .then_inc(*pre.sem(f"gx{g}", c))
                for c in range(B):
                    dve.wait_ge(*pre.at("gx2", c))

        st = Steps(k, "g", 1, pe="att uh row cols shift sum ctx zr hc",
                   act="tanh exp gates cand", dve="rhh ntop sinv cv hin omz zz zh h", pool="saved")
        block = ctx.enter_context(nc.Block())
        att = [ps[:, i, 0:B * S] for i in range(2)]
        gates = [ps[:, 2 + i, 0:4] for i in range(2)]
        cols, row, usum, uctx = ps[0:S, 4, 0:B], ps[0:1, 5, 0:B * S], ps[:, 5, 0:B], ps[:, 6, 0:B]
        cand = ps[:, 7, 0:4]

        def steps(eng, body):
            with eng.Fori(0, T // UNROLL) as j:
                for u in range(UNROLL):
                    body(j * UNROLL + u, u % 2)

        @block.tensor
        def _(pe):
            M = nc.tensor.matmul

            def open_att(p):
                M(att[p], k.ident[:], encp[:].rearrange("p b s -> p (b s)"), start=True, stop=False, skip_group_check=True)

            def open_gates(p, t):
                M(gates[p], k.ident[:], gx[:, bass.ds(t, 1), 0:4].rearrange("p o g -> p (o g)"), start=True, stop=False,
                  skip_group_check=True)

            open_att(0)
            open_gates(0, 0)

            def body(t, p):
                pe.wait_ge(*st.at("h", round=t))
                M(att[p].rearrange("p (b s) -> p b s", b=B), w["att_h"], h[p][:].unsqueeze(2).broadcast_to([P, B, S]),
                  start=False, stop=True, skip_group_check=True).then_inc(*st.sem("att"))
                M(cand, k.ident[:], gx[:, bass.ds(t, 1), 4:8].rearrange("p o g -> p (o g)"), start=True, stop=False,
                  skip_group_check=True)
                M(cand[:, 2:4], w["uh"][:, 2 * D:3 * D], h[p][:], start=False, stop=True, skip_group_check=True)\
                    .then_inc(*st.sem("uh"))
                pe.wait_ge(*st.at("tanh", round=t))
                M(row, w["v"], th[:].rearrange("p b s -> p (b s)"), start=True, stop=True).then_inc(*st.sem("row"))
                for c in range(B):
                    mm = M(cols[:, c:c + 1], th[:, c], w["v"], start=(c == 0), stop=False, skip_group_check=True)
                mm.then_inc(*st.sem("cols"))
                M(gates[p][:, 0:2], w["uh"][:, 0:D], h[p][:], start=False, stop=False, skip_group_check=True)
                M(gates[p][:, 2:4], w["uh"][:, D:2 * D], h[p][:], start=False, stop=False, skip_group_check=True)
                open_gates(1 - p, t + 1)
                pe.wait_ge(*st.at("ntop", round=t + 1))
                M(cols, k.ones[0:1, 0:S], ntop[:], start=False, stop=True, skip_group_check=True).then_inc(*st.sem("shift"))
                open_att(1 - p)
                pe.wait_ge(*st.at("exp", round=t))
                M(usum, k.ones[0:S, :], e[0:S], start=True, stop=True).then_inc(*st.sem("sum"))
                for c in range(B):
                    mm = M(uctx[:, c:c + 1], enc[0:S, c], e[0:S, c:c + 1], start=(c == 0), stop=(c == B - 1),
                           skip_group_check=True)
                mm.then_inc(*st.sem("ctx"))
                pe.wait_ge(*st.at("cv", round=t + 1))
                M(gates[p][:, 0:2], w["wic"][:, 0:D], cv[:], start=False, stop=False, skip_group_check=True)
                M(gates[p][:, 2:4], w["wic"][:, D:2 * D], cv[:], start=False, stop=True, skip_group_check=True)\
                    .then_inc(*st.sem("zr"))
                M(cand[:, 0:2], w["wic"][:, 2 * D:3 * D], cv[:], start=False, stop=True, skip_group_check=True)\
                    .then_inc(*st.sem("hc"))
            steps(pe, body)

        @block.scalar
        def _(act):
            A = nc.scalar.activation

            def body(t, p):
                act.wait_ge(*st.at("att", round=t))
                A(th[:].rearrange("p b s -> p (b s)"), att[p], ACT.Tanh).then_inc(*st.sem("tanh"))
                act.wait_ge(*st.at("shift", round=t))
                A(e[0:S], cols, ACT.Exp).then_inc(*st.sem("exp"))
                act.wait_ge(*st.at("zr", round=t))
                A(tzr[:], gates[p][:, 0:4], ACT.Tanh, scale=0.5).then_inc(*st.sem("gates"))
                act.wait_ge(*st.at("hin", round=t + 1))
                act.wait_ge(*st.at("gates", round=t))
                A(hh[:, 0:1], tzr[:, 2:3], ACT.Tanh, scale=rhh[:, 0:1], bias=hin[:, 0:1])
                A(hh[:, 1:2], tzr[:, 3:4], ACT.Tanh, scale=rhh[:, 1:2], bias=hin[:, 1:2]).then_inc(*st.sem("cand"))
            steps(act, body)

        @block.vector
        def _(dve):
            V = nc.vector
            for name in ("rhh", "ntop", "sinv", "cv", "hin", "omz", "zz", "zh", "h"):
                V.memset(zz[:], 0.0).then_inc(*st.sem(name))
                dve.wait_ge(*st.at(name))

            def body(t, p):
                n = t + 1
                dve.wait_ge(*st.at("uh", round=t))
                V.tensor_scalar(rhh[:], cand[:, 2:4], 0.5, None, ALU.mult).then_inc(*st.sem("rhh"))
                dve.wait_ge(*st.at("row", round=t))
                V.tensor_reduce(ntop[:], row.rearrange("p (b s) -> p b s", b=B), AX, ALU.max, negate=True)\
                    .then_inc(*st.sem("ntop"))
                dve.wait_ge(*st.at("sum", round=t))
                V.reciprocal(sinv[:], usum).then_inc(*st.sem("sinv"))
                dve.wait_ge(*st.at("ctx", round=t))
                dve.wait_ge(*st.at("sinv", round=n))
                V.tensor_tensor(cv[:], sinv[:], uctx, ALU.mult).then_inc(*st.sem("cv"))
                dve.wait_ge(*st.at("hc", round=t))
                V.tensor_tensor(hin[:], rhh[:], cand[:, 0:2], ALU.add).then_inc(*st.sem("hin"))
                dve.wait_ge(*st.at("gates", round=t))
                V.tensor_scalar(omz[:], tzr[:, 0:2], -0.5, 0.5, ALU.mult, ALU.add).then_inc(*st.sem("omz"))
                V.tensor_scalar(zz[:], tzr[:, 0:2], 0.5, 0.5, ALU.mult, ALU.add).then_inc(*st.sem("zz"))
                dve.wait_ge(*st.at("zz", round=n))
                V.tensor_tensor(zh[:], zz[:], h[p][:], ALU.mult).then_inc(*st.sem("zh"))
                dve.wait_ge(*st.at("zh", round=n))
                dve.wait_ge(*st.at("cand", round=t))
                dve.wait_ge(*st.at("saved", round=t))
                V.scalar_tensor_tensor(out=h[1 - p][:, 0:1], in0=hh[:, 0:1], scalar=omz[:, 0:1], in1=zh[:, 0:1],
                                       op0=ALU.mult, op1=ALU.add)
                V.scalar_tensor_tensor(out=h[1 - p][:, 1:2], in0=hh[:, 1:2], scalar=omz[:, 1:2], in1=zh[:, 1:2],
                                       op0=ALU.mult, op1=ALU.add).then_inc(*st.sem("h"))
            steps(dve, body)

        @block.gpsimd
        def _(pool):
            keep = k.cent[:, 0, 0:1]
            for i in range(2):
                nc.gpsimd.memset(keep, 0.0).then_inc(*st.sem("saved"))
                pool.wait_ge(*st.at("saved", round=i))

            def body(t, p):
                pool.wait_ge(*st.at("h", round=t + 1))
                at = k.x[:, :, bass.ds(t, 1)].rearrange("p b o -> p (b o)")
                nc.gpsimd.tensor_tensor(at, at, h[1 - p][:], ALU.add).then_inc(*st.sem("saved"))
            steps(pool, body)
            pool.wait_ge(*st.at("saved", round=T + 1))


def attention(k, label, n_iter, HP, dh, src, kv, n_kv, w_dram, shared_kv=False, bias=None, w_fixed=None):
    nc, ps = k.nc, k.ps
    NKT = -(-n_kv // P)
    kw = min(P, n_kv)
    SCALE = 1.0 / math.sqrt(dh)
    units = [(c, i) for c in range(B) for i in range(HP)]
    U = len(units)
    KD = dh if shared_kv else P
    WC = P + 2 * KD + P
    RA, RB = 2, 3
    KH = 1 if shared_kv else HP
    with ExitStack() as ctx:
        def sb(name, shape, dt=F32):
            return ctx.enter_context(nc.sbuf_tensor(f"{label}_{name}", shape, dt))

        wb = [sb(f"w{i}", [P, WC]) for i in range(2)]
        qh = sb("qh", [P, B, HP, T])
        kh, ka = sb("kh", [P, B, KH, n_kv]), sb("ka", [P, B, KH, n_kv])
        va = sb("va", [P, B, KH, NKT, 2 * dh])
        ncol = sb("ncol", [P, U, TT])
        ex = sb("ex", [P, RB, T])
        rinv = sb("rinv", [P, T])
        o = sb("o", [P, B, T])
        A_T = [(u, t) for u in range(U) for t in range(TT)]
        B_T = [(u, t) for u in range(U) for t in range(NKT)]
        an = {x: n for n, x in enumerate(A_T)}
        bn = {x: n for n, x in enumerate(B_T)}

        order = [("a", 0)]
        for u in range(U):
            if u + 1 < U:
                order.append(("a", u + 1))
            order += [("r", u), ("b", u)]
            if u % HP == HP - 1:
                order.append(("w", u // HP))
        pe_steps = ["q0", "k0", "v0", "q1", "k1", "v1"]
        act_steps, dve_steps = ["qc0", "qc1"], ["kc0", "vc0", "kc1", "vc1"]
        for what, u in order:
            if what == "a":
                pe_steps += [f"a{u}.{t}" for t in range(TT)]
                dve_steps += [f"m{u}.{t}" for t in range(TT)]
            elif what == "r":
                pe_steps += [f"r{u}"]
                dve_steps += [f"rc{u}"]
            elif what == "b":
                for t in range(NKT + 1):
                    pe_steps += ([f"b{u}.{t}"] if t < NKT else []) + ([f"v{u}.{t - 1}"] if t else [])
                act_steps += [f"e{u}.{t}" for t in range(NKT)]
                dve_steps += [f"inv{u}", f"o{u}"]
            else:
                pe_steps += [f"w{u}"]
                dve_steps += [f"res{u}"]
        st = Steps(k, label, 1, pe=" ".join(pe_steps), act=" ".join(act_steps), dve=" ".join(dve_steps),
                   pool="ka0 ka1")
        landed = [k.semaphore(f"{label}_landed{i}") for i in range(2)]
        primed = k.semaphore(f"{label}_primed")
        block = ctx.enter_context(nc.Block())

        def rounds(eng, body):
            lead = min(n_iter, 2)
            for g in range(lead):
                body(g, g % 2, g, 0)
            if n_iter > lead:
                with eng.Fori(0, (n_iter - lead) // 2) as j:
                    for u in range(2):
                        body(lead + u + 2 * j, u, 2, 1 + j)

        @block.sync
        def _(sp):
            def load(g, b, lead, n):
                if lead == 2:
                    sp.wait_ge(*st.at("w1", round=g - 2))
                sp.dma_start(wb[b][:], w_dram[bass.ds(g, 1)].rearrange("g p n -> (g p) n") if lead == 2 else w_dram[g])\
                    .then_inc(landed[b], 16)
            rounds(sp, load)
            for b in range(min(2, n_iter)):
                sp.wait_ge(landed[b], 16 * ((n_iter + 1 - b) // 2))

        @block.gpsimd
        def _(pool):
            G = nc.gpsimd
            G.memset(qh[:], 0.0).then_inc(primed, 1)
            G.memset(kh[:], 0.0).then_inc(primed, 1)
            G.memset(ka[:], 0.0).then_inc(primed, 1)
            G.memset(va[:], 1.0).then_inc(primed, 1)
            pool.wait_ge(primed, 4)
            G.memset(kh[dh:dh + 1], 1.0).then_inc(primed, 1)

            def body(g, b, lead, n):
                for c in range(B):
                    if lead:
                        pool.wait_ge(*st.at(f"a{(c + 1) * HP - 1}.{TT - 1}", round=g - 1))
                    pool.wait_ge(*st.at(f"kc{c}", round=g))
                    G.tensor_tensor(ka[0:dh, c], kh[0:dh, c], k.ones[0:dh, 0:1].unsqueeze(2).broadcast_to([dh, KH, n_kv]), ALU.mult).then_inc(*st.sem(f"ka{c}"))
            rounds(pool, body)

        @block.tensor
        def _(pe):
            M = nc.tensor.matmul

            def body(g, b, lead, n):
                W = wb[b]
                pe.wait_ge(landed[b], 16 * (n + 1))
                if lead:
                    pe.wait_ge(*st.at("res1", round=g - 1))
                for c in range(B):
                    M(ps[:, 3 * c], W[:, 0:P], src[:, c], start=True, stop=True).then_inc(*st.sem(f"q{c}"))
                    M(ps[0:KD, 3 * c + 1, 0:n_kv], W[:, P:P + KD], kv[:, c], start=True, stop=True)\
                        .then_inc(*st.sem(f"k{c}"))
                    for t in range(NKT):
                        mm = M(ps[0:kw, 3 * c + 2, t * KD:(t + 1) * KD], kv[:, c, t * P:t * P + kw],
                               W[:, P + KD:P + 2 * KD], start=True, stop=True)
                    mm.then_inc(*st.sem(f"v{c}"))
                for what, u in order:
                    c, i = units[u] if what != "w" else (u, 0)
                    ki = 0 if shared_kv else i
                    if what == "a":
                        if u == 0:
                            pe.wait_ge(*st.at("qc1", round=g))
                            pe.wait_ge(*st.at("vc1", round=g))
                        pe.wait_ge(*st.at(f"ka{c}", round=g))
                        for t in range(TT):
                            m = an[u, t]
                            if m >= RA:
                                pe.wait_ge(*st.at("m{}.{}".format(*A_T[m - RA]), round=g))
                            M(ps[:, m % RA, 0:n_kv], qh[:, c, i, t * P:(t + 1) * P], ka[:, c, ki], start=True, stop=True)\
                                .then_inc(*st.sem(f"a{u}.{t}"))
                    elif what == "r":
                        pe.wait_ge(*st.at(f"m{u}.{TT - 1}", round=g))
                        for t in range(TT):
                            mm = M(ps[dh:dh + 1, 6, t * P:(t + 1) * P], ncol[:, u, t:t + 1], k.ident[:],
                                   start=True, stop=True)
                        mm.then_inc(*st.sem(f"r{u}"))
                    elif what == "b":
                        pe.wait_ge(*st.at(f"rc{u}", round=g))
                        if u > 0:
                            pe.wait_ge(*st.at(f"o{u - 1}", round=g))
                        for t in range(NKT + 1):
                            if t < NKT:
                                m = bn[u, t]
                                if m >= RB:
                                    pe.wait_ge(*st.at("e{}.{}".format(*B_T[m - RB]), round=g))
                                M(ps[0:kw, 2 + m % RB], kh[:, c, ki, t * P:t * P + kw], qh[:, c, i], start=True, stop=True)\
                                    .then_inc(*st.sem(f"b{u}.{t}"))
                            if t:
                                pe.wait_ge(*st.at(f"e{u}.{t - 1}", round=g))
                                M(ps[0:2 * dh, 5], va[0:kw, c, ki, t - 1], ex[0:kw, bn[u, t - 1] % RB],
                                  start=(t == 1), stop=(t == NKT)).then_inc(*st.sem(f"v{u}.{t - 1}"))
                    else:
                        pe.wait_ge(*st.at(f"o{(c + 1) * HP - 1}", round=g))
                        M(ps[:, 7], W[:, P + 2 * KD:], o[:, c], start=True, stop=True).then_inc(*st.sem(f"w{c}"))
            rounds(pe, body)

        @block.scalar
        def _(act):
            act.wait_ge(primed, 5)

            def body(g, b, lead, n):
                for c in range(B):
                    act.wait_ge(*st.at(f"q{c}", round=g))
                    for i in range(HP):
                        ins = nc.scalar.copy(qh[0:dh, c, i], ps[i * dh:(i + 1) * dh, 3 * c])
                    ins.then_inc(*st.sem(f"qc{c}"))
                for u in range(U):
                    for t in range(NKT):
                        m = bn[u, t]
                        act.wait_ge(*st.at(f"b{u}.{t}", round=g))
                        if m >= RB:
                            act.wait_ge(*st.at("v{}.{}".format(*B_T[m - RB]), round=g))
                        nc.scalar.activation(ex[0:kw, m % RB], ps[0:kw, 2 + m % RB], ACT.Exp, scale=SCALE)\
                            .then_inc(*st.sem(f"e{u}.{t}"))
            rounds(act, body)

        @block.vector
        def _(dve):
            V = nc.vector
            dve.wait_ge(primed, 5)

            def body(g, b, lead, n):
                for c in range(B):
                    dve.wait_ge(*st.at(f"k{c}", round=g))
                    if lead:
                        dve.wait_ge(*st.at(f"ka{c}", round=g - 1))
                    for i in range(KH):
                        ins = V.tensor_copy(kh[0:dh, c, i], ps[i * dh:(i + 1) * dh, 3 * c + 1, 0:n_kv])
                    ins.then_inc(*st.sem(f"kc{c}"))
                    dve.wait_ge(*st.at(f"v{c}", round=g))
                    for i in range(KH):
                        ins = V.tensor_copy(va[0:kw, c, i, :, 0:dh],
                                            ps[0:kw, 3 * c + 2, 0:NKT * KD].rearrange("p (t n) -> p t n", t=NKT)
                                            [:, :, i * dh:(i + 1) * dh])
                    ins.then_inc(*st.sem(f"vc{c}"))
                for what, u in order:
                    c, i = units[u] if what != "w" else (u, 0)
                    if what == "a":
                        for t in range(TT):
                            dve.wait_ge(*st.at(f"a{u}.{t}", round=g))
                            V.tensor_reduce(ncol[:, u, t:t + 1], ps[:, an[u, t] % RA, 0:n_kv], AX, ALU.max, negate=True)\
                                .then_inc(*st.sem(f"m{u}.{t}"))
                    elif what == "r":
                        dve.wait_ge(*st.at(f"r{u}", round=g))
                        V.tensor_copy(qh[dh:dh + 1, c, i], ps[dh:dh + 1, 6]).then_inc(*st.sem(f"rc{u}"))
                    elif what == "b":
                        dve.wait_ge(*st.at(f"v{u}.{NKT - 1}", round=g))
                        V.reciprocal(rinv[0:dh], ps[dh:2 * dh, 5]).then_inc(*st.sem(f"inv{u}"))
                        dve.wait_ge(*st.at(f"inv{u}", round=g))
                        if i == 0 and lead:
                            dve.wait_ge(*st.at(f"w{c}", round=g - 1))
                        V.tensor_tensor(o[i * dh:(i + 1) * dh, c], rinv[0:dh], ps[0:dh, 5], ALU.mult)\
                            .then_inc(*st.sem(f"o{u}"))
                    else:
                        dve.wait_ge(*st.at(f"w{c}", round=g))
                        if lead:
                            dve.wait_ge(*st.at(f"res{c}", round=g - 1))
                            V.tensor_tensor(k.y[:, c], k.y[:, c], ps[:, 7], ALU.add).then_inc(*st.sem(f"res{c}"))
                        elif bias is not None:
                            V.scalar_tensor_tensor(out=k.y[:, c], in0=ps[:, 7], scalar=bias, in1=k.y[:, c],
                                                   op0=ALU.add, op1=ALU.add).then_inc(*st.sem(f"res{c}"))
                        else:
                            V.tensor_tensor(k.y[:, c], k.y[:, c], ps[:, 7], ALU.add).then_inc(*st.sem(f"res{c}"))
            rounds(dve, body)
            dve.wait_ge(*st.at("res1", round=n_iter - 1))


def copy_stage(k, label, dst, src):
    nc = k.nc
    with ExitStack() as ctx:
        copied = k.semaphore(f"{label}_copied")
        block = ctx.enter_context(nc.Block())

        @block.vector
        def _(dve):
            nc.vector.tensor_copy(dst[:], src[:]).then_inc(copied, 1)
            dve.wait_ge(copied, 1)


def add_stage(k, label, dst, src):
    nc = k.nc
    with ExitStack() as ctx:
        added = k.semaphore(f"{label}_added")
        block = ctx.enter_context(nc.Block())

        @block.vector
        def _(dve):
            nc.vector.tensor_tensor(dst[:], dst[:], src[:], ALU.add).then_inc(added, 1)
            dve.wait_ge(added, 1)


def gains_stage(k, label, w, b, n, gains):
    nc, ps = k.nc, k.ps
    with ExitStack() as ctx:
        st = Steps(k, label, 1, pe="emb", dve="bias one")
        block = ctx.enter_context(nc.Block())

        @block.tensor
        def _(pe):
            for j in range(2 * n):
                mm = nc.tensor.matmul(ps[:, 0, B * j:B * j + B], w[:, j * D:(j + 1) * D], k.cond[:], start=True, stop=True)
            mm.then_inc(*st.sem("emb"))

        @block.vector
        def _(dve):
            dve.wait_ge(*st.at("emb"))
            nc.vector.tensor_tensor(gains[:], ps[:, 0, 0:2 * n * B].rearrange("p (j b) -> p j b", b=B),
                                    b.unsqueeze(2).broadcast_to([P, 2 * n, B]), ALU.add).then_inc(*st.sem("bias"))
            dve.wait_ge(*st.at("bias"))
            nc.vector.tensor_scalar(gains[:, 0:2 * n:2], gains[:, 0:2 * n:2], 1.0, None, ALU.add).then_inc(*st.sem("one"))
            dve.wait_ge(*st.at("one"))


def adaln_stage(k, label, src, dst, gains, j):
    nc = k.nc
    with ExitStack() as ctx:
        st = Steps(k, label, 2, pe=LN_PE.format("x"), act=LN_ACT.format("x"), dve=LNA_DVE.format("x"))
        block = ctx.enter_context(nc.Block())

        @block.tensor
        def _(pe):
            ln_pe(k, pe, st, "x", lambda c: src[:, c], T, (0, 4), 2, lambda c: None)

        @block.scalar
        def _(act):
            ln_act(k, act, st, "x", T, (0, 4), 2)

        @block.vector
        def _(dve):
            ln_dve(k, dve, st, "x", lambda c: src[:, c], lambda c: dst[:, c], T, (0, 4), 2,
                   affine=lambda c: (gains[:, 2 * j, c:c + 1], gains[:, 2 * j + 1, c:c + 1]))
            for c in range(B):
                dve.wait_ge(*st.at("x.affine", c))


def glu_stage(k, label, src, w):
    nc, ps = k.nc, k.ps
    NB = DFF2 // P
    with ExitStack() as ctx:
        gl = ctx.enter_context(nc.sbuf_tensor(label + "_gelu", [P, B, T], F32))
        u = ctx.enter_context(nc.sbuf_tensor(label + "_u", [P, B, NB, T], F32))
        st = Steps(k, label, 2, pe="au0 au1 au2 au3 out", act="g0 g1 g2 g3", dve="u0 u1 u2 u3 res")
        block = ctx.enter_context(nc.Block())

        @block.tensor
        def _(pe):
            for j in range(NB):
                for c in range(B):
                    if j:
                        pe.wait_ge(*st.at(f"u{j - 1}", c))
                    nc.tensor.matmul(ps[:, 3 * c], w["ff_w1"][:, j * P:(j + 1) * P], src[:, c], start=True, stop=True)
                    nc.tensor.matmul(ps[:, 3 * c + 1], w["ff_w1"][:, DFF2 + j * P:DFF2 + (j + 1) * P], src[:, c],
                                     start=True, stop=True).then_inc(*st.sem(f"au{j}", c))
            for c in range(B):
                pe.wait_ge(*st.at(f"u{NB - 1}", c))
                for j in range(NB):
                    mm = nc.tensor.matmul(ps[:, 3 * c + 2], w["ff_w2"][:, j * D:(j + 1) * D], u[:, c, j],
                                          start=(j == 0), stop=(j == NB - 1))
                mm.then_inc(*st.sem("out", c))

        @block.scalar
        def _(act):
            for j in range(NB):
                for c in range(B):
                    act.wait_ge(*st.at(f"au{j}", c))
                    if j:
                        act.wait_ge(*st.at(f"u{j - 1}", c))
                    nc.scalar.activation(gl[:, c], ps[:, 3 * c + 1], ACT.Gelu, bias=w["ff_b1"][:, NB + j:NB + j + 1])\
                        .then_inc(*st.sem(f"g{j}", c))

        @block.vector
        def _(dve):
            for j in range(NB):
                for c in range(B):
                    dve.wait_ge(*st.at(f"g{j}", c))
                    nc.vector.scalar_tensor_tensor(out=u[:, c, j], in0=ps[:, 3 * c], scalar=w["ff_b1"][:, j:j + 1],
                                                   in1=gl[:, c], op0=ALU.add, op1=ALU.mult).then_inc(*st.sem(f"u{j}", c))
            for c in range(B):
                dve.wait_ge(*st.at("out", c))
                nc.vector.scalar_tensor_tensor(out=k.y[:, c], in0=ps[:, 3 * c + 2], scalar=w["ff_b2"], in1=k.y[:, c],
                                               op0=ALU.add, op1=ALU.add).then_inc(*st.sem("res", c))
            for c in range(B):
                dve.wait_ge(*st.at("res", c))


def transformer2_stage(k, w):
    nc = k.nc
    with ExitStack() as ctx:
        gains = ctx.enter_context(nc.sbuf_tensor("t2_gains", [P, 6, B], F32))
        hn = ctx.enter_context(nc.sbuf_tensor("t2_h", [P, B, T], F32))
        gains_stage(k, "t2g", w["norm_w"], w["norm_b"], 3, gains)
        norm_stage(k, "t2n")
        copy_stage(k, "t2c", k.y, k.xn)
        adaln_stage(k, "t2a", k.y, hn, gains, 0)
        attention(k, "t2s", H2 // 2, 2, DH2, hn, hn, T, k.dram["attn1"], bias=w["attn1_bo"])
        adaln_stage(k, "t2b", k.y, hn, gains, 1)
        attention(k, "t2x", H2 // 2, 2, DH2, hn, k.ctxT, S, k.dram["attn2"], bias=w["attn2_bo"])
        adaln_stage(k, "t2d", k.y, hn, gains, 2)
        glu_stage(k, "t2f", hn, w)
        add_stage(k, "t2r", k.x, k.y)


def ternary_stage(k, w):
    nc, ps = k.nc, k.ps
    NB = HID5 // P
    ROUND = 1.5 * 2.0 ** 23
    groups = [("fc", j, w["w_fc"][:, j * D:(j + 1) * D], D) for j in range(NB)] + [("proj", 0, w["w_proj"], HID5)]
    G = len(groups)
    with ExitStack() as ctx:
        def sb(name, shape, dt=F32):
            return ctx.enter_context(nc.sbuf_tensor("t5_" + name, shape, dt))

        absw, t1, wq = sb("absw", [P, HID5]), sb("t1", [P, G, HID5]), sb("wq", [P, G, HID5])
        asum, scale, inv = sb("asum", [P, G]), sb("scale", [P, G]), sb("inv", [P, G])
        fcT, projT = sb("fcT", [P, NB, P]), sb("projT", [P, NB, P])
        low = sb("low", [RANK5, B, 2, T])
        h, h2 = sb("h", [P, B, NB, T]), sb("h2", [P, B, NB, T])
        prep = Steps(k, "t5p", 1, pe="fcT projT", act=" ".join(f"abs{g}" for g in range(G)),
                     dve="mean mean2 scale inv " + " ".join(f"r{g} d{g} c{g} q{g} s{g}" for g in range(G)) + " scaled fcTs projTs")
        st = Steps(k, "t5", 2, pe="v b h0 h1 h2 h3 out", act="relu0 relu1 relu2 relu3",
                   dve="vs bs sq0 sq1 sq2 sq3 res")
        block = ctx.enter_context(nc.Block())

        @block.scalar
        def _(act):
            for g, (_, _, a, n) in enumerate(groups):
                if g:
                    act.wait_ge(*prep.at(f"abs{g - 1}"))
                nc.scalar.activation(absw[:, 0:n], a, ACT.Abs, accum_out=asum[:, g:g + 1]).then_inc(*prep.sem(f"abs{g}"))
            for j in range(NB):
                for c in range(B):
                    act.wait_ge(*st.at(f"h{j}", c))
                    nc.scalar.activation(h[:, c, j], ps[:, 3 * c + j % 2], ACT.Relu).then_inc(*st.sem(f"relu{j}", c))

        @block.vector
        def _(dve):
            V = nc.vector
            dve.wait_ge(*prep.at(f"abs{G - 1}"))
            V.tensor_scalar(scale[:, 0:NB], asum[:, 0:NB], 1.0 / D, None, ALU.mult).then_inc(*prep.sem("mean"))
            dve.wait_ge(*prep.at("mean"))
            V.tensor_scalar(scale[:, NB:G], asum[:, NB:G], 1.0 / HID5, None, ALU.mult).then_inc(*prep.sem("mean2"))
            dve.wait_ge(*prep.at("mean2"))
            V.tensor_scalar(scale[:], scale[:], 1e-5, None, ALU.max).then_inc(*prep.sem("scale"))
            dve.wait_ge(*prep.at("scale"))
            V.reciprocal(inv[:], scale[:]).then_inc(*prep.sem("inv"))
            dve.wait_ge(*prep.at("inv"))
            for g, (_, _, a, n) in enumerate(groups):
                V.tensor_scalar(t1[:, g, 0:n], a, inv[:, g:g + 1], ROUND, ALU.mult, ALU.add).then_inc(*prep.sem(f"r{g}"))
                dve.wait_ge(*prep.at(f"r{g}"))
                V.tensor_scalar(t1[:, g, 0:n], t1[:, g, 0:n], -ROUND, None, ALU.add).then_inc(*prep.sem(f"d{g}"))
                dve.wait_ge(*prep.at(f"d{g}"))
                V.tensor_scalar(t1[:, g, 0:n], t1[:, g, 0:n], 1.0, -1.0, ALU.min, ALU.max).then_inc(*prep.sem(f"c{g}"))
                dve.wait_ge(*prep.at(f"c{g}"))
                V.tensor_tensor(wq[:, g, 0:n], t1[:, g, 0:n], a, ALU.subtract).then_inc(*prep.sem(f"q{g}"))
                dve.wait_ge(*prep.at(f"q{g}"))
                V.tensor_tensor(wq[:, g, 0:n], wq[:, g, 0:n], a, ALU.add).then_inc(*prep.sem(f"s{g}"))
                dve.wait_ge(*prep.at(f"s{g}"))
            for g, (_, _, a, n) in enumerate(groups):
                ins = V.tensor_scalar(wq[:, g, 0:n], wq[:, g, 0:n], scale[:, g:g + 1], None, ALU.mult)
            ins.then_inc(*prep.sem("scaled"))
            dve.wait_ge(*prep.at("fcT"))
            V.tensor_copy(fcT[:].rearrange("p j n -> p (j n)"), ps[:, 6]).then_inc(*prep.sem("fcTs"))
            dve.wait_ge(*prep.at("projT"))
            V.tensor_copy(projT[:].rearrange("p j n -> p (j n)"), ps[:, 7]).then_inc(*prep.sem("projTs"))
            for c in range(B):
                dve.wait_ge(*st.at("v", c))
                V.tensor_copy(low[:, c, 0], ps[0:RANK5, 3 * c + 2]).then_inc(*st.sem("vs", c))
            for c in range(B):
                dve.wait_ge(*st.at("b", c))
                V.tensor_scalar(low[:, c, 1], ps[0:RANK5, 3 * c + 2], w["gate"][0:RANK5], None, ALU.mult)\
                    .then_inc(*st.sem("bs", c))
            for j in range(NB):
                for c in range(B):
                    dve.wait_ge(*st.at(f"relu{j}", c))
                    V.tensor_tensor(h2[:, c, j], h[:, c, j], h[:, c, j], ALU.mult).then_inc(*st.sem(f"sq{j}", c))
            for c in range(B):
                dve.wait_ge(*st.at("out", c))
                V.tensor_tensor(k.x[:, c], k.x[:, c], ps[:, 3 * c + 2], ALU.add).then_inc(*st.sem("res", c))
            for c in range(B):
                dve.wait_ge(*st.at("res", c))

        @block.tensor
        def _(pe):
            M = nc.tensor.matmul
            for c in range(B):
                M(ps[0:RANK5, 3 * c + 2], w["vT"], k.xn[:, c], start=True, stop=True).then_inc(*st.sem("v", c))
            pe.wait_ge(*prep.at("scaled"))
            for j in range(NB):
                mm = nc.tensor.transpose(ps[:, 6, j * P:(j + 1) * P], wq[:, j, 0:D], k.ident[:])
            mm.then_inc(*prep.sem("fcT"))
            for j in range(NB):
                mm = nc.tensor.transpose(ps[:, 7, j * P:(j + 1) * P], wq[:, NB, j * P:(j + 1) * P], k.ident[:])
            mm.then_inc(*prep.sem("projT"))
            for c in range(B):
                pe.wait_ge(*st.at("vs", c))
                M(ps[0:RANK5, 3 * c + 2], w["fastT"], low[:, c, 0], start=True, stop=True).then_inc(*st.sem("b", c))
            pe.wait_ge(*prep.at("projTs"))
            for j in range(NB):
                for c in range(B):
                    if j == 0:
                        pe.wait_ge(*st.at("bs", c))
                    if j >= 2:
                        pe.wait_ge(*st.at(f"relu{j - 2}", c))
                    M(ps[:, 3 * c + j % 2], fcT[:, j], k.xn[:, c], start=True, stop=False)
                    M(ps[:, 3 * c + j % 2], w["uT"][:, j * P:(j + 1) * P], low[:, c, 1], start=False, stop=True)\
                        .then_inc(*st.sem(f"h{j}", c))
            for c in range(B):
                for j in range(NB):
                    pe.wait_ge(*st.at(f"sq{j}", c))
                    mm = M(ps[:, 3 * c + 2], projT[:, j], h2[:, c, j], start=(j == 0), stop=(j == NB - 1))
                mm.then_inc(*st.sem("out", c))


PAIRS = [(i, j) for j in range(3) for i in range(3)]
MASK_ROW = DH3 * len(PAIRS)
SHIFT_ROW = 96
MASKED = -1e30
STACK_LOADS = 3 + 9


def transformer3_stage(k, w):
    nc, ps = k.nc, k.ps
    SCALE = 1.0 / math.sqrt(DH3)
    G = H3 // 4
    NB = DFF3 // P
    assert NB == G
    with ExitStack() as ctx:
        def sb(name, shape, dt=F32):
            return ctx.enter_context(nc.sbuf_tensor("t6_" + name, shape, dt))

        gains = sb("gains", [P, 6 * NL3, B])
        with ExitStack() as nctx:
            whole, norms = k.weights(nctx, "p6n")
            load_stage(k, whole, "p6n")
            gains_stage(k, "t6g", norms["norm_w"], norms["norm_b"], 3 * NL3, gains)
        hn = k.xn
        turn = nc.dram_tensor("t6_turn", (B, 2, 3, P, T), BF16).ap()
        wa, wx, wf = sb("wa", [P, 9 * P]), sb("wx", [P, 9 * P]), sb("wf", [P, 2 * DFF3 + NB + 1])
        qst, kst = sb("qst", [P, B, H3, T], BF16), sb("kst", [P, B, H3, T], BF16)
        kxt = sb("kxt", [P, B, H3, S], BF16)
        va, vx = sb("va", [P, B, TT, H3, 32]), sb("vx", [P, B, 1, H3, 32])
        t1, t2, rot = sb("t1", [P, 2, T]), sb("t2", [P, 2, T]), sb("rot", [P, 2, T])
        part = sb("part", [P, B, 2, 3, T], BF16)
        ncol = sb("ncol", [P, B, TT, H3])
        nhi, nlo = sb("nhi", [P, B, TT, H3], BF16), sb("nlo", [P, B, TT, H3], BF16)
        nrow = sb("nrow", [H3, B, 2, T], BF16)
        identb = sb("identb", [P, P], BF16)
        ex = sb("ex", [P, 4, 2, T])
        og, rs, on = sb("og", [P, T]), sb("rs", [P, T]), sb("on", [P, B, G, T])
        one16 = sb("one16", [H3, T], BF16)
        mraw, mx = sb("mraw", [H3, B, T + S], U8), sb("mx", [H3, B, T + S], BF16)
        hid = on

        with ExitStack() as pctx:
            dn = k.semaphore("t6_fill")
            ones_in = k.semaphore("t6_ones_in")
            raw_in = k.semaphore("t6_mask_in")
            dv = k.semaphore("t6_dve_fill")
            rows_in = k.semaphore("t6_rows_in")
            block = pctx.enter_context(nc.Block())

            @block.gpsimd
            def _(pool):
                for a in (qst, kst, kxt, va, vx):
                    nc.gpsimd.memset(a[:], 0.0).then_inc(dn, 1)
                nc.gpsimd.memset(one16[:], 1.0).then_inc(dn, 1)
                for n, part_of_ones in enumerate((kst[SHIFT_ROW:SHIFT_ROW + 2], kxt[SHIFT_ROW:SHIFT_ROW + 2],
                                                  va[:, :, :, :, DH3:DH3 + 1], vx[:, :, :, :, DH3:DH3 + 1])):
                    pool.wait_ge(dn, 6 + n)
                    nc.gpsimd.memset(part_of_ones, 1.0).then_inc(dn, 1)
                pool.wait_ge(dn, 10)

            @block.vector
            def _(dve):
                nc.vector.tensor_copy(identb[:], k.ident[:]).then_inc(dv, 1)
                dve.wait_ge(raw_in, 16)
                nc.vector.tensor_scalar(mx[:], mraw[:], MASKED, None, ALU.mult).then_inc(dv, 1)
                dve.wait_ge(dv, 2)

            @block.sync
            def _(sp):
                sp.dma_start(mraw[:], k.dram["masks"]).then_inc(raw_in, 16)
                sp.wait_ge(dn, 10)
                sp.wait_ge(dv, 2)
                for c in range(B):
                    sp.dma_start(qst[MASK_ROW:MASK_ROW + 1, c], one16[:]).then_inc(rows_in, 16)
                    sp.dma_start(kst[MASK_ROW:MASK_ROW + 1, c], mx[:, c, 0:T]).then_inc(rows_in, 16)
                    sp.dma_start(kxt[MASK_ROW:MASK_ROW + 1, c], mx[:, c, T:T + S]).then_inc(rows_in, 16)
                sp.wait_ge(rows_in, 16 * 6)

        PARTS = {"s": (wa, None, kst, va, T), "x": (wx, k.ctxT, kxt, vx, S)}
        BB = 4
        AB, VB, MB = 4, 6, 7

        def blocks(pf):
            return [(g, t) for g in range(G) for t in range(-(-PARTS[pf][4] // P))]

        def order(pf):
            a0 = [("a", 0, h) for h in range(H3)]
            a1 = [("a", 1, h) for h in range(H3)]
            nb = len(blocks(pf))
            run = a0 + [("t", 0, 0)]
            per = H3 // nb
            for n in range(nb):
                run += a1[n * per:(n + 1) * per] + [("b", 0, n)]
            run += [("w", 0, 0), ("t", 1, 0)]
            run += [("b", 1, n) for n in range(nb)] + [("w", 1, 0)]
            return run

        tiles_a = {"s": TT, "x": 1}
        pe_s, act_s, dve_s, pool_s = [], [], [], []
        for pf in "sx":
            nkt = -(-PARTS[pf][4] // P)
            for c in range(B):
                pe_s += [f"{pf}q{c}", f"{pf}k{c}", f"{pf}v{c}"]
                dve_s += [f"{pf}{n}{c}" for n in ("qa", "qb", "qr", "q1", "qd", "q2", "q3", "ka", "kb", "vc")]
                pool_s += [f"{pf}{n}{c}" for n in ("kr", "k1", "kd", "k2", "k3")]
            for what, c, n in order(pf):
                if what == "a":
                    pe_s += [f"{pf}a{c}.{n}.{t}" for t in range(tiles_a[pf])]
                    dve_s += [f"{pf}m{c}.{n}.{t}" for t in range(tiles_a[pf])]
                elif what == "t":
                    pe_s += [f"{pf}thi{c}", f"{pf}tlo{c}"]
                    dve_s += [f"{pf}hi{c}", f"{pf}lo{c}", f"{pf}rhi{c}", f"{pf}rlo{c}"]
                elif what == "b":
                    pe_s += [f"{pf}b{c}.{n}.0", f"{pf}b{c}.{n}.1", f"{pf}v{c}.{n}"]
                    act_s += [f"{pf}e{c}.{n}.0", f"{pf}e{c}.{n}.1"]
                    if blocks(pf)[n][1] == nkt - 1:
                        pe_s += [f"{pf}sum{c}.{blocks(pf)[n][0]}"]
                        act_s += [f"{pf}ln{c}.{blocks(pf)[n][0]}", f"{pf}inv{c}.{blocks(pf)[n][0]}"]
                        dve_s += [f"{pf}og{c}.{blocks(pf)[n][0]}", f"{pf}on{c}.{blocks(pf)[n][0]}"]
                else:
                    pe_s += [f"{pf}w{c}"]
                    dve_s += [f"{pf}res{c}"]
        for j in range(NB):
            for c in range(B):
                pe_s += [f"f{c}.{j}"]
                act_s += [f"g{c}.{j}"]
        for c in range(B):
            pe_s += [f"fo{c}"]
            dve_s += [f"fres{c}"]
        st = Steps(k, "t6", 1, lead=1, pe=" ".join(pe_s), act=" ".join(act_s), dve=" ".join(dve_s),
                   pool=" ".join(pool_s))
        ln = Steps(k, "t6n", 2, lead=1, pe=" ".join(LN_PE.format(n) for n in "sxf"),
                   act=" ".join(LN_ACT.format(n) for n in "sxf"), dve=" ".join(LNA_DVE.format(n) for n in "sxf"))
        landed = {n: k.semaphore(f"t6_{n}_landed") for n in ("wa", "wx", "wf")}
        stacked = {(pf, c): k.semaphore(f"t6_{pf}_stacked{c}") for pf in "sx" for c in range(B)}
        shifted = {(pf, c): k.semaphore(f"t6_{pf}_shifted{c}") for pf in "sx" for c in range(B)}
        turn_in = {(c, q): k.semaphore(f"t6_turn_in{c}{q}") for c in range(B) for q in range(2)}
        block = ctx.enter_context(nc.Block())

        @block.sync
        def _(sp):
            with sp.Fori(0, NL3) as l:
                turned = {key: 0 for key in turn_in}
                def weights(name, dst, last):
                    sp.wait_ge(*last)
                    src = k.dram["t6_" + name][bass.ds(l, 1)].rearrange("g p n -> (g p) n")
                    sp.dma_start(dst[:], src).then_inc(landed[name], 16)

                weights("wa", wa, st.at("sw1", round=l - 1))
                weights("wx", wx, st.at("xw1", round=l - 1))
                weights("wf", wf, st.at("fres1", round=l - 1))
                for pf in "sx":
                    kt, n_kv = PARTS[pf][2], PARTS[pf][4]
                    for c in range(B):
                        for q, step in enumerate(("q3", "k3")):
                            n = (T, n_kv)[q]
                            sp.wait_ge(*st.at(f"{pf}{step}{c}", round=l))
                            turned[c, q] += 1
                            sp.dma_start(turn[c, q, :, :, 0:n].rearrange("i p n -> p i n"), part[:, c, q, :, 0:n])\
                                .then_inc(turn_in[c, q], 16)
                            sp.wait_ge(turn_in[c, q], l * 32 + 16 * turned[c, q])
                            for j in range(3):
                                if q == 0:
                                    sp.dma_start(qst[24 * j:24 * j + 24, c],
                                                 turn[c, q].rearrange("i (d h) n -> (i d) h n", d=DH3)).then_inc(stacked[pf, c], 16)
                                    continue
                                for i in range(3):
                                    p = 3 * j + i
                                    sp.dma_start(kt[p * DH3:(p + 1) * DH3, c],
                                                 turn[c, q, j, :, 0:n].rearrange("(d h) n -> d h n", d=DH3))\
                                        .then_inc(stacked[pf, c], 16)
                    for c in range(B):
                        sp.wait_ge(*st.at(f"{pf}rlo{c}", round=l))
                        for i in range(2):
                            sp.dma_start(qst[SHIFT_ROW + i:SHIFT_ROW + i + 1, c], nrow[:, c, i]).then_inc(shifted[pf, c], 16)
            for n in ("wa", "wx", "wf"):
                sp.wait_ge(landed[n], 16 * NL3)
            for key in turn_in:
                sp.wait_ge(turn_in[key], 16 * 2 * NL3)
            for key in stacked:
                sp.wait_ge(stacked[key], 16 * STACK_LOADS * NL3)
                sp.wait_ge(shifted[key], 16 * 2 * NL3)

        @block.tensor
        def _(pe):
            M = nc.tensor.matmul
            st.prime(pe, "pe")
            ln.prime(pe, "pe")
            with pe.Fori(0, NL3) as l:
                for pf in "sx":
                    W, kv, kt, vt, n_kv = PARTS[pf]
                    nkt, kw = -(-n_kv // P), min(P, n_kv)
                    last = "fres" if pf == "s" else "sres"
                    ln_pe(k, pe, ln, pf, lambda c: k.y[:, c], T, (AB, AB + 1), 2,
                          lambda c: pe.wait_ge(*st.at(f"{last}{c}", round=l - 1 if pf == "s" else l)), l)
                    pe.wait_ge(landed["w" + ("a" if pf == "s" else "x")], 16 * (l + 1))
                    for c in range(B):
                        pe.wait_ge(*ln.at(pf + ".affine", c, l))
                        if c:
                            pe.wait_ge(*st.at(f"{pf}vc0", round=l))
                        M(ps[:, 0], W[:, 0:P], hn[:, c], start=True, stop=True)
                        M(ps[:, 1], W[:, P:2 * P], hn[:, c], start=True, stop=True).then_inc(*st.sem(f"{pf}q{c}"))
                        src = hn[:, c] if kv is None else kv[:, c]
                        M(ps[:, 2, 0:n_kv], W[:, 2 * P:3 * P], src, start=True, stop=True)
                        M(ps[:, 3, 0:n_kv], W[:, 3 * P:4 * P], src, start=True, stop=True).then_inc(*st.sem(f"{pf}k{c}"))
                        for t in range(nkt):
                            mm = M(ps[0:kw, VB, t * P:(t + 1) * P], src[:, t * P:t * P + kw], W[:, 4 * P:5 * P],
                                   start=True, stop=True)
                        mm.then_inc(*st.sem(f"{pf}v{c}"))
                    na, nb, prev_a, prev_b = 0, 0, [], []
                    for what, c, n in order(pf):
                        if what == "a":
                            if n == 0:
                                pe.wait_ge(stacked[pf, c], 16 * STACK_LOADS * (l + 1))
                            for t in range(tiles_a[pf]):
                                if na >= 2:
                                    pe.wait_ge(*st.at(prev_a[na - 2], round=l))
                                for q in ([t] if pf == "s" else range(TT)):
                                    o = 0 if pf == "s" else q * n_kv
                                    mm = M(ps[:, AB + na % 2, o:o + n_kv], qst[0:MASK_ROW + 1, c, n, q * P:(q + 1) * P],
                                           kt[0:MASK_ROW + 1, c, n], start=True, stop=True)
                                mm.then_inc(*st.sem(f"{pf}a{c}.{n}.{t}"))
                                prev_a.append(f"{pf}m{c}.{n}.{t}")
                                na += 1
                        elif what == "t":
                            for i, (cols, name, was) in enumerate(((nhi, "thi", "lo"), (nlo, "tlo", "rhi"))):
                                pe.wait_ge(*st.at(f"{pf}{was}{c}", round=l))
                                if i == 0 and c == 1:
                                    pe.wait_ge(*st.at(f"{pf}res0", round=l))
                                for t in range(TT):
                                    mm = M(ps[0:H3, MB, t * P:(t + 1) * P], cols[:, c, t], identb[:], start=True, stop=True)
                                mm.then_inc(*st.sem(f"{pf}{name}{c}"))
                        elif what == "b":
                            g, t = blocks(pf)[n]
                            if n == 0:
                                pe.wait_ge(shifted[pf, c], 16 * 2 * (l + 1))
                                if c == 0:
                                    pe.wait_ge(*st.at(f"{pf}vc1", round=l))
                            for i in range(2):
                                if nb >= 2:
                                    pe.wait_ge(*st.at(prev_b[nb - 2], round=l))
                                for j in range(2):
                                    h = 4 * g + 2 * i + j
                                    mm = M(ps[0:kw, 2 * i + j], kt[0:SHIFT_ROW + 2, c, h, t * P:t * P + kw],
                                           qst[0:SHIFT_ROW + 2, c, h], start=True, stop=True)
                                mm.then_inc(*st.sem(f"{pf}b{c}.{n}.{i}"))
                                prev_b.append(f"{pf}e{c}.{n}.{i}")
                                nb += 1
                            if t == 0 and (g or c):
                                pe.wait_ge(*st.at(f"{pf}og{c}.{g - 1}" if g else f"{pf}og0.{G - 1}", round=l))
                            pe.wait_ge(*st.at(f"{pf}e{c}.{n}.1", round=l))
                            for j in range(4):
                                mm = M(ps[32 * j:32 * j + 32, VB], vt[0:kw, c, t, 4 * g + j], ex[0:kw, 2 * (n % 2) + j // 2, j % 2],
                                       start=(t == 0), stop=(t == nkt - 1))
                            mm.then_inc(*st.sem(f"{pf}v{c}.{n}"))
                            if t == nkt - 1:
                                pe.wait_ge(*st.at(f"{pf}og{c}.{g}", round=l))
                                if g:
                                    pe.wait_ge(*st.at(f"{pf}ln{c}.{g - 1}", round=l))
                                elif c == 0:
                                    pe.wait_ge(*st.at(f"{pf}rlo0", round=l))
                                else:
                                    pe.wait_ge(*st.at(f"{pf}rlo1", round=l))
                                M(ps[:, MB], w["spread"], og[:], start=True, stop=True).then_inc(*st.sem(f"{pf}sum{c}.{g}"))
                        else:
                            pe.wait_ge(*st.at(f"{pf}on{c}.{G - 1}", round=l))
                            for g in range(G):
                                mm = M(ps[:, MB], W[:, (5 + g) * P:(6 + g) * P], on[:, c, g], start=(g == 0), stop=(g == G - 1))
                            mm.then_inc(*st.sem(f"{pf}w{c}"))
                ln_pe(k, pe, ln, "f", lambda c: k.y[:, c], T, (AB, AB + 1), 2,
                      lambda c: pe.wait_ge(*st.at(f"xres{c}", round=l)), l)
                pe.wait_ge(landed["wf"], 16 * (l + 1))
                for j in range(NB):
                    for c in range(B):
                        if j == 0:
                            pe.wait_ge(*ln.at("f.affine", c, l))
                        if j >= 2:
                            pe.wait_ge(*st.at(f"g{c}.{j - 2}", round=l))
                        M(ps[:, 2 * c + j % 2], wf[:, j * P:(j + 1) * P], hn[:, c], start=True, stop=True)\
                            .then_inc(*st.sem(f"f{c}.{j}"))
                for c in range(B):
                    for j in range(NB):
                        pe.wait_ge(*st.at(f"g{c}.{j}", round=l))
                        mm = M(ps[:, VB + c], wf[:, DFF3 + j * D:DFF3 + (j + 1) * D], hid[:, c, j], start=(j == 0), stop=(j == NB - 1))
                    mm.then_inc(*st.sem(f"fo{c}"))

        @block.scalar
        def _(act):
            A = nc.scalar.activation
            st.prime(act, "act")
            ln.prime(act, "act")
            with act.Fori(0, NL3) as l:
                for pf in "sx":
                    n_kv = PARTS[pf][4]
                    nkt, kw = -(-n_kv // P), min(P, n_kv)
                    ln_act(k, act, ln, pf, T, (AB, AB + 1), 2, l)
                    late = []
                    for what, c, n in order(pf):
                        if what != "b":
                            continue
                        g, t = blocks(pf)[n]
                        for i in range(2):
                            act.wait_ge(*st.at(f"{pf}b{c}.{n}.{i}", round=l))
                            if n >= 2:
                                act.wait_ge(*st.at(f"{pf}v{c}.{n - 2}", round=l))
                            elif c:
                                act.wait_ge(*st.at(f"{pf}v0.{len(blocks(pf)) - 2 + n}", round=l))
                            A(ex[0:kw, 2 * (n % 2) + i], ps[0:kw, 2 * i:2 * i + 2], ACT.Exp, scale=SCALE)\
                                .then_inc(*st.sem(f"{pf}e{c}.{n}.{i}"))
                        if t == nkt - 1:
                            act.wait_ge(*st.at(f"{pf}sum{c}.{g}", round=l))
                            if g or c:
                                act.wait_ge(*st.at(f"{pf}on{c}.{g - 1}" if g else f"{pf}on0.{G - 1}", round=l))
                            A(rs[:], ps[:, MB], ACT.Ln).then_inc(*st.sem(f"{pf}ln{c}.{g}"))
                            act.wait_ge(*st.at(f"{pf}ln{c}.{g}", round=l))
                            A(rs[:], rs[:], ACT.Exp, scale=-1.0).then_inc(*st.sem(f"{pf}inv{c}.{g}"))
                ln_act(k, act, ln, "f", T, (AB, AB + 1), 2, l)
                for j in range(NB):
                    for c in range(B):
                        act.wait_ge(*st.at(f"f{c}.{j}", round=l))
                        A(hid[:, c, j], ps[:, 2 * c + j % 2], ACT.Gelu, bias=wf[:, 2 * DFF3 + j:2 * DFF3 + j + 1])\
                            .then_inc(*st.sem(f"g{c}.{j}"))

        @block.gpsimd
        def _(pool):
            st.prime(pool, "pool")
            with pool.Fori(0, NL3) as l:
                for pf in "sx":
                    n = PARTS[pf][4]
                    for c in range(B):
                        def step(name, out, a, b, op):
                            nc.gpsimd.tensor_tensor(out, a, b, op).then_inc(*st.sem(f"{pf}{name}{c}"))
                            pool.wait_ge(*st.at(f"{pf}{name}{c}", round=l))

                        kr, x1, x2 = rot[:, 1, 0:n], t1[:, 1, 0:n], t2[:, 1, 0:n]
                        k1, k2, k3 = (part[:, c, 1, i, 0:n] for i in range(3))
                        pool.wait_ge(*st.at(f"{pf}kb{c}", round=l))
                        step("kr", kr, x1, x2, ALU.add)
                        step("k1", k1, x1, x2, ALU.add)
                        step("kd", x1, kr, k1, ALU.subtract)
                        step("k2", k2, kr, k1, ALU.subtract)
                        step("k3", k3, x1, k2, ALU.subtract)

        @block.vector
        def _(dve):
            V = nc.vector
            st.prime(dve, "dve")
            ln.prime(dve, "dve")
            with dve.Fori(0, NL3) as l:
                def gain(j):
                    def of(c):
                        at = l * 6 + 2 * j
                        return (gains[:, bass.ds(at, 1), c], gains[:, bass.ds(at + 1, 1), c])
                    return of

                for pf in "sx":
                    W, kv, kt, vt, n_kv = PARTS[pf]
                    nkt, kw = -(-n_kv // P), min(P, n_kv)
                    ln_dve(k, dve, ln, pf, lambda c: k.y[:, c], lambda c: hn[:, c], T, (AB, AB + 1), 2, l,
                           affine=gain("sxf".index(pf)))
                    for c in range(B):
                        def step(name, out, a, b, op):
                            V.tensor_tensor(out, a, b, op).then_inc(*st.sem(f"{pf}{name}{c}"))
                            dve.wait_ge(*st.at(f"{pf}{name}{c}", round=l))

                        q1, q2, q3 = (part[:, c, 0, i] for i in range(3))
                        dve.wait_ge(*st.at(f"{pf}q{c}", round=l))
                        step("qa", t1[:, 0], w["cos"], ps[:, 0], ALU.mult)
                        step("qb", t2[:, 0], w["sin"], ps[:, 1], ALU.mult)
                        step("qr", rot[:, 0], t1[:, 0], t2[:, 0], ALU.add)
                        step("q1", q1, t1[:, 0], t2[:, 0], ALU.add)
                        step("qd", t1[:, 0], rot[:, 0], q1, ALU.subtract)
                        step("q2", q2, rot[:, 0], q1, ALU.subtract)
                        step("q3", q3, t1[:, 0], q2, ALU.subtract)
                        dve.wait_ge(*st.at(f"{pf}k{c}", round=l))
                        if c:
                            dve.wait_ge(*st.at(f"{pf}k30", round=l))
                        step("ka", t1[:, 1, 0:n_kv], w["cos"][:, 0:n_kv], ps[:, 2, 0:n_kv], ALU.mult)
                        step("kb", t2[:, 1, 0:n_kv], w["sin"][:, 0:n_kv], ps[:, 3, 0:n_kv], ALU.mult)
                        dve.wait_ge(*st.at(f"{pf}v{c}", round=l))
                        V.tensor_copy(vt[0:kw, c, :, :, 0:DH3], ps[0:kw, VB, 0:nkt * P].rearrange("p (t h d) -> p t h d", t=nkt, d=DH3))\
                            .then_inc(*st.sem(f"{pf}vc{c}"))
                    na = 0
                    for what, c, n in order(pf):
                        if what == "a":
                            for t in range(tiles_a[pf]):
                                dve.wait_ge(*st.at(f"{pf}a{c}.{n}.{t}", round=l))
                                if pf == "s":
                                    V.tensor_reduce(ncol[:, c, t, n:n + 1], ps[:, AB + na % 2], AX, ALU.max, negate=True)\
                                        .then_inc(*st.sem(f"{pf}m{c}.{n}.{t}"))
                                else:
                                    V.tensor_reduce(ncol[:, c, :, n], ps[:, AB + na % 2, 0:TT * n_kv].rearrange("p (t n) -> p t n", t=TT),
                                                    AX, ALU.max, negate=True).then_inc(*st.sem(f"{pf}m{c}.{n}.{t}"))
                                na += 1
                        elif what == "t":
                            dve.wait_ge(*st.at(f"{pf}m{c}.{H3 - 1}.{tiles_a[pf] - 1}", round=l))
                            V.tensor_copy(nhi[:, c], ncol[:, c]).then_inc(*st.sem(f"{pf}hi{c}"))
                            dve.wait_ge(*st.at(f"{pf}hi{c}", round=l))
                            V.tensor_tensor(nlo[:, c], ncol[:, c], nhi[:, c], ALU.subtract).then_inc(*st.sem(f"{pf}lo{c}"))
                            dve.wait_ge(*st.at(f"{pf}thi{c}", round=l))
                            V.tensor_copy(nrow[:, c, 0], ps[0:H3, MB]).then_inc(*st.sem(f"{pf}rhi{c}"))
                            dve.wait_ge(*st.at(f"{pf}tlo{c}", round=l))
                            V.tensor_copy(nrow[:, c, 1], ps[0:H3, MB]).then_inc(*st.sem(f"{pf}rlo{c}"))
                        elif what == "b":
                            g, t = blocks(pf)[n]
                            if t == nkt - 1:
                                dve.wait_ge(*st.at(f"{pf}v{c}.{n}", round=l))
                                if g or c:
                                    dve.wait_ge(*st.at(f"{pf}on{c}.{g - 1}" if g else f"{pf}on0.{G - 1}", round=l))
                                V.tensor_copy(og[:], ps[:, VB]).then_inc(*st.sem(f"{pf}og{c}.{g}"))
                                dve.wait_ge(*st.at(f"{pf}og{c}.{g}", round=l))
                                dve.wait_ge(*st.at(f"{pf}inv{c}.{g}", round=l))
                                V.tensor_tensor(on[:, c, g], og[:], rs[:], ALU.mult).then_inc(*st.sem(f"{pf}on{c}.{g}"))
                        else:
                            dve.wait_ge(*st.at(f"{pf}w{c}", round=l))
                            V.tensor_tensor(k.y[:, c], k.y[:, c], ps[:, MB], ALU.add).then_inc(*st.sem(f"{pf}res{c}"))
                ln_dve(k, dve, ln, "f", lambda c: k.y[:, c], lambda c: hn[:, c], T, (AB, AB + 1), 2, l, affine=gain(2))
                for c in range(B):
                    dve.wait_ge(*st.at(f"fo{c}", round=l))
                    V.scalar_tensor_tensor(out=k.y[:, c], in0=ps[:, VB + c], scalar=wf[:, 2 * DFF3 + NB:2 * DFF3 + NB + 1],
                                           in1=k.y[:, c], op0=ALU.add, op1=ALU.add).then_inc(*st.sem(f"fres{c}"))
            dve.wait_ge(*st.at("fres1", round=NL3 - 1))


def layer3_stage(k, w):
    norm_stage(k, "t6p")
    copy_stage(k, "t6c", k.y, k.xn)
    transformer3_stage(k, w)
    add_stage(k, "t6r", k.x, k.y)


def rms_stage(k, label, src, dst, gain, eps):
    nc, ps = k.nc, k.ps
    with ExitStack() as ctx:
        e = ctx.enter_context(nc.sbuf_tensor(label + "_eps", [P, 1], F32))
        st = Steps(k, label, 2, pe="ms", act="sq ln rstd", dve="out", pool="eps")
        block = ctx.enter_context(nc.Block())

        @block.gpsimd
        def _(pool):
            nc.gpsimd.memset(e[:], eps).then_inc(*st.sem("eps"))

        @block.tensor
        def _(pe):
            for c in range(B):
                pe.wait_ge(*st.at("sq", c))
                nc.tensor.matmul(ps[:, 4 * c], k.mean_w[:], k.sq[:, c], start=True, stop=True).then_inc(*st.sem("ms", c))

        @block.scalar
        def _(act):
            for c in range(B):
                nc.scalar.activation(k.sq[:, c], src[:, c], ACT.Square).then_inc(*st.sem("sq", c))
            nc.scalar.preload_act_table_set("natural_log_exp_and_others")
            act.wait_ge(*st.at("eps"))
            for c in range(B):
                act.wait_ge(*st.at("ms", c))
                nc.scalar.activation(k.rstd[:, c], ps[:, 4 * c], ACT.Ln, bias=e[:, 0:1]).then_inc(*st.sem("ln", c))
                act.wait_ge(*st.at("ln", c))
                nc.scalar.activation(k.rstd[:, c], k.rstd[:, c], ACT.Exp, scale=-0.5).then_inc(*st.sem("rstd", c))

        @block.vector
        def _(dve):
            for c in range(B):
                dve.wait_ge(*st.at("rstd", c))
                nc.vector.scalar_tensor_tensor(out=dst[:, c], in0=src[:, c], scalar=gain, in1=k.rstd[:, c],
                                               op0=ALU.mult, op1=ALU.mult).then_inc(*st.sem("out", c))
            for c in range(B):
                dve.wait_ge(*st.at("out", c))


def final_stage(k, w):
    nc = k.nc
    with ExitStack() as ctx:
        hn = ctx.enter_context(nc.sbuf_tensor("t7_h", [P, B, T], F32))
        norm_stage(k, "t7n")
        copy_stage(k, "t7c", k.y, k.xn)
        rms_stage(k, "t7a", k.y, hn, w["g1"], 1e-6)
        attention(k, "t7s", 1, H4, DK4, hn, hn, T, k.dram["attn4"], shared_kv=True)
        rms_stage(k, "t7b", k.y, k.xn, w["g2"], 1e-6)
        add_stage(k, "t7r", k.x, k.y)
    moe_stage(k, "m7", "renorm", E4, F4, 1, k.dram["experts4"], w)


def layer1_stage(k, w):
    norm_stage(k, "n1")
    moe_stage(k, "m1", "scores", E0, I0, SI0 // I0, k.dram["experts0"], w)


def layer2_stage(k, w):
    norm_stage(k, "n2")
    gru_stage(k, w)


def layer3_moe_stage(k, w):
    norm_stage(k, "n3")
    moe_stage(k, "m3", "sigmoid", E1, I1, SI1 // I1, k.dram["experts1"], w)


def layer5_stage(k, w):
    norm_stage(k, "n5")
    ternary_stage(k, w)


def build(nc, dram, layout, out):
    with ExitStack() as ctx:
        k = Core(nc, ctx, dram, layout)
        setup_stage(k)
        k.release()
        stages = (slots_stage, layer1_stage, layer2_stage, layer3_moe_stage, transformer2_stage, layer5_stage,
                  layer3_stage, final_stage)
        for n, stage in enumerate(stages):
            with ExitStack() as wctx:
                whole, parts = k.weights(wctx, f"p{n}")
                load_stage(k, whole, f"p{n}")
                stage(k, parts)
            k.release()
        store_stage(k, out)
        k.release()


def col(a):
    return a.reshape(-1, 1)


def tiles(a):
    n = a.shape[0] // P
    return a.reshape(n, P, a.shape[1]).transpose(1, 0, 2).reshape(P, n * a.shape[1])


def laid_out(i):
    packs = {}
    packs["p0"] = [(n, i["L0_xcond_" + n]) for n in ("wk", "wv", "wq", "wu", "w1", "w2")] + \
        [(n, col(i["L0_xcond_" + n])) for n in ("q_mu", "q_logsig", "lnkv_g", "lnkv_b", "lnq_g", "lnq_b", "lnm_g",
                                                "lnm_b", "lnp_g", "lnp_b", "bk", "bq", "bu", "b1", "b2")] + \
        [("bv", i["L0_xcond_bv"].reshape(1, D))]
    def rows(a, n):
        return np.broadcast_to(a.reshape(1, n), (P, n))

    def rank(n):
        return rows(np.arange(n, 0, -1, dtype=np.float32), n)

    packs["p1"] = [("router", np.concatenate([i["L0_ffn_gate_w"], i["L0_ffn_shared_expert_gate_w"]]).T), ("rank", rank(E0))]
    packs["p3"] = [("router", i["L1_ffn_router_w"]), ("rank", rank(E1)), ("bias", rows(i["L1_ffn_expert_bias"], E1))]
    packs["p7"] = [("g1", col(i["L3_ffn_g1"])), ("g2", col(i["L3_ffn_g2"])), ("router", i["L3_ffn_Wr"].T), ("rank", rank(E4)), ("bias", rows(i["L3_ffn_expert_bias"], E4))]
    wi = i["L1_xcond_Wi"]
    packs["p2"] = [("att_h", i["L1_xcond_W_att"][0:D]), ("att_e", i["L1_xcond_W_att"][D:]), ("v", i["L1_xcond_V_att"]),
                   ("wix", wi[0:D]), ("wic", wi[D:]), ("uh", i["L1_xcond_Uh"]), ("bi", i["L1_xcond_b"].reshape(3, D).T)]
    L2 = {n[len("L2_xcond_"):]: a for n, a in i.items() if n.startswith("L2_xcond_")}
    packs["p4"] = [("norm_w", np.concatenate([L2[f"norm{j}_w"] for j in (1, 2, 3)], axis=1)),
                   ("norm_b", np.concatenate([L2[f"norm{j}_b"].reshape(2, D).T for j in (1, 2, 3)], axis=1)),
                   ("attn1_bo", col(L2["attn1_bo"])), ("attn2_bo", col(L2["attn2_bo"])),
                   ("ff_w1", L2["ff_w1"]), ("ff_b1", L2["ff_b1"].reshape(-1, P).T), ("ff_w2", tiles(L2["ff_w2"])),
                   ("ff_b2", col(L2["ff_b2"]))]
    packs["p5"] = [("w_fc", tiles(i["L2_ffn_w_fc"])), ("w_proj", i["L2_ffn_w_proj"]), ("vT", i["L2_ffn_v"].T),
                   ("fastT", i["L2_ffn_fast_b"].T), ("uT", i["L2_ffn_u"].T),
                   ("gate", np.broadcast_to(i["L2_ffn_gate"].reshape(1, 1), (P, 1)))]
    L3 = {n[len("L3_xcond_"):]: a for n, a in i.items() if n.startswith("L3_xcond_")}
    feature = np.arange(P) // H3
    by_feature = np.arange(P) % H3 * DH3 + feature
    half = DH3 // 2
    angle = np.arange(T, dtype=np.float32)[None] / np.float32(10000.0) ** (feature % half / half).astype(np.float32)[:, None]
    sign = np.where(feature < half, -1.0, 1.0).astype(np.float32)[:, None]
    partner = by_feature ^ half
    spread = np.zeros((P, P), np.float32)
    for j in range(0, P, 32):
        spread[j + DH3, j:j + 32] = 1.0
    packs["p6n"] = [("norm_w", np.concatenate([L3[f"n{j}_w"][l].T for l in range(NL3) for j in (1, 2, 3)], axis=1)),
                   ("norm_b", np.concatenate([L3[f"n{j}_b"][l].reshape(2, D).T for l in range(NL3) for j in (1, 2, 3)], axis=1))]
    packs["p6"] = [("cos", np.cos(angle).astype(np.float32)), ("sin", (np.sin(angle) * sign).astype(np.float32)),
                   ("spread", spread)]
    layout = {p: [(n, a.shape[0], a.shape[1]) for n, a in rows] for p, rows in packs.items()}
    arrays = {}
    for p, rows in packs.items():
        whole = np.zeros((P, sum(a.shape[1] for _, a in rows)), np.float32)
        at = 0
        for _, a in rows:
            whole[0:a.shape[0], at:at + a.shape[1]] = a
            at += a.shape[1]
        arrays[p] = whole
    arrays["x"] = np.ascontiguousarray(i["x"].transpose(2, 0, 1))
    arrays["ctx"] = np.ascontiguousarray(i["ctx_1024"].transpose(2, 0, 1))
    arrays["cond"] = np.ascontiguousarray(i["cond_1024"].T)

    def expert(gate, up, down):
        n = down.shape[0]
        full = np.zeros((-(-n // P) * P, D), np.float32)
        full[0:n] = down
        return np.concatenate([gate, up, tiles(full)], axis=1)

    gu, dn = i["L0_ffn_experts_gate_up"], i["L0_ffn_experts_down"]
    arrays["experts0"] = np.stack(
        [expert(gu[e, 0:I0].T, gu[e, I0:].T, dn[e].T) for e in range(E0)] +
        [expert(i["L0_ffn_shared_gate_w"][s:s + I0].T, i["L0_ffn_shared_up_w"][s:s + I0].T,
                i["L0_ffn_shared_down_w"][:, s:s + I0].T) for s in range(0, SI0, I0)])
    arrays["experts1"] = np.stack(
        [expert(i["L1_ffn_routed_w1"][e], i["L1_ffn_routed_w2"][e], i["L1_ffn_routed_w3"][e]) for e in range(E1)] +
        [expert(i["L1_ffn_shared_w1"][0][:, s:s + I1], i["L1_ffn_shared_w2"][0][:, s:s + I1],
                i["L1_ffn_shared_w3"][0][s:s + I1]) for s in range(0, SI1, I1)])
    arrays["experts4"] = np.stack(
        [expert(i["L3_ffn_eW1"][e].T, i["L3_ffn_eW3"][e].T, i["L3_ffn_eW2"][e].T) for e in range(E4)] +
        [expert(i["L3_ffn_sW1"].T, i["L3_ffn_sW3"].T, i["L3_ffn_sW2"].T)])
    for n in ("attn1", "attn2"):
        arrays[n] = np.stack([np.concatenate([L2[n + "_wq"][:, g:g + P], L2[n + "_wk"][:, g:g + P], L2[n + "_wv"][:, g:g + P],
                                              L2[n + "_wo"][g:g + P]], axis=1) for g in range(0, INNER2, P)])
    arrays["attn4"] = np.concatenate([i["L3_ffn_" + n].T for n in ("Wq", "Wkc", "Wvc", "Wo")], axis=1)[None]

    def quadrants(a):
        out = np.zeros((P, H3 // 4, D), np.float32)
        for h in range(H3):
            out[32 * (h % 4):32 * (h % 4) + DH3, h // 4] = a[h * DH3:(h + 1) * DH3]
        return out.reshape(P, -1)

    def attention3(q, kk, v, o):
        return np.concatenate([q.T[:, by_feature], q.T[:, partner], kk.T[:, by_feature], kk.T[:, partner], v.T, quadrants(o.T)], axis=1)

    arrays["t6_wa"] = np.stack([attention3(*np.split(L3["qkv_w"][l], 3), L3["so_w"][l]) for l in range(NL3)])
    arrays["t6_wx"] = np.stack([attention3(L3["cq_w"][l], L3["ck_w"][l], L3["cv_w"][l], L3["co_w"][l]) for l in range(NL3)])
    arrays["t6_wf"] = np.stack([np.concatenate([L3["f1_w"][l].T, tiles(L3["f2_w"][l].T), L3["f1_b"][l].reshape(-1, P).T,
                                                col(L3["f2_b"][l])], axis=1) for l in range(NL3)])
    masks = np.concatenate([i["mask_BxS_bf0"], i["mask_BxS2_bf0"]], axis=1)
    arrays["masks"] = np.ascontiguousarray(np.broadcast_to(masks, (H3, B, T + S)))
    return arrays, layout


def kernel(**inputs):
    import concourse.bacc as bacc
    from concourse.bass_utils import run_bass_kernel_spmd

    arrays, layout = laid_out({n: np.asarray(a) for n, a in inputs.items()})
    nc = bacc.Bacc("TRN2", target_bir_lowering=False, num_devices=1)
    dram = {n: nc.dram_tensor(f"in_{n}", a.shape, mybir.dt.from_np(a.dtype), kind="ExternalInput").ap()
            for n, a in arrays.items()}
    out = nc.dram_tensor("out_x", (P, B, T), F32, kind="ExternalOutput").ap()
    build(nc, dram, layout, out)
    r = run_bass_kernel_spmd(nc, [{f"in_{n}": a for n, a in arrays.items()}], core_ids=[0])
    return np.ascontiguousarray(r.results[0]["out_x"].transpose(1, 2, 0))
```

```python
import concourse.bass as bass
from concourse import mybir
from contextlib import ExitStack
import math
import numpy as np

F32 = mybir.dt.float32
BF16 = mybir.dt.bfloat16
U8 = mybir.dt.uint8
ALU = mybir.AluOpType
ACT = mybir.ActivationFunctionType
AX = mybir.AxisListType.X
AXY = mybir.AxisListType.XY

B, T, D, S = 2, 512, 128, 77
NT = B * T
P = 128
TT = T // P
NTT = NT // P
LN_EPS = 1e-5

E0, I0, SI0 = 8, 176, 352
E1, I1, SI1 = 16, 128, 512
H2, DH2 = 16, 64
INNER2, DFF2 = H2 * DH2, 4 * D
NL3, H3, DH3, DFF3 = 6, 16, 8, 512
E4, H4, DK4, F4 = 8, 4, 32, 128
HID5, RANK5 = 512, 16


class Steps:

    def __init__(self, k, stage, lanes, lead=0, **steps):
        self.sems, self.place, self.size, self.lead, self.lanes = {}, {}, {}, lead, lanes
        for engine, names in steps.items():
            names = names.split()
            self.size[engine] = len(names)
            for lane in range(lanes):
                self.sems[engine, lane] = k.semaphore(f"{stage}_{engine}_{lane}")
            for i, name in enumerate(names):
                assert name not in self.place, name
                self.place[name] = (engine, i)

    def sem(self, name, lane=0):
        return self.sems[self.place[name][0], lane], 1

    def at(self, name, lane=0, round=0):
        engine, i = self.place[name]
        return self.sems[engine, lane], round * self.size[engine] + (i + 1 + self.lead * self.size[engine])

    def prime(self, eng, engine):
        for lane in range(self.lanes):
            eng.sem_inc(self.sems[engine, lane], self.lead * self.size[engine])


class Core:

    def __init__(self, nc, ctx, dram, layout):
        def sb(name, shape, dt=F32):
            return ctx.enter_context(nc.sbuf_tensor(name, shape, dt))

        self.nc, self.dram, self.layout = nc, dram, layout
        self.x = sb("x_res", [P, B, T])
        self.xn = sb("x_norm", [P, B, T])
        self.y = sb("y", [P, B, T])
        self.cond = sb("condT", [P, B])
        self.ctxT = sb("ctxT", [P, B, S])
        self.mean_w = sb("mean_w", [P, P])
        self.ones = sb("ones", [P, P])
        self.ident = sb("ident", [P, P])
        self.eps = sb("eps", [P, 1])
        self.cent = sb("cent", [P, B, T])
        self.sq = sb("sq", [P, B, T])
        self.rstd = sb("rstd", [P, B, T])
        self.ps = ctx.enter_context(nc.psum_tensor("ps", [P, 8, 512], F32))
        self.signals = []

    def semaphore(self, name):
        self.signals.append(self.nc.alloc_semaphore(name))
        return self.signals[-1]

    def release(self):
        self.nc.clear_and_free_semaphores(self.signals)
        self.nc.all_engine_barrier()
        self.signals = []

    def weights(self, ctx, pack):
        rows = self.layout[pack]
        whole = ctx.enter_context(self.nc.sbuf_tensor("w_" + pack, [P, sum(n for _, _, n in rows)], F32))
        parts, at = {}, 0
        for name, p, n in rows:
            parts[name] = whole[0:p, at:at + n]
            at += n
        return whole, parts


LN_PE, LN_ACT, LN_DVE = "{0}.mean {0}.var", "{0}.sq {0}.ln {0}.rstd", "{0}.cent {0}.norm"
LNA_DVE = LN_DVE + " {0}.affine"


def ln_pe(k, pe, st, name, src, width, banks, lanes, ready, rnd=0):
    for c in range(lanes):
        ready(c)
        k.nc.tensor.matmul(k.ps[:, banks[c], 0:width], k.mean_w[:], src(c), start=True, stop=True)\
            .then_inc(*st.sem(name + ".mean", c))
    for c in range(lanes):
        pe.wait_ge(*st.at(name + ".sq", c, rnd))
        k.nc.tensor.matmul(k.ps[:, banks[c], 0:width], k.mean_w[:], k.sq[:, c, 0:width], start=True, stop=True)\
            .then_inc(*st.sem(name + ".var", c))


def ln_act(k, act, st, name, width, banks, lanes, rnd=0):
    for c in range(lanes):
        act.wait_ge(*st.at(name + ".cent", c, rnd))
        k.nc.scalar.activation(k.sq[:, c, 0:width], k.cent[:, c, 0:width], ACT.Square)\
            .then_inc(*st.sem(name + ".sq", c))
    k.nc.scalar.preload_act_table_set("natural_log_exp_and_others")
    for c in range(lanes):
        act.wait_ge(*st.at(name + ".var", c, rnd))
        k.nc.scalar.activation(k.rstd[:, c, 0:width], k.ps[:, banks[c], 0:width], ACT.Ln, bias=k.eps[:, 0:1])\
            .then_inc(*st.sem(name + ".ln", c))
        act.wait_ge(*st.at(name + ".ln", c, rnd))
        k.nc.scalar.activation(k.rstd[:, c, 0:width], k.rstd[:, c, 0:width], ACT.Exp, scale=-0.5)\
            .then_inc(*st.sem(name + ".rstd", c))


def ln_dve(k, dve, st, name, src, dst, width, banks, lanes, rnd=0, affine=None):
    for c in range(lanes):
        dve.wait_ge(*st.at(name + ".mean", c, rnd))
        k.nc.vector.tensor_tensor(k.cent[:, c, 0:width], src(c), k.ps[:, banks[c], 0:width], ALU.subtract)\
            .then_inc(*st.sem(name + ".cent", c))
    for c in range(lanes):
        dve.wait_ge(*st.at(name + ".rstd", c, rnd))
        k.nc.vector.tensor_tensor(dst(c), k.cent[:, c, 0:width], k.rstd[:, c, 0:width], ALU.mult)\
            .then_inc(*st.sem(name + ".norm", c))
        if affine is not None:
            gain, shift = affine(c)
            dve.wait_ge(*st.at(name + ".norm", c, rnd))
            k.nc.vector.tensor_scalar(dst(c), dst(c), gain, shift, ALU.mult, ALU.add)\
                .then_inc(*st.sem(name + ".affine", c))


def setup_stage(k):
    nc = k.nc
    with ExitStack() as ctx:
        made = k.semaphore("constants_made")
        landed = k.semaphore("inputs_landed")
        block = ctx.enter_context(nc.Block())

        @block.sync
        def _(sp):
            sp.dma_start(k.x[:], k.dram["x"]).then_inc(landed, 16)
            sp.dma_start(k.ctxT[:], k.dram["ctx"]).then_inc(landed, 16)
            sp.dma_start(k.cond[:], k.dram["cond"]).then_inc(landed, 16)
            sp.wait_ge(landed, 16 * 3)

        @block.gpsimd
        def _(pool):
            nc.gpsimd.memset(k.ident[:], 0.0).then_inc(made, 1)
            nc.gpsimd.memset(k.mean_w[:], 1.0 / D).then_inc(made, 1)
            nc.gpsimd.memset(k.ones[:], 1.0).then_inc(made, 1)
            nc.gpsimd.memset(k.eps[:], LN_EPS).then_inc(made, 1)
            pool.wait_ge(made, 4)
            nc.gpsimd.affine_select(out=k.ident[:], in_=k.ident[:], compare_op=ALU.not_equal, fill=1.0, base=0,
                                    pattern=[[-1, P]], channel_multiplier=1).then_inc(made, 1)
            pool.wait_ge(made, 5)


def load_stage(k, whole, pack):
    with ExitStack() as ctx:
        landed = k.semaphore("landed_" + pack)
        block = ctx.enter_context(k.nc.Block())

        @block.sync
        def _(sp):
            sp.dma_start(whole[:], k.dram[pack]).then_inc(landed, 16)
            sp.wait_ge(landed, 16)


def store_stage(k, out):
    nc = k.nc
    with ExitStack() as ctx:
        stored = k.semaphore("result_stored")
        block = ctx.enter_context(nc.Block())

        @block.sync
        def _(sp):
            sp.dma_start(out, k.x[:]).then_inc(stored, 16)
            sp.wait_ge(stored, 16)


def slots_stage(k, w):
    nc, ps = k.nc, k.ps
    ROUNDS = 3
    SCALE = math.sqrt(D)
    with ExitStack() as ctx:
        def sb(name, shape, dt=F32):
            return ctx.enter_context(nc.sbuf_tensor("s0_" + name, shape, dt))

        slots, mid, y, q, hid = (sb(n, [P, B, T]) for n in ("slots", "mid", "y", "q", "hid"))
        cn, kT = sb("cn", [P, B, S]), sb("kT", [P, B, S])
        v = sb("v", [P, B, D])
        e, rsum = sb("e", [P, B, T]), sb("rsum", [P, B, T])
        top, ssum = sb("top", [P, B]), sb("ssum", [P, B])
        sig, base = sb("sig", [P, 1]), sb("base", [P, B])
        BANK = (0, 4)
        pre = Steps(k, "s0pre", 2,
                    pe="c.mean c.var x.mean x.var key value", act="c.sq c.ln c.rstd x.sq x.ln x.rstd sig",
                    dve="c.cent c.norm c.affine x.cent x.norm kT v base slots")
        st = Steps(k, "s0", 2,
                   pe="q.mean q.var query logit colsum upd wu m.mean m.var w1 w2 p.mean p.var",
                   act="q.sq q.ln q.rstd e m.sq m.ln m.rstd gelu p.sq p.ln p.rstd",
                   dve="q.cent q.norm q.affine qT top tops inv attn rsum updn wuo m.cent m.norm m.affine w2o "
                       "p.cent p.norm p.affine")
        end = k.semaphore("s0_added")
        block = ctx.enter_context(nc.Block())

        @block.tensor
        def _(pe):
            ln_pe(k, pe, pre, "c", lambda c: k.ctxT[:, c], S, (1, 5), 2, lambda c: None)
            ln_pe(k, pe, pre, "x", lambda c: k.x[:, c], T, BANK, 2, lambda c: None if c else pe.wait_ge(*pre.at("c.rstd", 1)))
            for c in range(B):
                pe.wait_ge(*pre.at("c.affine", c))
                nc.tensor.matmul(ps[:, 2 + 4 * c, 0:S], w["wk"], cn[:, c], start=True, stop=True).then_inc(*pre.sem("key", c))
                nc.tensor.matmul(ps[0:S, 3 + 4 * c, 0:D], cn[:, c], w["wv"], start=True, stop=False)
                nc.tensor.matmul(ps[0:S, 3 + 4 * c, 0:D], k.ones[0:1, 0:S], w["bv"], start=False, stop=True)\
                    .then_inc(*pre.sem("value", c))
            for r in range(ROUNDS):
                ready = (lambda c: pe.wait_ge(*pre.at("slots", c))) if r == 0 else \
                    (lambda c: pe.wait_ge(*st.at("p.affine", c, r - 1)))
                ln_pe(k, pe, st, "q", lambda c: slots[:, c], T, BANK, 2, ready, r)
                for c in range(B):
                    pe.wait_ge(*st.at("q.affine", c, r))
                    nc.tensor.matmul(ps[:, 1 + 4 * c], w["wq"], y[:, c], start=True, stop=True).then_inc(*st.sem("query", c))
                for c in range(B):
                    pe.wait_ge(*st.at("qT", c, r))
                    nc.tensor.matmul(ps[0:S, 2 + 4 * c], kT[:, c], q[:, c], start=True, stop=True).then_inc(*st.sem("logit", c))
                for c in range(B):
                    pe.wait_ge(*st.at("attn", c, r))
                    nc.tensor.matmul(ps[:, 3 + 4 * c], k.ones[0:S, :], e[0:S, c], start=True, stop=True)\
                        .then_inc(*st.sem("colsum", c))
                    nc.tensor.matmul(ps[:, 1 + 4 * c], v[0:S, c], e[0:S, c], start=True, stop=True)\
                        .then_inc(*st.sem("upd", c))
                for c in range(B):
                    pe.wait_ge(*st.at("updn", c, r))
                    nc.tensor.matmul(ps[:, 2 + 4 * c], w["wu"], y[:, c], start=True, stop=True).then_inc(*st.sem("wu", c))
                ln_pe(k, pe, st, "m", lambda c: mid[:, c], T, BANK, 2, lambda c: pe.wait_ge(*st.at("wuo", c, r)), r)
                for c in range(B):
                    pe.wait_ge(*st.at("m.affine", c, r))
                    nc.tensor.matmul(ps[:, 1 + 4 * c], w["w1"], y[:, c], start=True, stop=True).then_inc(*st.sem("w1", c))
                for c in range(B):
                    pe.wait_ge(*st.at("gelu", c, r))
                    nc.tensor.matmul(ps[:, 2 + 4 * c], w["w2"], hid[:, c], start=True, stop=True).then_inc(*st.sem("w2", c))
                ln_pe(k, pe, st, "p", lambda c: mid[:, c], T, BANK, 2, lambda c: pe.wait_ge(*st.at("w2o", c, r)), r)

        @block.scalar
        def _(act):
            ln_act(k, act, pre, "c", S, (1, 5), 2)
            ln_act(k, act, pre, "x", T, BANK, 2)
            nc.scalar.activation(sig[:], w["q_logsig"], ACT.Exp).then_inc(*pre.sem("sig"))
            for r in range(ROUNDS):
                ln_act(k, act, st, "q", T, BANK, 2, r)
                for c in range(B):
                    act.wait_ge(*st.at("tops", c, r))
                    nc.scalar.activation(e[0:S, c], ps[0:S, 2 + 4 * c], ACT.Exp, bias=top[0:S, c:c + 1], scale=SCALE,
                                         accum_out=ssum[0:S, c:c + 1]).then_inc(*st.sem("e", c))
                ln_act(k, act, st, "m", T, BANK, 2, r)
                for c in range(B):
                    act.wait_ge(*st.at("w1", c, r))
                    nc.scalar.activation(hid[:, c], ps[:, 1 + 4 * c], ACT.Gelu, bias=w["b1"]).then_inc(*st.sem("gelu", c))
                ln_act(k, act, st, "p", T, BANK, 2, r)

        @block.vector
        def _(dve):
            ln_dve(k, dve, pre, "c", lambda c: k.ctxT[:, c], lambda c: cn[:, c], S, (1, 5), 2,
                   affine=lambda c: (w["lnkv_g"], w["lnkv_b"]))
            ln_dve(k, dve, pre, "x", lambda c: k.x[:, c], lambda c: k.xn[:, c], T, BANK, 2)
            for c in range(B):
                dve.wait_ge(*pre.at("key", c))
                nc.vector.tensor_scalar(kT[:, c], ps[:, 2 + 4 * c, 0:S], w["bk"], None, ALU.add).then_inc(*pre.sem("kT", c))
                dve.wait_ge(*pre.at("value", c))
                nc.vector.tensor_copy(v[0:S, c], ps[0:S, 3 + 4 * c, 0:D]).then_inc(*pre.sem("v", c))
                nc.vector.tensor_tensor(base[:, c:c + 1], w["b2"], k.cond[:, c:c + 1], ALU.add).then_inc(*pre.sem("base", c))
                if c == 0:
                    dve.wait_ge(*pre.at("sig"))
                dve.wait_ge(*pre.at("x.norm", c))
                nc.vector.tensor_scalar(slots[:, c], k.xn[:, c], sig[:, 0:1], w["q_mu"], ALU.mult, ALU.add)\
                    .then_inc(*pre.sem("slots", c))
            for r in range(ROUNDS):
                ln_dve(k, dve, st, "q", lambda c: slots[:, c], lambda c: y[:, c], T, BANK, 2, r,
                       affine=lambda c: (w["lnq_g"], w["lnq_b"]))
                for c in range(B):
                    dve.wait_ge(*st.at("query", c, r))
                    nc.vector.tensor_scalar(q[:, c], ps[:, 1 + 4 * c], w["bq"], None, ALU.add).then_inc(*st.sem("qT", c))
                for c in range(B):
                    dve.wait_ge(*st.at("logit", c, r))
                    nc.vector.tensor_reduce(top[0:S, c:c + 1], ps[0:S, 2 + 4 * c], AX, ALU.max, negate=True)\
                        .then_inc(*st.sem("top", c))
                    dve.wait_ge(*st.at("top", c, r))
                    nc.vector.tensor_scalar(top[0:S, c:c + 1], top[0:S, c:c + 1], SCALE, None, ALU.mult)\
                        .then_inc(*st.sem("tops", c))
                for c in range(B):
                    dve.wait_ge(*st.at("e", c, r))
                    nc.vector.reciprocal(ssum[0:S, c:c + 1], ssum[0:S, c:c + 1]).then_inc(*st.sem("inv", c))
                    dve.wait_ge(*st.at("inv", c, r))
                    nc.vector.tensor_scalar(e[0:S, c], e[0:S, c], ssum[0:S, c:c + 1], 1e-8, ALU.mult, ALU.add)\
                        .then_inc(*st.sem("attn", c))
                for c in range(B):
                    dve.wait_ge(*st.at("colsum", c, r))
                    nc.vector.reciprocal(rsum[:, c], ps[:, 3 + 4 * c]).then_inc(*st.sem("rsum", c))
                    dve.wait_ge(*st.at("upd", c, r))
                    dve.wait_ge(*st.at("rsum", c, r))
                    nc.vector.tensor_tensor(y[:, c], rsum[:, c], ps[:, 1 + 4 * c], ALU.mult).then_inc(*st.sem("updn", c))
                for c in range(B):
                    dve.wait_ge(*st.at("wu", c, r))
                    nc.vector.scalar_tensor_tensor(out=mid[:, c], in0=ps[:, 2 + 4 * c], scalar=w["bu"], in1=slots[:, c],
                                                   op0=ALU.add, op1=ALU.add).then_inc(*st.sem("wuo", c))
                ln_dve(k, dve, st, "m", lambda c: mid[:, c], lambda c: y[:, c], T, BANK, 2, r,
                       affine=lambda c: (w["lnm_g"], w["lnm_b"]))
                for c in range(B):
                    dve.wait_ge(*st.at("w2", c, r))
                    nc.vector.scalar_tensor_tensor(out=mid[:, c], in0=ps[:, 2 + 4 * c], scalar=base[:, c:c + 1],
                                                   in1=mid[:, c], op0=ALU.add, op1=ALU.add).then_inc(*st.sem("w2o", c))
                ln_dve(k, dve, st, "p", lambda c: mid[:, c], lambda c: slots[:, c], T, BANK, 2, r,
                       affine=lambda c: (w["lnp_g"], w["lnp_b"]))
            for c in range(B):
                dve.wait_ge(*st.at("p.affine", c, ROUNDS - 1))
                nc.vector.tensor_tensor(k.x[:, c], k.x[:, c], slots[:, c], ALU.add).then_inc(end, 1)
            dve.wait_ge(end, 2)


def norm_stage(k, label):
    nc = k.nc
    with ExitStack() as ctx:
        st = Steps(k, label, 2, pe=LN_PE.format("x"), act=LN_ACT.format("x"), dve=LN_DVE.format("x"))
        block = ctx.enter_context(nc.Block())

        @block.tensor
        def _(pe):
            ln_pe(k, pe, st, "x", lambda c: k.x[:, c], T, (0, 4), 2, lambda c: None)

        @block.scalar
        def _(act):
            ln_act(k, act, st, "x", T, (0, 4), 2)

        @block.vector
        def _(dve):
            ln_dve(k, dve, st, "x", lambda c: k.x[:, c], lambda c: k.xn[:, c], T, (0, 4), 2)
            for c in range(B):
                dve.wait_ge(*st.at("x.norm", c))


PICK = "{0}.max {0}.eq {0}.rank {0}.first {0}.pick"


def pick_dve(k, dve, st, name, sel, top, first, eq, rank, pick, E):
    V = k.nc.vector
    V.tensor_reduce(top[:], sel[:], AX, ALU.max).then_inc(*st.sem(name + ".max"))
    dve.wait_ge(*st.at(name + ".max"))
    V.tensor_tensor(eq[:], sel[:], top[:].unsqueeze(2).broadcast_to([P, NTT, E]), ALU.is_equal).then_inc(*st.sem(name + ".eq"))
    dve.wait_ge(*st.at(name + ".eq"))
    V.tensor_tensor(eq[:], eq[:], rank.unsqueeze(1).broadcast_to([P, NTT, E]), ALU.mult).then_inc(*st.sem(name + ".rank"))
    dve.wait_ge(*st.at(name + ".rank"))
    V.tensor_reduce(first[:], eq[:], AX, ALU.max).then_inc(*st.sem(name + ".first"))
    dve.wait_ge(*st.at(name + ".first"))
    V.tensor_tensor(pick[:], eq[:], first[:].unsqueeze(2).broadcast_to([P, NTT, E]), ALU.is_equal).then_inc(*st.sem(name + ".pick"))
    dve.wait_ge(*st.at(name + ".pick"))


def moe_stage(k, label, kind, E, I, n_shared, expert_dram, w):
    nc, ps = k.nc, k.ps
    N = E + n_shared
    cuts = [(i, min(P, I - i)) for i in range(0, I, P)]
    nk = len(cuts)
    WC = 2 * I + nk * D
    with ExitStack() as ctx:
        def sb(name, shape, dt=F32):
            return ctx.enter_context(nc.sbuf_tensor(f"{label}_{name}", shape, dt))

        logit, sel, eq, pick1, pick2 = (sb(n, [P, NTT, E]) for n in ("logit", "sel", "eq", "pick1", "pick2"))
        gate = sb("gate", [P, NTT, N])
        top1, top2, first, tot = (sb(n, [P, NTT]) for n in ("top1", "top2", "first", "tot"))
        sg = sb("sg", [P, NTT])
        wb = [sb(f"wexp{i}", [P, WC]) for i in range(2)]
        th = sb("th", [P, B, nk, T])
        h = sb("h", [P, 2, B, nk, T])
        scaled = sb("scaled", [P, B, TT, D])
        acc = sb("acc", [P, B, TT, D])
        scored = "score sel" if kind == "sigmoid" else "lg max sub sum inv score sel"
        gated = "both gates" if kind != "renorm" else "gap more inv2 w2 g1 g2 gates"
        rt = Steps(k, label + "r", 1, pe="logits",
                   act="prob" + (" gap_exp" if kind == "renorm" else " shared_tanh" if kind == "scores" else ""),
                   dve=" ".join((scored, PICK.format("a"), "drop", PICK.format("b"), gated, "shared")), pool="acc0")
        R = E + (kind == "scores")
        st = Steps(k, label, 2,
                   pe=" ".join(f"gu{i}" for i in range(nk)), act=" ".join(f"t{i}" for i in range(nk)),
                   dve=" ".join(f"s{i} h{i}" for i in range(nk)))
        dn = Steps(k, label + "d", 2, pe="y", dve="scaled", pool="added")
        landed = [k.semaphore(f"{label}_expert_landed{i}") for i in range(2)]
        turned = k.semaphore(f"{label}_turned")
        ended = k.semaphore(f"{label}_ended")
        peel = 2 if N % 2 == 0 else 3
        GB, UB, YB = (0, 3), (1, 4), (2, 5)
        block = ctx.enter_context(nc.Block())

        def rounds(eng, body):
            for e in range(peel):
                body(e, e % 2, e, e // 2)
            with eng.Fori(0, (N - peel) // 2) as j:
                for u in range(2):
                    body(peel + u + 2 * j, (peel + u) % 2, 3, (peel + u) // 2 + j)

        @block.sync
        def _(sp):
            def load(e, b, lead, n):
                if lead >= 2:
                    for c in range(B):
                        sp.wait_ge(*dn.at("y", c, e - 2))
                sp.dma_start(wb[b][:], expert_dram[bass.ds(e, 1)].rearrange("e p n -> (e p) n")
                             if lead == 3 else expert_dram[e]).then_inc(landed[b], 16)
            rounds(sp, load)
            sp.wait_ge(landed[0], 16 * ((N + 1) // 2))
            sp.wait_ge(landed[1], 16 * (N // 2))

        @block.tensor
        def _(pe):
            for t in range(NTT):
                mm = nc.tensor.matmul(ps[:, 6, t * R:(t + 1) * R], k.xn[:, t // TT, (t % TT) * P:(t % TT + 1) * P],
                                      w["router"], start=True, stop=True)
            mm.then_inc(*rt.sem("logits"))

            def up(e, b, lead, n):
                pe.wait_ge(landed[b], 16 * (n + 1))
                for i, (o, m) in enumerate(cuts):
                    for c in range(B):
                        if i > 0:
                            pe.wait_ge(*st.at(f"h{i - 1}", c, e))
                        elif lead:
                            pe.wait_ge(*st.at(f"h{nk - 1}", c, e - 1))
                        nc.tensor.matmul(ps[0:m, GB[c]], wb[b][:, o:o + m], k.xn[:, c], start=True, stop=True)
                        nc.tensor.matmul(ps[0:m, UB[c]], wb[b][:, I + o:I + o + m], k.xn[:, c], start=True, stop=True)\
                            .then_inc(*st.sem(f"gu{i}", c))

            def down(e, b, lead):
                for c in range(B):
                    pe.wait_ge(*st.at(f"h{nk - 1}", c, e))
                    if lead:
                        pe.wait_ge(*dn.at("scaled", c, e - 1))
                    for t in range(TT):
                        for i, (o, m) in enumerate(cuts):
                            mm = nc.tensor.matmul(ps[:, YB[c], t * D:(t + 1) * D], h[0:m, b, c, i, t * P:(t + 1) * P],
                                                  wb[b][0:m, 2 * I + i * D:2 * I + (i + 1) * D],
                                                  start=(i == 0), stop=(i == nk - 1))
                    mm.then_inc(*dn.sem("y", c))

            def body(e, b, lead, n):
                up(e, b, lead, n)
                if lead:
                    down(e - 1, 1 - b, min(lead - 1, 1))
            rounds(pe, body)
            down(N - 1, (N - 1) % 2, 1)
            pe.wait_ge(*dn.at("scaled", 0, N - 1))
            pe.wait_ge(*dn.at("scaled", 1, N - 1))
            for c in range(B):
                pe.wait_ge(*dn.at("added", c, N - 1))
                for t in range(TT):
                    mm = nc.tensor.transpose(ps[:, YB[c], t * P:(t + 1) * P], acc[:, c, t], k.ident[:])
                mm.then_inc(turned, 1)

        @block.scalar
        def _(act):
            lg = ps[:, 6, 0:NTT * R].rearrange("p (t e) -> p t e", e=R)
            if kind == "sigmoid":
                act.wait_ge(*rt.at("logits"))
                nc.scalar.activation(logit[:], lg[:, :, 0:E], ACT.Tanh, scale=0.5).then_inc(*rt.sem("prob"))
            else:
                act.wait_ge(*rt.at("sub"))
                nc.scalar.activation(logit[:], logit[:], ACT.Exp).then_inc(*rt.sem("prob"))
            if kind == "renorm":
                act.wait_ge(*rt.at("gap"))
                nc.scalar.activation(first[:], first[:], ACT.Exp).then_inc(*rt.sem("gap_exp"))
            if kind == "scores":
                nc.scalar.activation(sg[:], lg[:, :, E], ACT.Tanh, scale=0.5).then_inc(*rt.sem("shared_tanh"))

            def body(e, b, lead, n):
                for i, (o, m) in enumerate(cuts):
                    for c in range(B):
                        act.wait_ge(*st.at(f"gu{i}", c, e))
                        nc.scalar.activation(th[0:m, c, i], ps[0:m, GB[c]], ACT.Tanh, scale=0.5).then_inc(*st.sem(f"t{i}", c))
            rounds(act, body)

        @block.gpsimd
        def _(pool):
            nc.gpsimd.memset(acc[:], 0.0).then_inc(*rt.sem("acc0"))
            pool.wait_ge(*rt.at("acc0"))

            def body(e, b, lead, n):
                for c in range(B):
                    pool.wait_ge(*dn.at("scaled", c, e))
                    if lead:
                        pool.wait_ge(*dn.at("added", c, e - 1))
                    nc.gpsimd.tensor_tensor(acc[:, c], acc[:, c], scaled[:, c], ALU.add).then_inc(*dn.sem("added", c))
            rounds(pool, body)

        @block.vector
        def _(dve):
            V = nc.vector
            lg = ps[:, 6, 0:NTT * R].rearrange("p (t e) -> p t e", e=R)

            def wide(a):
                return a[:].unsqueeze(2).broadcast_to([P, NTT, E])

            def over_tokens(a):
                return a.unsqueeze(1).broadcast_to([P, NTT, E])

            def step(name, ins):
                ins.then_inc(*rt.sem(name))
                dve.wait_ge(*rt.at(name))

            if kind == "sigmoid":
                dve.wait_ge(*rt.at("prob"))
                step("score", V.tensor_scalar(logit[:], logit[:], 0.5, 0.5, ALU.mult, ALU.add))
                step("sel", V.tensor_tensor(sel[:], logit[:], over_tokens(w["bias"]), ALU.add))
            else:
                dve.wait_ge(*rt.at("logits"))
                if kind == "renorm":
                    step("lg", V.tensor_tensor(logit[:], lg[:, :, 0:E], over_tokens(w["bias"]), ALU.add))
                else:
                    step("lg", V.tensor_copy(logit[:], lg[:, :, 0:E]))
                step("max", V.tensor_reduce(top1[:], logit[:], AX, ALU.max))
                step("sub", V.tensor_tensor(logit[:], logit[:], wide(top1), ALU.subtract))
                dve.wait_ge(*rt.at("prob"))
                step("sum", V.tensor_reduce(tot[:], logit[:], AX, ALU.add))
                step("inv", V.reciprocal(tot[:], tot[:]))
                step("score", V.tensor_tensor(logit[:], logit[:], wide(tot), ALU.mult))
                step("sel", V.tensor_copy(sel[:], logit[:]))
            pick_dve(k, dve, rt, "a", sel, top1, first, eq, w["rank"], pick1, E)
            step("drop", V.scalar_tensor_tensor(out=sel[:], in0=pick1[:], scalar=-3e38, in1=sel[:],
                                                op0=ALU.mult, op1=ALU.add))
            pick_dve(k, dve, rt, "b", sel, top2, first, eq, w["rank"], pick2, E)
            if kind == "renorm":
                step("gap", V.tensor_tensor(first[:], top2[:], top1[:], ALU.subtract))
                dve.wait_ge(*rt.at("gap_exp"))
                step("more", V.tensor_scalar(tot[:], first[:], 1.0, None, ALU.add))
                step("inv2", V.reciprocal(top1[:], tot[:]))
                step("w2", V.tensor_tensor(top2[:], first[:], top1[:], ALU.mult))
                step("g1", V.tensor_tensor(pick1[:], pick1[:], wide(top1), ALU.mult))
                step("g2", V.tensor_tensor(pick2[:], pick2[:], wide(top2), ALU.mult))
                step("gates", V.tensor_tensor(gate[:, :, 0:E], pick1[:], pick2[:], ALU.add))
            else:
                step("both", V.tensor_tensor(pick1[:], pick1[:], pick2[:], ALU.add))
                step("gates", V.tensor_tensor(gate[:, :, 0:E], pick1[:], logit[:], ALU.mult))
            if kind == "scores":
                dve.wait_ge(*rt.at("shared_tanh"))
                step("shared", V.tensor_scalar(gate[:, :, E:N], sg[:].unsqueeze(2).broadcast_to([P, NTT, n_shared]),
                                               0.5, 0.5, ALU.mult, ALU.add))
            else:
                step("shared", V.memset(gate[:, :, E:N], 1.0))

            def body(e, b, lead, n):
                for i, (o, m) in enumerate(cuts):
                    for c in range(B):
                        dve.wait_ge(*st.at(f"t{i}", c, e))
                        V.scalar_tensor_tensor(out=th[0:m, c, i], in0=th[0:m, c, i], scalar=1.0, in1=ps[0:m, GB[c]],
                                               op0=ALU.add, op1=ALU.mult).then_inc(*st.sem(f"s{i}", c))
                    for c in range(B):
                        dve.wait_ge(*st.at(f"s{i}", c, e))
                        if lead >= 2 and i == 0:
                            dve.wait_ge(*dn.at("y", c, e - 2))
                        V.scalar_tensor_tensor(out=h[0:m, b, c, i], in0=th[0:m, c, i], scalar=0.5, in1=ps[0:m, UB[c]],
                                               op0=ALU.mult, op1=ALU.mult).then_inc(*st.sem(f"h{i}", c))
                if lead:
                    scale(e - 1, min(lead - 1, 1))

            def scale(e, lead):
                for c in range(B):
                    dve.wait_ge(*dn.at("y", c, e))
                    if lead:
                        dve.wait_ge(*dn.at("added", c, e - 1))
                    g = gate[:, c * TT:(c + 1) * TT, bass.ds(e, 1)] if not isinstance(e, int) else gate[:, c * TT:(c + 1) * TT, e:e + 1]
                    V.tensor_tensor(scaled[:, c], ps[:, YB[c]].rearrange("p (t d) -> p t d", d=D),
                                    g.broadcast_to([P, TT, D]), ALU.mult).then_inc(*dn.sem("scaled", c))
            rounds(dve, body)
            scale(N - 1, 1)
            for c in range(B):
                dve.wait_ge(turned, c + 1)
                V.tensor_tensor(k.x[:, c], k.x[:, c], ps[:, YB[c]], ALU.add).then_inc(ended, 1)
            dve.wait_ge(ended, 2)


def gru_stage(k, w):
    nc, ps = k.nc, k.ps
    UNROLL = 64
    WARMING = 16
    with ExitStack() as ctx:
        def sb(name, shape, dt=F32):
            return ctx.enter_context(nc.sbuf_tensor("g_" + name, shape, dt))

        gx = sb("gx", [P, T + 1, 8])
        encp = sb("encp", [P, B, S])
        encg = sb("encg", [P, 3, B, S])
        identb = sb("identb", [P, P], BF16)
        gxs = sb("gxs", [P, 3, T + 1, 8], BF16)
        encs = sb("encs", [P, 3, B, S], BF16)
        uhs = sb("uhs", [P, 3, 3 * D], BF16)
        hs = [sb(f"hs{i}", [P, 3, B], BF16) for i in range(2)]
        rest, half_h = sb("rest", [P, B]), sb("half_h", [P, B])
        vrep = sb("vrep", [P, P])
        h = [sb(f"h{i}", [P, B]) for i in range(2)]
        th, e = sb("th", [P, B, S]), sb("e", [P, B, S])
        used = sb("used", [P, 3, B, S])
        ntop, esum, sinv = sb("ntop", [P, B]), sb("esum", [P, B]), sb("sinv", [P, B])
        mac = sb("mac", [P, 6])
        zr, tzr = sb("zr", [P, 4]), sb("tzr", [P, 4])
        rhh, hb, hin, pre_h, hh = (sb(n, [P, B]) for n in ("rhh", "hb", "hin", "pre_h", "hh"))
        omz, zh = sb("omz", [P, B]), sb("zh", [P, B])
        with ExitStack() as pctx:
            pre = Steps(k, "gpre", 2, pe="encp c0 c1 c2 g0 g1 g2", dve="encp_s c0_s c1_s c2_s gx0 gx1 gx2 vrep", pool="zero h0")
            split = k.semaphore("g_split")
            block = pctx.enter_context(nc.Block())

            @block.tensor
            def _(pe):
                for c in range(B):
                    nc.tensor.matmul(ps[:, 4 * c, 0:S], w["att_e"], k.ctxT[:, c], start=True, stop=True).then_inc(*pre.sem("encp", c))
                for g in range(3):
                    for c in range(B):
                        if g:
                            pe.wait_ge(*pre.at(f"c{g - 1}_s", c))
                        nc.tensor.matmul(ps[:, 4 * c + 1, 0:S], w["wic"][:, g * D:(g + 1) * D], k.ctxT[:, c],
                                         start=True, stop=True).then_inc(*pre.sem(f"c{g}", c))
                for g in range(3):
                    for c in range(B):
                        if g >= 2:
                            pe.wait_ge(*pre.at(f"gx{g - 2}", c))
                        nc.tensor.matmul(ps[:, 4 * c + 2 + g % 2], w["wix"][:, g * D:(g + 1) * D], k.xn[:, c],
                                         start=True, stop=True).then_inc(*pre.sem(f"g{g}", c))

            @block.gpsimd
            def _(pool):
                nc.gpsimd.memset(gx[:, :, 6:8], 0.0).then_inc(*pre.sem("zero", 0))
                nc.gpsimd.memset(gx[:, T:T + 1, 0:6], 0.0).then_inc(*pre.sem("zero", 1))
                nc.gpsimd.tensor_copy(h[0][:], k.cond[:]).then_inc(*pre.sem("h0"))
                pool.wait_ge(*pre.at("h0"))
                pool.wait_ge(*pre.at("zero", 1))

            @block.vector
            def _(dve):
                V = nc.vector
                for c in range(B):
                    dve.wait_ge(*pre.at("encp", c))
                    V.tensor_copy(encp[:, c], ps[:, 4 * c, 0:S]).then_inc(*pre.sem("encp_s", c))
                for g in range(3):
                    for c in range(B):
                        dve.wait_ge(*pre.at(f"c{g}", c))
                        V.tensor_copy(encg[:, g, c], ps[:, 4 * c + 1, 0:S]).then_inc(*pre.sem(f"c{g}_s", c))
                for g in range(3):
                    for c in range(B):
                        dve.wait_ge(*pre.at(f"g{g}", c))
                        V.tensor_scalar(gx[:, 0:T, 2 * g + c], ps[:, 4 * c + 2 + g % 2], w["bi"][:, g:g + 1], None, ALU.add)\
                            .then_inc(*pre.sem(f"gx{g}", c))
                V.tensor_copy(identb[:], k.ident[:])
                dve.wait_ge(*pre.at("zero", 1))
                count = 0
                for c in range(B):
                    dve.wait_ge(*pre.at("gx2", c))
                for rest, parts in ((encp[:], encs), (gx[:], gxs), (w["uh"], uhs)):
                    for i in range(3):
                        V.tensor_copy(parts[:, i], rest).then_inc(split, 1)
                        count += 1
                        dve.wait_ge(split, count)
                        if i < 2:
                            V.tensor_tensor(rest, rest, parts[:, i], ALU.subtract).then_inc(split, 1)
                            count += 1
                            dve.wait_ge(split, count)
                for c in range(B):
                    V.tensor_copy(vrep[:, 64 * c:64 * c + 64], w["v"].broadcast_to([P, 64])).then_inc(*pre.sem("vrep", c))
                for c in range(B):
                    dve.wait_ge(*pre.at("vrep", c))

        att = [[ps[:, 2 * i + c, 0:S] for c in range(B)] for i in range(2)]
        gates = [ps[:, 4 + i, 0:8] for i in range(2)]
        score = [ps[:, 6 + c, 0:S] for c in range(B)]

        st = Steps(k, "g", 1, pe="att0 att1 score0 score1 gates",
                   act="tanh0 tanh1 exp0 exp1 zr cand",
                   dve="hs1 half rest hs2 hs3 top0 top1 z0 r0 rhh r1 z1 sinv hb zr0 zr1 h0 h1 in0 in1 ph0 ph1 omz zh h", pool="saved")
        with nc.Fori(0, T // UNROLL) as j:
            with nc.Block() as block:
                @block.tensor
                def _(pe):
                    M = nc.tensor.matmul

                    def open_banks(p, t):
                        for c in range(B):
                            for i in range(3):
                                M(att[p][c], identb[:], encs[:, i, c], start=(i == 0), stop=False, skip_group_check=True)
                        for i in range(3):
                            mm = M(gates[p], identb[:], gxs[:, i, bass.ds(j * UNROLL + t, 1)].rearrange("p o g -> p (o g)"), start=(i == 0),
                                   stop=False, skip_group_check=True)
                        return mm

                    open_banks(0, 0)

                    def recurrent(p, g):
                        at = (0, 2, 6)[g]
                        for i, j in ((0, 0), (0, 1), (1, 0), (1, 1), (0, 2), (2, 0)):
                            mm = M(gates[p][:, at:at + 2], uhs[:, i, g * D:(g + 1) * D], hs[p][:, j], start=False,
                                   stop=(g == 2 and i == 2), skip_group_check=True)
                        return mm

                    def body(t, p):
                        if t:
                            pe.wait_ge(*st.at("h", round=t - 1))
                        for c in range(B):
                            M(att[p][c], w["att_h"], h[p][:, c:c + 1].broadcast_to([P, S]), start=False, stop=True,
                              skip_group_check=True).then_inc(*st.sem(f"att{c}"))
                        for c in range(B):
                            pe.wait_ge(*st.at(f"tanh{c}", round=t))
                            M(score[c], vrep[:], th[:, c], start=True, stop=True).then_inc(*st.sem(f"score{c}"))
                        pe.wait_ge(*st.at("hs3", round=t))
                        recurrent(p, 0)
                        recurrent(p, 1)
                        recurrent(p, 2).then_inc(*st.sem("gates"))
                        if t + 1 < UNROLL:
                            for n in range(WARMING):
                                M(ps[:, 2 * (1 - p), 256:512], identb[:], uhs[:, 0, 0:256], start=True, stop=True,
                                  skip_group_check=True)
                            open_banks(1 - p, t + 1)
                    for u in range(UNROLL):
                        body(u, u % 2)

                @block.scalar
                def _(act):
                    A = nc.scalar.activation

                    def body(t, p):
                        for c in range(B):
                            act.wait_ge(*st.at(f"att{c}", round=t))
                            A(th[:, c], att[p][c], ACT.Tanh).then_inc(*st.sem(f"tanh{c}"))
                        for c in range(B):
                            act.wait_ge(*st.at(f"top{c}", round=t))
                            A(e[:, c], score[c], ACT.Exp, bias=ntop[:, c:c + 1], accum_out=esum[:, c:c + 1])\
                                .then_inc(*st.sem(f"exp{c}"))
                        act.wait_ge(*st.at("zr1", round=t))
                        A(tzr[:], zr[:], ACT.Tanh, scale=0.5).then_inc(*st.sem("zr"))
                        act.wait_ge(*st.at("ph1", round=t))
                        A(hh[:], pre_h[:], ACT.Tanh).then_inc(*st.sem("cand"))
                    for u in range(UNROLL):
                        body(u, u % 2)

                @block.vector
                def _(dve):
                    V = nc.vector
                    def body(t, p):
                        G = gates[p]

                        def weigh(name, g, c):
                            V.scalar_tensor_tensor(out=used[:, g, c], in0=encg[:, g, c], scalar=1.0, in1=e[:, c], op0=ALU.mult, op1=ALU.mult,
                                                   accum_out=mac[:, 2 * g + c:2 * g + c + 1]).then_inc(*st.sem(name))

                        def fma(name, out, a, scalar, b):
                            V.scalar_tensor_tensor(out=out, in0=a, scalar=scalar, in1=b, op0=ALU.mult, op1=ALU.add)\
                                .then_inc(*st.sem(name))

                        if t:
                            dve.wait_ge(*st.at("h", round=t - 1))
                        V.tensor_copy(hs[p][:, 0], h[p][:]).then_inc(*st.sem("hs1"))
                        V.tensor_scalar(half_h[:], h[p][:], 0.5, None, ALU.mult).then_inc(*st.sem("half"))
                        dve.wait_ge(*st.at("hs1", round=t))
                        V.tensor_tensor(rest[:], h[p][:], hs[p][:, 0], ALU.subtract).then_inc(*st.sem("rest"))
                        V.tensor_tensor(hs[p][:, 1], h[p][:], hs[p][:, 0], ALU.subtract).then_inc(*st.sem("hs2"))
                        dve.wait_ge(*st.at("hs2", round=t))
                        V.tensor_tensor(hs[p][:, 2], rest[:], hs[p][:, 1], ALU.subtract).then_inc(*st.sem("hs3"))
                        for c in range(B):
                            dve.wait_ge(*st.at(f"score{c}", round=t))
                            V.tensor_reduce(ntop[:, c:c + 1], score[c], AX, ALU.max, negate=True).then_inc(*st.sem(f"top{c}"))
                        dve.wait_ge(*st.at("exp0", round=t))
                        weigh("z0", 0, 0)
                        weigh("r0", 1, 0)
                        dve.wait_ge(*st.at("gates", round=t))
                        V.tensor_scalar(rhh[:], G[:, 6:8], 0.5, None, ALU.mult).then_inc(*st.sem("rhh"))
                        dve.wait_ge(*st.at("exp1", round=t))
                        weigh("r1", 1, 1)
                        weigh("z1", 0, 1)
                        V.reciprocal(sinv[:], esum[:]).then_inc(*st.sem("sinv"))
                        dve.wait_ge(*st.at("rhh", round=t))
                        V.tensor_tensor(hb[:], rhh[:], G[:, 4:6], ALU.add).then_inc(*st.sem("hb"))
                        dve.wait_ge(*st.at("sinv", round=t))
                        for c in range(B):
                            fma(f"zr{c}", zr[:, c:4:2], mac[:, c:4:2], sinv[:, c:c + 1], G[:, c:4:2])
                        weigh("h0", 2, 0)
                        weigh("h1", 2, 1)
                        for c in range(B):
                            dve.wait_ge(*st.at(f"h{c}", round=t))
                            fma(f"in{c}", hin[:, c:c + 1], mac[:, 4 + c:5 + c], sinv[:, c:c + 1], hb[:, c:c + 1])
                        dve.wait_ge(*st.at("zr", round=t))
                        for c in range(B):
                            dve.wait_ge(*st.at(f"in{c}", round=t))
                            fma(f"ph{c}", pre_h[:, c:c + 1], tzr[:, 2 + c:3 + c], rhh[:, c:c + 1], hin[:, c:c + 1])
                        if t >= 2:
                            dve.wait_ge(*st.at("saved", round=t - 2))
                        V.tensor_scalar(omz[:], tzr[:, 0:2], -0.5, 0.5, ALU.mult, ALU.add).then_inc(*st.sem("omz"))
                        V.scalar_tensor_tensor(out=zh[:], in0=tzr[:, 0:2], scalar=1.0, in1=half_h[:], op0=ALU.add, op1=ALU.mult)\
                            .then_inc(*st.sem("zh"))
                        dve.wait_ge(*st.at("zh", round=t))
                        dve.wait_ge(*st.at("cand", round=t))
                        for c in range(B):
                            one = V.scalar_tensor_tensor(out=h[1 - p][:, c:c + 1], in0=hh[:, c:c + 1], scalar=omz[:, c:c + 1],
                                                         in1=zh[:, c:c + 1], op0=ALU.mult, op1=ALU.add)
                        one.then_inc(*st.sem("h"))
                    for u in range(UNROLL):
                        body(u, u % 2)

                @block.gpsimd
                def _(pool):
                    def body(t, p):
                        pool.wait_ge(*st.at("h", round=t))
                        at = k.x[:, :, bass.ds(j * UNROLL + t, 1)].rearrange("p b o -> p (b o)")
                        nc.gpsimd.tensor_tensor(at, at, h[1 - p][:], ALU.add).then_inc(*st.sem("saved"))
                    for u in range(UNROLL):
                        body(u, u % 2)
                    pool.wait_ge(*st.at("saved", round=UNROLL - 1))

            for sem in st.sems.values():
                nc.gpsimd.sem_clear(sem)
            nc.all_engine_barrier()


def attention(k, label, n_iter, HP, dh, src, kv, n_kv, w_dram, shared_kv=False, bias=None, w_fixed=None):
    nc, ps = k.nc, k.ps
    NKT = -(-n_kv // P)
    kw = min(P, n_kv)
    SCALE = 1.0 / math.sqrt(dh)
    units = [(c, i) for c in range(B) for i in range(HP)]
    U = len(units)
    KD = dh if shared_kv else P
    WC = P + 2 * KD + P
    RA, RB = 2, 3
    KH = 1 if shared_kv else HP
    with ExitStack() as ctx:
        def sb(name, shape, dt=F32):
            return ctx.enter_context(nc.sbuf_tensor(f"{label}_{name}", shape, dt))

        wb = [sb(f"w{i}", [P, WC]) for i in range(2)]
        qh = sb("qh", [P, B, HP, T])
        kh, ka = sb("kh", [P, B, KH, n_kv]), sb("ka", [P, B, KH, n_kv])
        va = sb("va", [P, B, KH, NKT, 2 * dh])
        ncol = sb("ncol", [P, U, TT])
        ex = sb("ex", [P, RB, T])
        rinv = sb("rinv", [P, T])
        o = sb("o", [P, B, T])
        A_T = [(u, t) for u in range(U) for t in range(TT)]
        B_T = [(u, t) for u in range(U) for t in range(NKT)]
        an = {x: n for n, x in enumerate(A_T)}
        bn = {x: n for n, x in enumerate(B_T)}

        order = [("a", 0, t) for t in range(TT)]
        late = []
        for u in range(U):
            order.append(("r", u, 0))
            for t in range(max(TT, NKT)):
                if t < TT and u + 1 < U:
                    order.append(("a", u + 1, t))
                if t < NKT:
                    order.append(("b", u, t))
                order += late
                late = []
                if t < NKT:
                    late = [("v", u, t)]
                    if t == NKT - 1 and u % HP == HP - 1:
                        late.append(("w", u // HP, 0))
        order += late
        pe_steps = ["q0", "k0", "v0", "q1", "k1", "v1"]
        act_steps, dve_steps = ["qc0", "qc1"], ["kc0", "vc0", "kc1", "vc1"]
        for what, u, t in order:
            if what == "a":
                pe_steps += [f"a{u}.{t}"]
                dve_steps += [f"m{u}.{t}"]
            elif what == "r":
                pe_steps += [f"r{u}"]
                dve_steps += [f"rc{u}"]
            elif what == "b":
                pe_steps += [f"b{u}.{t}"]
                act_steps += [f"e{u}.{t}"]
            elif what == "v":
                pe_steps += [f"v{u}.{t}"]
                if t == NKT - 1:
                    act_steps += [f"ln{u}", f"inv{u}"]
                    dve_steps += [f"o{u}"]
            else:
                pe_steps += [f"w{u}"]
                dve_steps += [f"res{u}"]
        st = Steps(k, label, 1, pe=" ".join(pe_steps), act=" ".join(act_steps), dve=" ".join(dve_steps),
                   pool="ka0 ka1")
        landed = [k.semaphore(f"{label}_landed{i}") for i in range(2)]
        primed = k.semaphore(f"{label}_primed")
        block = ctx.enter_context(nc.Block())

        def rounds(eng, body):
            lead = min(n_iter, 2)
            for g in range(lead):
                body(g, g % 2, g, 0)
            if n_iter > lead:
                with eng.Fori(0, (n_iter - lead) // 2) as j:
                    for u in range(2):
                        body(lead + u + 2 * j, u, 2, 1 + j)

        @block.sync
        def _(sp):
            def load(g, b, lead, n):
                if lead == 2:
                    sp.wait_ge(*st.at("w1", round=g - 2))
                sp.dma_start(wb[b][:], w_dram[bass.ds(g, 1)].rearrange("g p n -> (g p) n") if lead == 2 else w_dram[g])\
                    .then_inc(landed[b], 16)
            rounds(sp, load)
            for b in range(min(2, n_iter)):
                sp.wait_ge(landed[b], 16 * ((n_iter + 1 - b) // 2))

        @block.gpsimd
        def _(pool):
            G = nc.gpsimd
            G.memset(qh[:], 0.0).then_inc(primed, 1)
            G.memset(kh[:], 0.0).then_inc(primed, 1)
            G.memset(ka[:], 0.0).then_inc(primed, 1)
            G.memset(va[:], 1.0).then_inc(primed, 1)
            pool.wait_ge(primed, 4)
            G.memset(kh[dh:dh + 1], 1.0).then_inc(primed, 1)

            def body(g, b, lead, n):
                for c in range(B):
                    if lead:
                        pool.wait_ge(*st.at(f"a{(c + 1) * HP - 1}.{TT - 1}", round=g - 1))
                    pool.wait_ge(*st.at(f"kc{c}", round=g))
                    G.tensor_tensor(ka[0:dh, c], kh[0:dh, c], k.ones[0:dh, 0:1].unsqueeze(2).broadcast_to([dh, KH, n_kv]), ALU.mult).then_inc(*st.sem(f"ka{c}"))
            rounds(pool, body)

        @block.tensor
        def _(pe):
            M = nc.tensor.matmul

            def body(g, b, lead, n):
                W = wb[b]
                pe.wait_ge(landed[b], 16 * (n + 1))
                if lead:
                    pe.wait_ge(*st.at("res1", round=g - 1))
                for c in range(B):
                    M(ps[:, 3 * c], W[:, 0:P], src[:, c], start=True, stop=True).then_inc(*st.sem(f"q{c}"))
                    M(ps[0:KD, 3 * c + 1, 0:n_kv], W[:, P:P + KD], kv[:, c], start=True, stop=True)\
                        .then_inc(*st.sem(f"k{c}"))
                    for t in range(NKT):
                        mm = M(ps[0:kw, 3 * c + 2, t * KD:(t + 1) * KD], kv[:, c, t * P:t * P + kw],
                               W[:, P + KD:P + 2 * KD], start=True, stop=True)
                    mm.then_inc(*st.sem(f"v{c}"))
                for what, u, t in order:
                    c, i = units[u] if what != "w" else (u, 0)
                    ki = 0 if shared_kv else i
                    if what == "a":
                        if u == 0 and t == 0:
                            pe.wait_ge(*st.at("qc1", round=g))
                            pe.wait_ge(*st.at("vc1", round=g))
                        if t == 0:
                            pe.wait_ge(*st.at(f"ka{c}", round=g))
                        m = an[u, t]
                        if m >= RA:
                            pe.wait_ge(*st.at("m{}.{}".format(*A_T[m - RA]), round=g))
                        M(ps[:, m % RA, 0:n_kv], qh[:, c, i, t * P:(t + 1) * P], ka[:, c, ki], start=True, stop=True)\
                            .then_inc(*st.sem(f"a{u}.{t}"))
                    elif what == "r":
                        pe.wait_ge(*st.at(f"m{u}.{TT - 1}", round=g))
                        for q in range(TT):
                            mm = M(ps[dh:dh + 1, 6, q * P:(q + 1) * P], ncol[:, u, q:q + 1], k.ident[:],
                                   start=True, stop=True)
                        mm.then_inc(*st.sem(f"r{u}"))
                    elif what == "b":
                        if t == 0:
                            pe.wait_ge(*st.at(f"rc{u}", round=g))
                        m = bn[u, t]
                        if m >= RB:
                            pe.wait_ge(*st.at("e{}.{}".format(*B_T[m - RB]), round=g))
                        M(ps[0:kw, 2 + m % RB], kh[:, c, ki, t * P:t * P + kw], qh[:, c, i], start=True, stop=True)\
                            .then_inc(*st.sem(f"b{u}.{t}"))
                    elif what == "v":
                        if t == 0 and u > 0:
                            pe.wait_ge(*st.at(f"o{u - 1}", round=g))
                        pe.wait_ge(*st.at(f"e{u}.{t}", round=g))
                        M(ps[0:2 * dh, 5], va[0:kw, c, ki, t], ex[0:kw, bn[u, t] % RB],
                          start=(t == 0), stop=(t == NKT - 1)).then_inc(*st.sem(f"v{u}.{t}"))
                    else:
                        pe.wait_ge(*st.at(f"o{(c + 1) * HP - 1}", round=g))
                        M(ps[:, 7], W[:, P + 2 * KD:], o[:, c], start=True, stop=True).then_inc(*st.sem(f"w{c}"))
            rounds(pe, body)

        @block.scalar
        def _(act):
            act.wait_ge(primed, 5)
            nc.scalar.preload_act_table_set("natural_log_exp_and_others")

            def body(g, b, lead, n):
                for c in range(B):
                    act.wait_ge(*st.at(f"q{c}", round=g))
                    for i in range(HP):
                        ins = nc.scalar.copy(qh[0:dh, c, i], ps[i * dh:(i + 1) * dh, 3 * c])
                    ins.then_inc(*st.sem(f"qc{c}"))
                for what, u, t in order:
                    if what == "b":
                        m = bn[u, t]
                        act.wait_ge(*st.at(f"b{u}.{t}", round=g))
                        if m >= RB:
                            act.wait_ge(*st.at("v{}.{}".format(*B_T[m - RB]), round=g))
                        nc.scalar.activation(ex[0:kw, m % RB], ps[0:kw, 2 + m % RB], ACT.Exp, scale=SCALE)\
                            .then_inc(*st.sem(f"e{u}.{t}"))
                    elif what == "v" and t == NKT - 1:
                        act.wait_ge(*st.at(f"v{u}.{t}", round=g))
                        nc.scalar.activation(rinv[0:dh], ps[dh:2 * dh, 5], ACT.Ln).then_inc(*st.sem(f"ln{u}"))
                        act.wait_ge(*st.at(f"ln{u}", round=g))
                        nc.scalar.activation(rinv[0:dh], rinv[0:dh], ACT.Exp, scale=-1.0).then_inc(*st.sem(f"inv{u}"))
            rounds(act, body)

        @block.vector
        def _(dve):
            V = nc.vector
            dve.wait_ge(primed, 5)

            def body(g, b, lead, n):
                for c in range(B):
                    dve.wait_ge(*st.at(f"k{c}", round=g))
                    if lead:
                        dve.wait_ge(*st.at(f"ka{c}", round=g - 1))
                    for i in range(KH):
                        ins = V.tensor_copy(kh[0:dh, c, i], ps[i * dh:(i + 1) * dh, 3 * c + 1, 0:n_kv])
                    ins.then_inc(*st.sem(f"kc{c}"))
                    dve.wait_ge(*st.at(f"v{c}", round=g))
                    for i in range(KH):
                        ins = V.tensor_copy(va[0:kw, c, i, :, 0:dh],
                                            ps[0:kw, 3 * c + 2, 0:NKT * KD].rearrange("p (t n) -> p t n", t=NKT)
                                            [:, :, i * dh:(i + 1) * dh])
                    ins.then_inc(*st.sem(f"vc{c}"))
                for what, u, t in order:
                    c, i = units[u] if what != "w" else (u, 0)
                    if what == "b":
                        continue
                    if what == "a":
                        dve.wait_ge(*st.at(f"a{u}.{t}", round=g))
                        V.tensor_reduce(ncol[:, u, t:t + 1], ps[:, an[u, t] % RA, 0:n_kv], AX, ALU.max, negate=True)\
                            .then_inc(*st.sem(f"m{u}.{t}"))
                    elif what == "r":
                        dve.wait_ge(*st.at(f"r{u}", round=g))
                        V.tensor_copy(qh[dh:dh + 1, c, i], ps[dh:dh + 1, 6]).then_inc(*st.sem(f"rc{u}"))
                    elif what == "v":
                        if t < NKT - 1:
                            continue
                        dve.wait_ge(*st.at(f"inv{u}", round=g))
                        if i == 0 and lead:
                            dve.wait_ge(*st.at(f"w{c}", round=g - 1))
                        V.tensor_tensor(o[i * dh:(i + 1) * dh, c], rinv[0:dh], ps[0:dh, 5], ALU.mult)\
                            .then_inc(*st.sem(f"o{u}"))
                    else:
                        dve.wait_ge(*st.at(f"w{c}", round=g))
                        if lead:
                            dve.wait_ge(*st.at(f"res{c}", round=g - 1))
                            V.tensor_tensor(k.y[:, c], k.y[:, c], ps[:, 7], ALU.add).then_inc(*st.sem(f"res{c}"))
                        elif bias is not None:
                            V.scalar_tensor_tensor(out=k.y[:, c], in0=ps[:, 7], scalar=bias, in1=k.y[:, c],
                                                   op0=ALU.add, op1=ALU.add).then_inc(*st.sem(f"res{c}"))
                        else:
                            V.tensor_tensor(k.y[:, c], k.y[:, c], ps[:, 7], ALU.add).then_inc(*st.sem(f"res{c}"))
            rounds(dve, body)
            dve.wait_ge(*st.at("res1", round=n_iter - 1))


def copy_stage(k, label, dst, src):
    nc = k.nc
    with ExitStack() as ctx:
        copied = k.semaphore(f"{label}_copied")
        block = ctx.enter_context(nc.Block())

        @block.vector
        def _(dve):
            nc.vector.tensor_copy(dst[:], src[:]).then_inc(copied, 1)
            dve.wait_ge(copied, 1)


def add_stage(k, label, dst, src):
    nc = k.nc
    with ExitStack() as ctx:
        added = k.semaphore(f"{label}_added")
        block = ctx.enter_context(nc.Block())

        @block.vector
        def _(dve):
            nc.vector.tensor_tensor(dst[:], dst[:], src[:], ALU.add).then_inc(added, 1)
            dve.wait_ge(added, 1)


def gains_stage(k, label, w, b, n, gains):
    nc, ps = k.nc, k.ps
    with ExitStack() as ctx:
        st = Steps(k, label, 1, pe="emb", dve="bias one")
        block = ctx.enter_context(nc.Block())

        @block.tensor
        def _(pe):
            for j in range(2 * n):
                mm = nc.tensor.matmul(ps[:, 0, B * j:B * j + B], w[:, j * D:(j + 1) * D], k.cond[:], start=True, stop=True)
            mm.then_inc(*st.sem("emb"))

        @block.vector
        def _(dve):
            dve.wait_ge(*st.at("emb"))
            nc.vector.tensor_tensor(gains[:], ps[:, 0, 0:2 * n * B].rearrange("p (j b) -> p j b", b=B),
                                    b.unsqueeze(2).broadcast_to([P, 2 * n, B]), ALU.add).then_inc(*st.sem("bias"))
            dve.wait_ge(*st.at("bias"))
            nc.vector.tensor_scalar(gains[:, 0:2 * n:2], gains[:, 0:2 * n:2], 1.0, None, ALU.add).then_inc(*st.sem("one"))
            dve.wait_ge(*st.at("one"))


def adaln_stage(k, label, src, dst, gains, j):
    nc = k.nc
    with ExitStack() as ctx:
        st = Steps(k, label, 2, pe=LN_PE.format("x"), act=LN_ACT.format("x"), dve=LNA_DVE.format("x"))
        block = ctx.enter_context(nc.Block())

        @block.tensor
        def _(pe):
            ln_pe(k, pe, st, "x", lambda c: src[:, c], T, (0, 4), 2, lambda c: None)

        @block.scalar
        def _(act):
            ln_act(k, act, st, "x", T, (0, 4), 2)

        @block.vector
        def _(dve):
            ln_dve(k, dve, st, "x", lambda c: src[:, c], lambda c: dst[:, c], T, (0, 4), 2,
                   affine=lambda c: (gains[:, 2 * j, c:c + 1], gains[:, 2 * j + 1, c:c + 1]))
            for c in range(B):
                dve.wait_ge(*st.at("x.affine", c))


def glu_stage(k, label, src, w):
    nc, ps = k.nc, k.ps
    NB = DFF2 // P
    with ExitStack() as ctx:
        gl = ctx.enter_context(nc.sbuf_tensor(label + "_gelu", [P, B, T], F32))
        u = ctx.enter_context(nc.sbuf_tensor(label + "_u", [P, B, NB, T], F32))
        st = Steps(k, label, 2, pe="au0 au1 au2 au3 out", act="g0 g1 g2 g3", dve="u0 u1 u2 u3 res")
        block = ctx.enter_context(nc.Block())

        @block.tensor
        def _(pe):
            for j in range(NB):
                for c in range(B):
                    if j:
                        pe.wait_ge(*st.at(f"u{j - 1}", c))
                    nc.tensor.matmul(ps[:, 3 * c], w["ff_w1"][:, j * P:(j + 1) * P], src[:, c], start=True, stop=True)
                    nc.tensor.matmul(ps[:, 3 * c + 1], w["ff_w1"][:, DFF2 + j * P:DFF2 + (j + 1) * P], src[:, c],
                                     start=True, stop=True).then_inc(*st.sem(f"au{j}", c))
            for c in range(B):
                pe.wait_ge(*st.at(f"u{NB - 1}", c))
                for j in range(NB):
                    mm = nc.tensor.matmul(ps[:, 3 * c + 2], w["ff_w2"][:, j * D:(j + 1) * D], u[:, c, j],
                                          start=(j == 0), stop=(j == NB - 1))
                mm.then_inc(*st.sem("out", c))

        @block.scalar
        def _(act):
            for j in range(NB):
                for c in range(B):
                    act.wait_ge(*st.at(f"au{j}", c))
                    if j:
                        act.wait_ge(*st.at(f"u{j - 1}", c))
                    nc.scalar.activation(gl[:, c], ps[:, 3 * c + 1], ACT.Gelu, bias=w["ff_b1"][:, NB + j:NB + j + 1])\
                        .then_inc(*st.sem(f"g{j}", c))

        @block.vector
        def _(dve):
            for j in range(NB):
                for c in range(B):
                    dve.wait_ge(*st.at(f"g{j}", c))
                    nc.vector.scalar_tensor_tensor(out=u[:, c, j], in0=ps[:, 3 * c], scalar=w["ff_b1"][:, j:j + 1],
                                                   in1=gl[:, c], op0=ALU.add, op1=ALU.mult).then_inc(*st.sem(f"u{j}", c))
            for c in range(B):
                dve.wait_ge(*st.at("out", c))
                nc.vector.scalar_tensor_tensor(out=k.y[:, c], in0=ps[:, 3 * c + 2], scalar=w["ff_b2"], in1=k.y[:, c],
                                               op0=ALU.add, op1=ALU.add).then_inc(*st.sem("res", c))
            for c in range(B):
                dve.wait_ge(*st.at("res", c))


def transformer2_stage(k, w):
    nc = k.nc
    with ExitStack() as ctx:
        gains = ctx.enter_context(nc.sbuf_tensor("t2_gains", [P, 6, B], F32))
        hn = ctx.enter_context(nc.sbuf_tensor("t2_h", [P, B, T], F32))
        gains_stage(k, "t2g", w["norm_w"], w["norm_b"], 3, gains)
        norm_stage(k, "t2n")
        copy_stage(k, "t2c", k.y, k.xn)
        adaln_stage(k, "t2a", k.y, hn, gains, 0)
        attention(k, "t2s", H2 // 2, 2, DH2, hn, hn, T, k.dram["attn1"], bias=w["attn1_bo"])
        adaln_stage(k, "t2b", k.y, hn, gains, 1)
        attention(k, "t2x", H2 // 2, 2, DH2, hn, k.ctxT, S, k.dram["attn2"], bias=w["attn2_bo"])
        adaln_stage(k, "t2d", k.y, hn, gains, 2)
        glu_stage(k, "t2f", hn, w)
        add_stage(k, "t2r", k.x, k.y)


def ternary_stage(k, w):
    nc, ps = k.nc, k.ps
    NB = HID5 // P
    ROUND = 1.5 * 2.0 ** 23
    groups = [("fc", j, w["w_fc"][:, j * D:(j + 1) * D], D) for j in range(NB)] + [("proj", 0, w["w_proj"], HID5)]
    G = len(groups)
    with ExitStack() as ctx:
        def sb(name, shape, dt=F32):
            return ctx.enter_context(nc.sbuf_tensor("t5_" + name, shape, dt))

        absw, t1, wq = sb("absw", [P, HID5]), sb("t1", [P, G, HID5]), sb("wq", [P, G, HID5])
        asum, scale, inv = sb("asum", [P, G]), sb("scale", [P, G]), sb("inv", [P, G])
        fcT, projT = sb("fcT", [P, NB, P]), sb("projT", [P, NB, P])
        low = sb("low", [RANK5, B, 2, T])
        h, h2 = sb("h", [P, B, NB, T]), sb("h2", [P, B, NB, T])
        prep = Steps(k, "t5p", 1, pe="fcT projT", act=" ".join(f"abs{g}" for g in range(G)),
                     dve="mean mean2 scale inv " + " ".join(f"r{g} d{g} c{g} q{g} s{g}" for g in range(G)) + " scaled fcTs projTs")
        st = Steps(k, "t5", 2, pe="v b h0 h1 h2 h3 out", act="relu0 relu1 relu2 relu3",
                   dve="vs bs sq0 sq1 sq2 sq3 res")
        block = ctx.enter_context(nc.Block())

        @block.scalar
        def _(act):
            for g, (_, _, a, n) in enumerate(groups):
                if g:
                    act.wait_ge(*prep.at(f"abs{g - 1}"))
                nc.scalar.activation(absw[:, 0:n], a, ACT.Abs, accum_out=asum[:, g:g + 1]).then_inc(*prep.sem(f"abs{g}"))
            for j in range(NB):
                for c in range(B):
                    act.wait_ge(*st.at(f"h{j}", c))
                    nc.scalar.activation(h[:, c, j], ps[:, 3 * c + j % 2], ACT.Relu).then_inc(*st.sem(f"relu{j}", c))

        @block.vector
        def _(dve):
            V = nc.vector
            dve.wait_ge(*prep.at(f"abs{G - 1}"))
            V.tensor_scalar(scale[:, 0:NB], asum[:, 0:NB], 1.0 / D, None, ALU.mult).then_inc(*prep.sem("mean"))
            dve.wait_ge(*prep.at("mean"))
            V.tensor_scalar(scale[:, NB:G], asum[:, NB:G], 1.0 / HID5, None, ALU.mult).then_inc(*prep.sem("mean2"))
            dve.wait_ge(*prep.at("mean2"))
            V.tensor_scalar(scale[:], scale[:], 1e-5, None, ALU.max).then_inc(*prep.sem("scale"))
            dve.wait_ge(*prep.at("scale"))
            V.reciprocal(inv[:], scale[:]).then_inc(*prep.sem("inv"))
            dve.wait_ge(*prep.at("inv"))
            for g, (_, _, a, n) in enumerate(groups):
                V.tensor_scalar(t1[:, g, 0:n], a, inv[:, g:g + 1], ROUND, ALU.mult, ALU.add).then_inc(*prep.sem(f"r{g}"))
                dve.wait_ge(*prep.at(f"r{g}"))
                V.tensor_scalar(t1[:, g, 0:n], t1[:, g, 0:n], -ROUND, None, ALU.add).then_inc(*prep.sem(f"d{g}"))
                dve.wait_ge(*prep.at(f"d{g}"))
                V.tensor_scalar(t1[:, g, 0:n], t1[:, g, 0:n], 1.0, -1.0, ALU.min, ALU.max).then_inc(*prep.sem(f"c{g}"))
                dve.wait_ge(*prep.at(f"c{g}"))
                V.tensor_tensor(wq[:, g, 0:n], t1[:, g, 0:n], a, ALU.subtract).then_inc(*prep.sem(f"q{g}"))
                dve.wait_ge(*prep.at(f"q{g}"))
                V.tensor_tensor(wq[:, g, 0:n], wq[:, g, 0:n], a, ALU.add).then_inc(*prep.sem(f"s{g}"))
                dve.wait_ge(*prep.at(f"s{g}"))
            for g, (_, _, a, n) in enumerate(groups):
                ins = V.tensor_scalar(wq[:, g, 0:n], wq[:, g, 0:n], scale[:, g:g + 1], None, ALU.mult)
            ins.then_inc(*prep.sem("scaled"))
            dve.wait_ge(*prep.at("fcT"))
            V.tensor_copy(fcT[:].rearrange("p j n -> p (j n)"), ps[:, 6]).then_inc(*prep.sem("fcTs"))
            dve.wait_ge(*prep.at("projT"))
            V.tensor_copy(projT[:].rearrange("p j n -> p (j n)"), ps[:, 7]).then_inc(*prep.sem("projTs"))
            for c in range(B):
                dve.wait_ge(*st.at("v", c))
                V.tensor_copy(low[:, c, 0], ps[0:RANK5, 3 * c + 2]).then_inc(*st.sem("vs", c))
            for c in range(B):
                dve.wait_ge(*st.at("b", c))
                V.tensor_scalar(low[:, c, 1], ps[0:RANK5, 3 * c + 2], w["gate"][0:RANK5], None, ALU.mult)\
                    .then_inc(*st.sem("bs", c))
            for j in range(NB):
                for c in range(B):
                    dve.wait_ge(*st.at(f"relu{j}", c))
                    V.tensor_tensor(h2[:, c, j], h[:, c, j], h[:, c, j], ALU.mult).then_inc(*st.sem(f"sq{j}", c))
            for c in range(B):
                dve.wait_ge(*st.at("out", c))
                V.tensor_tensor(k.x[:, c], k.x[:, c], ps[:, 3 * c + 2], ALU.add).then_inc(*st.sem("res", c))
            for c in range(B):
                dve.wait_ge(*st.at("res", c))

        @block.tensor
        def _(pe):
            M = nc.tensor.matmul
            for c in range(B):
                M(ps[0:RANK5, 3 * c + 2], w["vT"], k.xn[:, c], start=True, stop=True).then_inc(*st.sem("v", c))
            pe.wait_ge(*prep.at("scaled"))
            for j in range(NB):
                mm = nc.tensor.transpose(ps[:, 6, j * P:(j + 1) * P], wq[:, j, 0:D], k.ident[:])
            mm.then_inc(*prep.sem("fcT"))
            for j in range(NB):
                mm = nc.tensor.transpose(ps[:, 7, j * P:(j + 1) * P], wq[:, NB, j * P:(j + 1) * P], k.ident[:])
            mm.then_inc(*prep.sem("projT"))
            for c in range(B):
                pe.wait_ge(*st.at("vs", c))
                M(ps[0:RANK5, 3 * c + 2], w["fastT"], low[:, c, 0], start=True, stop=True).then_inc(*st.sem("b", c))
            pe.wait_ge(*prep.at("projTs"))
            for j in range(NB):
                for c in range(B):
                    if j == 0:
                        pe.wait_ge(*st.at("bs", c))
                    if j >= 2:
                        pe.wait_ge(*st.at(f"relu{j - 2}", c))
                    M(ps[:, 3 * c + j % 2], fcT[:, j], k.xn[:, c], start=True, stop=False)
                    M(ps[:, 3 * c + j % 2], w["uT"][:, j * P:(j + 1) * P], low[:, c, 1], start=False, stop=True)\
                        .then_inc(*st.sem(f"h{j}", c))
            for c in range(B):
                for j in range(NB):
                    pe.wait_ge(*st.at(f"sq{j}", c))
                    mm = M(ps[:, 3 * c + 2], projT[:, j], h2[:, c, j], start=(j == 0), stop=(j == NB - 1))
                mm.then_inc(*st.sem("out", c))


PAIRS = [(i, j) for j in range(3) for i in range(3)]
MASK_ROW = DH3 * len(PAIRS)
SHIFT_ROW = 96
MASKED = -1e30
STACK_LOADS = 3 + 9


def transformer3_stage(k, w):
    nc, ps = k.nc, k.ps
    SCALE = 1.0 / math.sqrt(DH3)
    G = H3 // 4
    NB = DFF3 // P
    assert NB == G
    with ExitStack() as ctx:
        def sb(name, shape, dt=F32):
            return ctx.enter_context(nc.sbuf_tensor("t6_" + name, shape, dt))

        gains = sb("gains", [P, 6 * NL3, B])
        with ExitStack() as nctx:
            whole, norms = k.weights(nctx, "p6n")
            load_stage(k, whole, "p6n")
            gains_stage(k, "t6g", norms["norm_w"], norms["norm_b"], 3 * NL3, gains)
        hn = k.xn
        turn = nc.dram_tensor("t6_turn", (B, 2, 3, P, T), BF16).ap()
        wa, wx, wf = sb("wa", [P, 9 * P]), sb("wx", [P, 9 * P]), sb("wf", [P, 2 * DFF3 + NB + 1])
        qst, kst = sb("qst", [P, B, H3, T], BF16), sb("kst", [P, B, H3, T], BF16)
        kxt = sb("kxt", [P, B, H3, S], BF16)
        va, vx = sb("va", [P, B, TT, H3, 32]), sb("vx", [P, B, 1, H3, 32])
        t1, t2, rot = sb("t1", [P, 2, T]), sb("t2", [P, 2, T]), sb("rot", [P, 2, T])
        part = sb("part", [P, B, 2, 3, T], BF16)
        ncol = sb("ncol", [P, B, TT, H3])
        nhi, nlo = sb("nhi", [P, B, TT, H3], BF16), sb("nlo", [P, B, TT, H3], BF16)
        nrow = sb("nrow", [H3, B, 2, T], BF16)
        identb = sb("identb", [P, P], BF16)
        ex = sb("ex", [P, 4, 2, T])
        og, rs, on = sb("og", [P, 2, T]), sb("rs", [P, 2, T]), sb("on", [P, B, G, T])
        one16 = sb("one16", [H3, T], BF16)
        mraw, mx = sb("mraw", [H3, B, T + S], U8), sb("mx", [H3, B, T + S], BF16)
        hid = on

        with ExitStack() as pctx:
            dn = k.semaphore("t6_fill")
            ones_in = k.semaphore("t6_ones_in")
            raw_in = k.semaphore("t6_mask_in")
            dv = k.semaphore("t6_dve_fill")
            rows_in = k.semaphore("t6_rows_in")
            block = pctx.enter_context(nc.Block())

            @block.gpsimd
            def _(pool):
                for a in (qst, kst, kxt, va, vx):
                    nc.gpsimd.memset(a[:], 0.0).then_inc(dn, 1)
                nc.gpsimd.memset(one16[:], 1.0).then_inc(dn, 1)
                for n, part_of_ones in enumerate((kst[SHIFT_ROW:SHIFT_ROW + 2], kxt[SHIFT_ROW:SHIFT_ROW + 2],
                                                  va[:, :, :, :, DH3:DH3 + 1], vx[:, :, :, :, DH3:DH3 + 1])):
                    pool.wait_ge(dn, 6 + n)
                    nc.gpsimd.memset(part_of_ones, 1.0).then_inc(dn, 1)
                pool.wait_ge(dn, 10)

            @block.vector
            def _(dve):
                nc.vector.tensor_copy(identb[:], k.ident[:]).then_inc(dv, 1)
                dve.wait_ge(raw_in, 16)
                nc.vector.tensor_scalar(mx[:], mraw[:], MASKED, None, ALU.mult).then_inc(dv, 1)
                dve.wait_ge(dv, 2)

            @block.sync
            def _(sp):
                sp.dma_start(mraw[:], k.dram["masks"]).then_inc(raw_in, 16)
                sp.wait_ge(dn, 10)
                sp.wait_ge(dv, 2)
                for c in range(B):
                    sp.dma_start(qst[MASK_ROW:MASK_ROW + 1, c], one16[:]).then_inc(rows_in, 16)
                    sp.dma_start(kst[MASK_ROW:MASK_ROW + 1, c], mx[:, c, 0:T]).then_inc(rows_in, 16)
                    sp.dma_start(kxt[MASK_ROW:MASK_ROW + 1, c], mx[:, c, T:T + S]).then_inc(rows_in, 16)
                sp.wait_ge(rows_in, 16 * 6)

        PARTS = {"s": (wa, None, kst, va, T), "x": (wx, k.ctxT, kxt, vx, S)}
        BB = 4
        AB, VB, MB = 4, 6, 7

        tiles_a = {"s": TT, "x": 1}

        def blocks(pf):
            return [(g, t) for g in range(G) for t in range(-(-PARTS[pf][4] // P))]

        def order(pf):
            a0, a1 = ([("a", c, (h, t)) for h in range(H3) for t in range(tiles_a[pf])] for c in range(B))
            nb = len(blocks(pf))
            run = a0 + [("t", 0, 0)]
            per = len(a1) // nb
            last = [t == -(-PARTS[pf][4] // P) - 1 for _, t in blocks(pf)]

            def block_run(c, between):
                part = []
                for n in range(nb + 2):
                    if n < nb:
                        some = between[n * per:(n + 1) * per]
                        part += some[:per // 2] + [("b0", c, n)] + some[per // 2:] + [("b1", c, n)]
                    if 1 <= n <= nb:
                        part += [("o", c, n - 1)]
                    if n >= 2 and last[n - 2]:
                        part += [("d", c, blocks(pf)[n - 2][0])]
                return part

            run += block_run(0, a1) + [("w", 0, 0), ("t", 1, 0)]
            run += block_run(1, []) + [("w", 1, 0)]
            return run

        pe_s, act_s, dve_s, pool_s = [], [], [], []
        for pf in "sx":
            nkt = -(-PARTS[pf][4] // P)
            for c in range(B):
                pe_s += [f"{pf}q{c}", f"{pf}k{c}", f"{pf}v{c}"]
                dve_s += [f"{pf}{n}{c}" for n in ("qa", "qb", "qr", "q1", "qd", "q2", "q3", "ka", "kb", "vc")]
                pool_s += [f"{pf}{n}{c}" for n in ("kr", "k1", "kd", "k2", "k3")]
            for what, c, n in order(pf):
                if what == "a":
                    pe_s += ["{}a{}.{}.{}".format(pf, c, *n)]
                    dve_s += ["{}m{}.{}.{}".format(pf, c, *n)]
                elif what == "t":
                    pe_s += [f"{pf}thi{c}", f"{pf}tlo{c}"]
                    dve_s += [f"{pf}hi{c}", f"{pf}lo{c}", f"{pf}rhi{c}", f"{pf}rlo{c}"]
                elif what in ("b0", "b1"):
                    pe_s += [f"{pf}b{c}.{n}.{what[1]}"]
                    act_s += [f"{pf}e{c}.{n}.{what[1]}"]
                elif what == "o":
                    pe_s += [f"{pf}v{c}.{n}"]
                    if blocks(pf)[n][1] == nkt - 1:
                        dve_s += [f"{pf}og{c}.{blocks(pf)[n][0]}"]
                elif what == "d":
                    pe_s += [f"{pf}sum{c}.{n}"]
                    act_s += [f"{pf}ln{c}.{n}", f"{pf}inv{c}.{n}"]
                    dve_s += [f"{pf}on{c}.{n}"]
                else:
                    pe_s += [f"{pf}w{c}"]
                    dve_s += [f"{pf}res{c}"]
        for j in range(NB):
            for c in range(B):
                pe_s += [f"f{c}.{j}"]
                act_s += [f"g{c}.{j}"]
        for c in range(B):
            pe_s += [f"fo{c}"]
            dve_s += [f"fres{c}"]
        st = Steps(k, "t6", 1, lead=1, pe=" ".join(pe_s), act=" ".join(act_s), dve=" ".join(dve_s),
                   pool=" ".join(pool_s))
        ln = Steps(k, "t6n", 2, lead=1, pe=" ".join(LN_PE.format(n) for n in "sxf"),
                   act=" ".join(LN_ACT.format(n) for n in "sxf"), dve=" ".join(LNA_DVE.format(n) for n in "sxf"))
        landed = {n: k.semaphore(f"t6_{n}_landed") for n in ("wa", "wx", "wf")}
        stacked = {(pf, c): k.semaphore(f"t6_{pf}_stacked{c}") for pf in "sx" for c in range(B)}
        shifted = {(pf, c): k.semaphore(f"t6_{pf}_shifted{c}") for pf in "sx" for c in range(B)}
        turn_in = {(c, q): k.semaphore(f"t6_turn_in{c}{q}") for c in range(B) for q in range(2)}
        block = ctx.enter_context(nc.Block())

        @block.sync
        def _(sp):
            with sp.Fori(0, NL3) as l:
                turned = {key: 0 for key in turn_in}
                def weights(name, dst, last):
                    sp.wait_ge(*last)
                    src = k.dram["t6_" + name][bass.ds(l, 1)].rearrange("g p n -> (g p) n")
                    sp.dma_start(dst[:], src).then_inc(landed[name], 16)

                weights("wa", wa, st.at("sw1", round=l - 1))
                weights("wx", wx, st.at("xw1", round=l - 1))
                weights("wf", wf, st.at("fres1", round=l - 1))
                for pf in "sx":
                    kt, n_kv = PARTS[pf][2], PARTS[pf][4]
                    for c in range(B):
                        for q, step in enumerate(("q3", "k3")):
                            n = (T, n_kv)[q]
                            sp.wait_ge(*st.at(f"{pf}{step}{c}", round=l))
                            turned[c, q] += 1
                            sp.dma_start(turn[c, q, :, :, 0:n].rearrange("i p n -> p i n"), part[:, c, q, :, 0:n])\
                                .then_inc(turn_in[c, q], 16)
                            sp.wait_ge(turn_in[c, q], l * 32 + 16 * turned[c, q])
                            for j in range(3):
                                if q == 0:
                                    sp.dma_start(qst[24 * j:24 * j + 24, c],
                                                 turn[c, q].rearrange("i (d h) n -> (i d) h n", d=DH3)).then_inc(stacked[pf, c], 16)
                                    continue
                                for i in range(3):
                                    p = 3 * j + i
                                    sp.dma_start(kt[p * DH3:(p + 1) * DH3, c],
                                                 turn[c, q, j, :, 0:n].rearrange("(d h) n -> d h n", d=DH3))\
                                        .then_inc(stacked[pf, c], 16)
                    for c in range(B):
                        sp.wait_ge(*st.at(f"{pf}rlo{c}", round=l))
                        for i in range(2):
                            sp.dma_start(qst[SHIFT_ROW + i:SHIFT_ROW + i + 1, c], nrow[:, c, i]).then_inc(shifted[pf, c], 16)
            for n in ("wa", "wx", "wf"):
                sp.wait_ge(landed[n], 16 * NL3)
            for key in turn_in:
                sp.wait_ge(turn_in[key], 16 * 2 * NL3)
            for key in stacked:
                sp.wait_ge(stacked[key], 16 * STACK_LOADS * NL3)
                sp.wait_ge(shifted[key], 16 * 2 * NL3)

        @block.tensor
        def _(pe):
            M = nc.tensor.matmul
            st.prime(pe, "pe")
            ln.prime(pe, "pe")
            with pe.Fori(0, NL3) as l:
                for pf in "sx":
                    W, kv, kt, vt, n_kv = PARTS[pf]
                    nkt, kw = -(-n_kv // P), min(P, n_kv)
                    last = "fres" if pf == "s" else "sres"
                    ln_pe(k, pe, ln, pf, lambda c: k.y[:, c], T, (AB, AB + 1), 2,
                          lambda c: pe.wait_ge(*st.at(f"{last}{c}", round=l - 1 if pf == "s" else l)), l)
                    pe.wait_ge(landed["w" + ("a" if pf == "s" else "x")], 16 * (l + 1))
                    for c in range(B):
                        pe.wait_ge(*ln.at(pf + ".affine", c, l))
                        if c:
                            pe.wait_ge(*st.at(f"{pf}vc0", round=l))
                        M(ps[:, 0], W[:, 0:P], hn[:, c], start=True, stop=True)
                        M(ps[:, 1], W[:, P:2 * P], hn[:, c], start=True, stop=True).then_inc(*st.sem(f"{pf}q{c}"))
                        src = hn[:, c] if kv is None else kv[:, c]
                        M(ps[:, 2, 0:n_kv], W[:, 2 * P:3 * P], src, start=True, stop=True)
                        M(ps[:, 3, 0:n_kv], W[:, 3 * P:4 * P], src, start=True, stop=True).then_inc(*st.sem(f"{pf}k{c}"))
                        for t in range(nkt):
                            mm = M(ps[0:kw, VB, t * P:(t + 1) * P], src[:, t * P:t * P + kw], W[:, 4 * P:5 * P],
                                   start=True, stop=True)
                        mm.then_inc(*st.sem(f"{pf}v{c}"))
                    na, nb, prev_a, prev_b = 0, 0, [], []
                    for what, c, n in order(pf):
                        if what == "a":
                            h, t = n
                            if n == (0, 0):
                                pe.wait_ge(stacked[pf, c], 16 * STACK_LOADS * (l + 1))
                            if na >= 2:
                                pe.wait_ge(*st.at(prev_a[na - 2], round=l))
                            for q in ([t] if pf == "s" else range(TT)):
                                o = 0 if pf == "s" else q * n_kv
                                mm = M(ps[:, AB + na % 2, o:o + n_kv], qst[0:MASK_ROW + 1, c, h, q * P:(q + 1) * P],
                                       kt[0:MASK_ROW + 1, c, h], start=True, stop=True)
                            mm.then_inc(*st.sem(f"{pf}a{c}.{h}.{t}"))
                            prev_a.append(f"{pf}m{c}.{h}.{t}")
                            na += 1
                        elif what == "t":
                            for i, (cols, name, was) in enumerate(((nhi, "thi", "lo"), (nlo, "tlo", "rhi"))):
                                pe.wait_ge(*st.at(f"{pf}{was}{c}", round=l))
                                if i == 0 and c == 1:
                                    pe.wait_ge(*st.at(f"{pf}res0", round=l))
                                for t in range(TT):
                                    mm = M(ps[0:H3, MB, t * P:(t + 1) * P], cols[:, c, t], identb[:], start=True, stop=True)
                                mm.then_inc(*st.sem(f"{pf}{name}{c}"))
                        elif what in ("b0", "b1"):
                            g, t = blocks(pf)[n]
                            i = int(what[1])
                            if n == 0 and i == 0:
                                pe.wait_ge(shifted[pf, c], 16 * 2 * (l + 1))
                                if c == 0:
                                    pe.wait_ge(*st.at(f"{pf}vc1", round=l))
                            if nb >= 2:
                                pe.wait_ge(*st.at(prev_b[nb - 2], round=l))
                            for j in range(2):
                                h = 4 * g + 2 * i + j
                                mm = M(ps[0:kw, 2 * i + j], kt[0:SHIFT_ROW + 2, c, h, t * P:t * P + kw],
                                       qst[0:SHIFT_ROW + 2, c, h], start=True, stop=True)
                            mm.then_inc(*st.sem(f"{pf}b{c}.{n}.{i}"))
                            prev_b.append(f"{pf}e{c}.{n}.{i}")
                            nb += 1
                        elif what == "o":
                            g, t = blocks(pf)[n]
                            if t == 0 and (g or c):
                                pe.wait_ge(*st.at(f"{pf}og{c}.{g - 1}" if g else f"{pf}og0.{G - 1}", round=l))
                            pe.wait_ge(*st.at(f"{pf}e{c}.{n}.1", round=l))
                            for j in range(4):
                                mm = M(ps[32 * j:32 * j + 32, VB], vt[0:kw, c, t, 4 * g + j], ex[0:kw, 2 * (n % 2) + j // 2, j % 2],
                                       start=(t == 0), stop=(t == nkt - 1))
                            mm.then_inc(*st.sem(f"{pf}v{c}.{n}"))
                        elif what == "d":
                            g = n
                            pe.wait_ge(*st.at(f"{pf}og{c}.{g}", round=l))
                            pe.wait_ge(*st.at(f"{pf}ln{c}.{g - 1}" if g else f"{pf}rlo{c}", round=l))
                            M(ps[:, MB], w["spread"], og[:, g % 2], start=True, stop=True).then_inc(*st.sem(f"{pf}sum{c}.{g}"))
                        else:
                            pe.wait_ge(*st.at(f"{pf}on{c}.{G - 1}", round=l))
                            for g in range(G):
                                mm = M(ps[:, MB], W[:, (5 + g) * P:(6 + g) * P], on[:, c, g], start=(g == 0), stop=(g == G - 1))
                            mm.then_inc(*st.sem(f"{pf}w{c}"))
                ln_pe(k, pe, ln, "f", lambda c: k.y[:, c], T, (AB, AB + 1), 2,
                      lambda c: pe.wait_ge(*st.at(f"xres{c}", round=l)), l)
                pe.wait_ge(landed["wf"], 16 * (l + 1))
                for j in range(NB):
                    for c in range(B):
                        if j == 0:
                            pe.wait_ge(*ln.at("f.affine", c, l))
                        if j >= 2:
                            pe.wait_ge(*st.at(f"g{c}.{j - 2}", round=l))
                        M(ps[:, 2 * c + j % 2], wf[:, j * P:(j + 1) * P], hn[:, c], start=True, stop=True)\
                            .then_inc(*st.sem(f"f{c}.{j}"))
                for c in range(B):
                    for j in range(NB):
                        pe.wait_ge(*st.at(f"g{c}.{j}", round=l))
                        mm = M(ps[:, VB + c], wf[:, DFF3 + j * D:DFF3 + (j + 1) * D], hid[:, c, j], start=(j == 0), stop=(j == NB - 1))
                    mm.then_inc(*st.sem(f"fo{c}"))

        @block.scalar
        def _(act):
            A = nc.scalar.activation
            st.prime(act, "act")
            ln.prime(act, "act")
            with act.Fori(0, NL3) as l:
                for pf in "sx":
                    n_kv = PARTS[pf][4]
                    nkt, kw = -(-n_kv // P), min(P, n_kv)
                    ln_act(k, act, ln, pf, T, (AB, AB + 1), 2, l)
                    for what, c, n in order(pf):
                        if what == "d":
                            g = n
                            act.wait_ge(*st.at(f"{pf}sum{c}.{g}", round=l))
                            if g >= 2 or c:
                                act.wait_ge(*st.at(f"{pf}on{c}.{g - 2}" if g >= 2 else f"{pf}on0.{G - 2 + g}", round=l))
                            A(rs[:, g % 2], ps[:, MB], ACT.Ln).then_inc(*st.sem(f"{pf}ln{c}.{g}"))
                            act.wait_ge(*st.at(f"{pf}ln{c}.{g}", round=l))
                            A(rs[:, g % 2], rs[:, g % 2], ACT.Exp, scale=-1.0).then_inc(*st.sem(f"{pf}inv{c}.{g}"))
                        if what not in ("b0", "b1"):
                            continue
                        i = int(what[1])
                        act.wait_ge(*st.at(f"{pf}b{c}.{n}.{i}", round=l))
                        if n >= 2:
                            act.wait_ge(*st.at(f"{pf}v{c}.{n - 2}", round=l))
                        elif c:
                            act.wait_ge(*st.at(f"{pf}v0.{len(blocks(pf)) - 2 + n}", round=l))
                        A(ex[0:kw, 2 * (n % 2) + i], ps[0:kw, 2 * i:2 * i + 2], ACT.Exp, scale=SCALE)\
                            .then_inc(*st.sem(f"{pf}e{c}.{n}.{i}"))
                ln_act(k, act, ln, "f", T, (AB, AB + 1), 2, l)
                for j in range(NB):
                    for c in range(B):
                        act.wait_ge(*st.at(f"f{c}.{j}", round=l))
                        A(hid[:, c, j], ps[:, 2 * c + j % 2], ACT.Gelu, bias=wf[:, 2 * DFF3 + j:2 * DFF3 + j + 1])\
                            .then_inc(*st.sem(f"g{c}.{j}"))

        @block.gpsimd
        def _(pool):
            st.prime(pool, "pool")
            with pool.Fori(0, NL3) as l:
                for pf in "sx":
                    n = PARTS[pf][4]
                    for c in range(B):
                        def step(name, out, a, b, op):
                            nc.gpsimd.tensor_tensor(out, a, b, op).then_inc(*st.sem(f"{pf}{name}{c}"))
                            pool.wait_ge(*st.at(f"{pf}{name}{c}", round=l))

                        kr, x1, x2 = rot[:, 1, 0:n], t1[:, 1, 0:n], t2[:, 1, 0:n]
                        k1, k2, k3 = (part[:, c, 1, i, 0:n] for i in range(3))
                        pool.wait_ge(*st.at(f"{pf}kb{c}", round=l))
                        step("kr", kr, x1, x2, ALU.add)
                        step("k1", k1, x1, x2, ALU.add)
                        step("kd", x1, kr, k1, ALU.subtract)
                        step("k2", k2, kr, k1, ALU.subtract)
                        step("k3", k3, x1, k2, ALU.subtract)

        @block.vector
        def _(dve):
            V = nc.vector
            st.prime(dve, "dve")
            ln.prime(dve, "dve")
            with dve.Fori(0, NL3) as l:
                def gain(j):
                    def of(c):
                        at = l * 6 + 2 * j
                        return (gains[:, bass.ds(at, 1), c], gains[:, bass.ds(at + 1, 1), c])
                    return of

                for pf in "sx":
                    W, kv, kt, vt, n_kv = PARTS[pf]
                    nkt, kw = -(-n_kv // P), min(P, n_kv)
                    ln_dve(k, dve, ln, pf, lambda c: k.y[:, c], lambda c: hn[:, c], T, (AB, AB + 1), 2, l,
                           affine=gain("sxf".index(pf)))
                    for c in range(B):
                        def step(name, out, a, b, op):
                            V.tensor_tensor(out, a, b, op).then_inc(*st.sem(f"{pf}{name}{c}"))
                            dve.wait_ge(*st.at(f"{pf}{name}{c}", round=l))

                        q1, q2, q3 = (part[:, c, 0, i] for i in range(3))
                        dve.wait_ge(*st.at(f"{pf}q{c}", round=l))
                        step("qa", t1[:, 0], w["cos"], ps[:, 0], ALU.mult)
                        step("qb", t2[:, 0], w["sin"], ps[:, 1], ALU.mult)
                        step("qr", rot[:, 0], t1[:, 0], t2[:, 0], ALU.add)
                        step("q1", q1, t1[:, 0], t2[:, 0], ALU.add)
                        step("qd", t1[:, 0], rot[:, 0], q1, ALU.subtract)
                        step("q2", q2, rot[:, 0], q1, ALU.subtract)
                        step("q3", q3, t1[:, 0], q2, ALU.subtract)
                        dve.wait_ge(*st.at(f"{pf}k{c}", round=l))
                        if c:
                            dve.wait_ge(*st.at(f"{pf}k30", round=l))
                        step("ka", t1[:, 1, 0:n_kv], w["cos"][:, 0:n_kv], ps[:, 2, 0:n_kv], ALU.mult)
                        step("kb", t2[:, 1, 0:n_kv], w["sin"][:, 0:n_kv], ps[:, 3, 0:n_kv], ALU.mult)
                        dve.wait_ge(*st.at(f"{pf}v{c}", round=l))
                        V.tensor_copy(vt[0:kw, c, :, :, 0:DH3], ps[0:kw, VB, 0:nkt * P].rearrange("p (t h d) -> p t h d", t=nkt, d=DH3))\
                            .then_inc(*st.sem(f"{pf}vc{c}"))
                    na = 0
                    for what, c, n in order(pf):
                        if what == "a":
                            h, t = n
                            dve.wait_ge(*st.at(f"{pf}a{c}.{h}.{t}", round=l))
                            if pf == "s":
                                V.tensor_reduce(ncol[:, c, t, h:h + 1], ps[:, AB + na % 2], AX, ALU.max, negate=True)\
                                    .then_inc(*st.sem(f"{pf}m{c}.{h}.{t}"))
                            else:
                                V.tensor_reduce(ncol[:, c, :, h], ps[:, AB + na % 2, 0:TT * n_kv].rearrange("p (t n) -> p t n", t=TT),
                                                AX, ALU.max, negate=True).then_inc(*st.sem(f"{pf}m{c}.{h}.{t}"))
                            na += 1
                        elif what == "t":
                            dve.wait_ge(*st.at(f"{pf}m{c}.{H3 - 1}.{tiles_a[pf] - 1}", round=l))
                            V.tensor_copy(nhi[:, c], ncol[:, c]).then_inc(*st.sem(f"{pf}hi{c}"))
                            dve.wait_ge(*st.at(f"{pf}hi{c}", round=l))
                            V.tensor_tensor(nlo[:, c], ncol[:, c], nhi[:, c], ALU.subtract).then_inc(*st.sem(f"{pf}lo{c}"))
                            dve.wait_ge(*st.at(f"{pf}thi{c}", round=l))
                            V.tensor_copy(nrow[:, c, 0], ps[0:H3, MB]).then_inc(*st.sem(f"{pf}rhi{c}"))
                            dve.wait_ge(*st.at(f"{pf}tlo{c}", round=l))
                            V.tensor_copy(nrow[:, c, 1], ps[0:H3, MB]).then_inc(*st.sem(f"{pf}rlo{c}"))
                        elif what == "o":
                            g, t = blocks(pf)[n]
                            if t == nkt - 1:
                                dve.wait_ge(*st.at(f"{pf}v{c}.{n}", round=l))
                                if g >= 2 or c:
                                    dve.wait_ge(*st.at(f"{pf}on{c}.{g - 2}" if g >= 2 else f"{pf}on0.{G - 2 + g}", round=l))
                                V.tensor_copy(og[:, g % 2], ps[:, VB]).then_inc(*st.sem(f"{pf}og{c}.{g}"))
                        elif what == "d":
                            dve.wait_ge(*st.at(f"{pf}og{c}.{n}", round=l))
                            dve.wait_ge(*st.at(f"{pf}inv{c}.{n}", round=l))
                            V.tensor_tensor(on[:, c, n], og[:, n % 2], rs[:, n % 2], ALU.mult).then_inc(*st.sem(f"{pf}on{c}.{n}"))
                        elif what in ("b0", "b1"):
                            continue
                        else:
                            dve.wait_ge(*st.at(f"{pf}w{c}", round=l))
                            V.tensor_tensor(k.y[:, c], k.y[:, c], ps[:, MB], ALU.add).then_inc(*st.sem(f"{pf}res{c}"))
                ln_dve(k, dve, ln, "f", lambda c: k.y[:, c], lambda c: hn[:, c], T, (AB, AB + 1), 2, l, affine=gain(2))
                for c in range(B):
                    dve.wait_ge(*st.at(f"fo{c}", round=l))
                    V.scalar_tensor_tensor(out=k.y[:, c], in0=ps[:, VB + c], scalar=wf[:, 2 * DFF3 + NB:2 * DFF3 + NB + 1],
                                           in1=k.y[:, c], op0=ALU.add, op1=ALU.add).then_inc(*st.sem(f"fres{c}"))
            dve.wait_ge(*st.at("fres1", round=NL3 - 1))


def layer3_stage(k, w):
    norm_stage(k, "t6p")
    copy_stage(k, "t6c", k.y, k.xn)
    transformer3_stage(k, w)
    add_stage(k, "t6r", k.x, k.y)


def rms_stage(k, label, src, dst, gain, eps):
    nc, ps = k.nc, k.ps
    with ExitStack() as ctx:
        e = ctx.enter_context(nc.sbuf_tensor(label + "_eps", [P, 1], F32))
        st = Steps(k, label, 2, pe="ms", act="sq ln rstd", dve="out", pool="eps")
        block = ctx.enter_context(nc.Block())

        @block.gpsimd
        def _(pool):
            nc.gpsimd.memset(e[:], eps).then_inc(*st.sem("eps"))

        @block.tensor
        def _(pe):
            for c in range(B):
                pe.wait_ge(*st.at("sq", c))
                nc.tensor.matmul(ps[:, 4 * c], k.mean_w[:], k.sq[:, c], start=True, stop=True).then_inc(*st.sem("ms", c))

        @block.scalar
        def _(act):
            for c in range(B):
                nc.scalar.activation(k.sq[:, c], src[:, c], ACT.Square).then_inc(*st.sem("sq", c))
            nc.scalar.preload_act_table_set("natural_log_exp_and_others")
            act.wait_ge(*st.at("eps"))
            for c in range(B):
                act.wait_ge(*st.at("ms", c))
                nc.scalar.activation(k.rstd[:, c], ps[:, 4 * c], ACT.Ln, bias=e[:, 0:1]).then_inc(*st.sem("ln", c))
                act.wait_ge(*st.at("ln", c))
                nc.scalar.activation(k.rstd[:, c], k.rstd[:, c], ACT.Exp, scale=-0.5).then_inc(*st.sem("rstd", c))

        @block.vector
        def _(dve):
            for c in range(B):
                dve.wait_ge(*st.at("rstd", c))
                nc.vector.scalar_tensor_tensor(out=dst[:, c], in0=src[:, c], scalar=gain, in1=k.rstd[:, c],
                                               op0=ALU.mult, op1=ALU.mult).then_inc(*st.sem("out", c))
            for c in range(B):
                dve.wait_ge(*st.at("out", c))


def final_stage(k, w):
    nc = k.nc
    with ExitStack() as ctx:
        hn = ctx.enter_context(nc.sbuf_tensor("t7_h", [P, B, T], F32))
        norm_stage(k, "t7n")
        copy_stage(k, "t7c", k.y, k.xn)
        rms_stage(k, "t7a", k.y, hn, w["g1"], 1e-6)
        attention(k, "t7s", 1, H4, DK4, hn, hn, T, k.dram["attn4"], shared_kv=True)
        rms_stage(k, "t7b", k.y, k.xn, w["g2"], 1e-6)
        add_stage(k, "t7r", k.x, k.y)
    moe_stage(k, "m7", "renorm", E4, F4, 1, k.dram["experts4"], w)


def layer1_stage(k, w):
    norm_stage(k, "n1")
    moe_stage(k, "m1", "scores", E0, I0, SI0 // I0, k.dram["experts0"], w)


def layer2_stage(k, w):
    norm_stage(k, "n2")
    gru_stage(k, w)


def layer3_moe_stage(k, w):
    norm_stage(k, "n3")
    moe_stage(k, "m3", "sigmoid", E1, I1, SI1 // I1, k.dram["experts1"], w)


def layer5_stage(k, w):
    norm_stage(k, "n5")
    ternary_stage(k, w)


def build(nc, dram, layout, out):
    with ExitStack() as ctx:
        k = Core(nc, ctx, dram, layout)
        setup_stage(k)
        k.release()
        stages = (slots_stage, layer1_stage, layer2_stage, layer3_moe_stage, transformer2_stage, layer5_stage,
                  layer3_stage, final_stage)
        for n, stage in enumerate(stages):
            with ExitStack() as wctx:
                whole, parts = k.weights(wctx, f"p{n}")
                load_stage(k, whole, f"p{n}")
                stage(k, parts)
            k.release()
        store_stage(k, out)
        k.release()


def col(a):
    return a.reshape(-1, 1)


def tiles(a):
    n = a.shape[0] // P
    return a.reshape(n, P, a.shape[1]).transpose(1, 0, 2).reshape(P, n * a.shape[1])


def laid_out(i):
    packs = {}
    packs["p0"] = [(n, i["L0_xcond_" + n]) for n in ("wk", "wv", "wq", "wu", "w1", "w2")] + \
        [(n, col(i["L0_xcond_" + n])) for n in ("q_mu", "q_logsig", "lnkv_g", "lnkv_b", "lnq_g", "lnq_b", "lnm_g",
                                                "lnm_b", "lnp_g", "lnp_b", "bk", "bq", "bu", "b1", "b2")] + \
        [("bv", i["L0_xcond_bv"].reshape(1, D))]
    def rows(a, n):
        return np.broadcast_to(a.reshape(1, n), (P, n))

    def rank(n):
        return rows(np.arange(n, 0, -1, dtype=np.float32), n)

    packs["p1"] = [("router", np.concatenate([i["L0_ffn_gate_w"], i["L0_ffn_shared_expert_gate_w"]]).T), ("rank", rank(E0))]
    packs["p3"] = [("router", i["L1_ffn_router_w"]), ("rank", rank(E1)), ("bias", rows(i["L1_ffn_expert_bias"], E1))]
    packs["p7"] = [("g1", col(i["L3_ffn_g1"])), ("g2", col(i["L3_ffn_g2"])), ("router", i["L3_ffn_Wr"].T), ("rank", rank(E4)), ("bias", rows(i["L3_ffn_expert_bias"], E4))]
    wi = i["L1_xcond_Wi"]
    packs["p2"] = [("att_h", i["L1_xcond_W_att"][0:D]), ("att_e", i["L1_xcond_W_att"][D:]), ("v", i["L1_xcond_V_att"]),
                   ("wix", wi[0:D]), ("wic", wi[D:]), ("uh", i["L1_xcond_Uh"]), ("bi", i["L1_xcond_b"].reshape(3, D).T)]
    L2 = {n[len("L2_xcond_"):]: a for n, a in i.items() if n.startswith("L2_xcond_")}
    packs["p4"] = [("norm_w", np.concatenate([L2[f"norm{j}_w"] for j in (1, 2, 3)], axis=1)),
                   ("norm_b", np.concatenate([L2[f"norm{j}_b"].reshape(2, D).T for j in (1, 2, 3)], axis=1)),
                   ("attn1_bo", col(L2["attn1_bo"])), ("attn2_bo", col(L2["attn2_bo"])),
                   ("ff_w1", L2["ff_w1"]), ("ff_b1", L2["ff_b1"].reshape(-1, P).T), ("ff_w2", tiles(L2["ff_w2"])),
                   ("ff_b2", col(L2["ff_b2"]))]
    packs["p5"] = [("w_fc", tiles(i["L2_ffn_w_fc"])), ("w_proj", i["L2_ffn_w_proj"]), ("vT", i["L2_ffn_v"].T),
                   ("fastT", i["L2_ffn_fast_b"].T), ("uT", i["L2_ffn_u"].T),
                   ("gate", np.broadcast_to(i["L2_ffn_gate"].reshape(1, 1), (P, 1)))]
    L3 = {n[len("L3_xcond_"):]: a for n, a in i.items() if n.startswith("L3_xcond_")}
    feature = np.arange(P) // H3
    by_feature = np.arange(P) % H3 * DH3 + feature
    half = DH3 // 2
    angle = np.arange(T, dtype=np.float32)[None] / np.float32(10000.0) ** (feature % half / half).astype(np.float32)[:, None]
    sign = np.where(feature < half, -1.0, 1.0).astype(np.float32)[:, None]
    partner = by_feature ^ half
    spread = np.zeros((P, P), np.float32)
    for j in range(0, P, 32):
        spread[j + DH3, j:j + 32] = 1.0
    packs["p6n"] = [("norm_w", np.concatenate([L3[f"n{j}_w"][l].T for l in range(NL3) for j in (1, 2, 3)], axis=1)),
                   ("norm_b", np.concatenate([L3[f"n{j}_b"][l].reshape(2, D).T for l in range(NL3) for j in (1, 2, 3)], axis=1))]
    packs["p6"] = [("cos", np.cos(angle).astype(np.float32)), ("sin", (np.sin(angle) * sign).astype(np.float32)),
                   ("spread", spread)]
    layout = {p: [(n, a.shape[0], a.shape[1]) for n, a in rows] for p, rows in packs.items()}
    arrays = {}
    for p, rows in packs.items():
        whole = np.zeros((P, sum(a.shape[1] for _, a in rows)), np.float32)
        at = 0
        for _, a in rows:
            whole[0:a.shape[0], at:at + a.shape[1]] = a
            at += a.shape[1]
        arrays[p] = whole
    arrays["x"] = np.ascontiguousarray(i["x"].transpose(2, 0, 1))
    arrays["ctx"] = np.ascontiguousarray(i["ctx_1024"].transpose(2, 0, 1))
    arrays["cond"] = np.ascontiguousarray(i["cond_1024"].T)

    def expert(gate, up, down):
        n = down.shape[0]
        full = np.zeros((-(-n // P) * P, D), np.float32)
        full[0:n] = down
        return np.concatenate([gate, up, tiles(full)], axis=1)

    gu, dn = i["L0_ffn_experts_gate_up"], i["L0_ffn_experts_down"]
    arrays["experts0"] = np.stack(
        [expert(gu[e, 0:I0].T, gu[e, I0:].T, dn[e].T) for e in range(E0)] +
        [expert(i["L0_ffn_shared_gate_w"][s:s + I0].T, i["L0_ffn_shared_up_w"][s:s + I0].T,
                i["L0_ffn_shared_down_w"][:, s:s + I0].T) for s in range(0, SI0, I0)])
    arrays["experts1"] = np.stack(
        [expert(i["L1_ffn_routed_w1"][e], i["L1_ffn_routed_w2"][e], i["L1_ffn_routed_w3"][e]) for e in range(E1)] +
        [expert(i["L1_ffn_shared_w1"][0][:, s:s + I1], i["L1_ffn_shared_w2"][0][:, s:s + I1],
                i["L1_ffn_shared_w3"][0][s:s + I1]) for s in range(0, SI1, I1)])
    arrays["experts4"] = np.stack(
        [expert(i["L3_ffn_eW1"][e].T, i["L3_ffn_eW3"][e].T, i["L3_ffn_eW2"][e].T) for e in range(E4)] +
        [expert(i["L3_ffn_sW1"].T, i["L3_ffn_sW3"].T, i["L3_ffn_sW2"].T)])
    for n in ("attn1", "attn2"):
        arrays[n] = np.stack([np.concatenate([L2[n + "_wq"][:, g:g + P], L2[n + "_wk"][:, g:g + P], L2[n + "_wv"][:, g:g + P],
                                              L2[n + "_wo"][g:g + P]], axis=1) for g in range(0, INNER2, P)])
    arrays["attn4"] = np.concatenate([i["L3_ffn_" + n].T for n in ("Wq", "Wkc", "Wvc", "Wo")], axis=1)[None]

    def quadrants(a):
        out = np.zeros((P, H3 // 4, D), np.float32)
        for h in range(H3):
            out[32 * (h % 4):32 * (h % 4) + DH3, h // 4] = a[h * DH3:(h + 1) * DH3]
        return out.reshape(P, -1)

    def attention3(q, kk, v, o):
        return np.concatenate([q.T[:, by_feature], q.T[:, partner], kk.T[:, by_feature], kk.T[:, partner], v.T, quadrants(o.T)], axis=1)

    arrays["t6_wa"] = np.stack([attention3(*np.split(L3["qkv_w"][l], 3), L3["so_w"][l]) for l in range(NL3)])
    arrays["t6_wx"] = np.stack([attention3(L3["cq_w"][l], L3["ck_w"][l], L3["cv_w"][l], L3["co_w"][l]) for l in range(NL3)])
    arrays["t6_wf"] = np.stack([np.concatenate([L3["f1_w"][l].T, tiles(L3["f2_w"][l].T), L3["f1_b"][l].reshape(-1, P).T,
                                                col(L3["f2_b"][l])], axis=1) for l in range(NL3)])
    masks = np.concatenate([i["mask_BxS_bf0"], i["mask_BxS2_bf0"]], axis=1)
    arrays["masks"] = np.ascontiguousarray(np.broadcast_to(masks, (H3, B, T + S)))
    return arrays, layout


def kernel(**inputs):
    import concourse.bacc as bacc
    from concourse.bass_utils import run_bass_kernel_spmd

    arrays, layout = laid_out({n: np.asarray(a) for n, a in inputs.items()})
    nc = bacc.Bacc("TRN2", target_bir_lowering=False, num_devices=1)
    dram = {n: nc.dram_tensor(f"in_{n}", a.shape, mybir.dt.from_np(a.dtype), kind="ExternalInput").ap()
            for n, a in arrays.items()}
    out = nc.dram_tensor("out_x", (P, B, T), F32, kind="ExternalOutput").ap()
    build(nc, dram, layout, out)
    r = run_bass_kernel_spmd(nc, [{f"in_{n}": a for n, a in arrays.items()}], core_ids=[0])
    return np.ascontiguousarray(r.results[0]["out_x"].transpose(1, 2, 0))
```
